# Optimizing a Trainium2 kernel written in Bass

```python
import numpy as np
import jax
import jax.numpy as jnp

def _softmax(x, axis=-1):
    return jax.nn.softmax(x, axis=axis)

def _gelu(x):
    return jax.nn.gelu(x, approximate=True)

def _silu(x):
    return jax.nn.silu(x)

def _sigmoid(x):
    return jax.nn.sigmoid(x)

def _layernorm(x, axis=-1, eps=1e-05):
    m = jnp.mean(x, axis=axis, keepdims=True)
    v = jnp.var(x, axis=axis, keepdims=True)
    return (x - m) / jnp.sqrt(v + eps)

def _scatter_add(tgt, idx, src, axis=0):
    return tgt.at[idx].add(src)

def _segment_sum(src, seg, n):
    return jax.ops.segment_sum(src, seg, n)
kernel_name = 'mk_perceiver_d2_seqx_r8_4fb63a'

def setup_inputs(seed: int=0):
    np.random.seed(seed)
    _w = jnp.asarray

    def _rec_inputs():
        import jax
        import jax.numpy as jnp
        _rk = jax.random.key(seed)
        x = 0.0003765 + 1 * jax.random.normal(jax.random.fold_in(_rk, 1), (4, 128, 128), jnp.float32)
        _lenS = 128 - jax.random.randint(jax.random.fold_in(_rk, 7), (4,), 0, max(1, 128 // 4) + 1, jnp.int32)
        _lenS2 = 2048 - jax.random.randint(jax.random.fold_in(_rk, 8), (4,), 0, max(1, 2048 // 4) + 1, jnp.int32)
        _ctx_1024P = jax.random.normal(jax.random.fold_in(_rk, 11), (4, 16, 128), jnp.float32)
        _ctx_1024c = jax.random.dirichlet(jax.random.fold_in(_rk, 511), 0.3 * jnp.ones((16,), jnp.float32), (4, 2048))
        _ctx_1024t = jnp.einsum('bsk,bkd->bsd', _ctx_1024c, _ctx_1024P)
        _ctx_1024t = _ctx_1024t * jax.lax.rsqrt(jnp.mean(jnp.square(_ctx_1024t)) + 1e-12) * 0.953939
        ctx_1024 = -0.000292821 + 1.00034 * (_ctx_1024t + 0.3 * jax.random.normal(jax.random.fold_in(_rk, 611), (4, 2048, 128), jnp.float32))
        _validS = jnp.arange(128)[None, :] < _lenS[:, None]
        _validS2 = jnp.arange(2048)[None, :] < _lenS2[:, None]
        _causal = jnp.tril(jnp.ones((128, 128), dtype=bool))
        mask_BxS2_bk1 = jnp.broadcast_to(_validS2[:, :], (4, 2048))
        return (x, ctx_1024, mask_BxS2_bk1)
    x, ctx_1024, mask_BxS2_bk1 = _rec_inputs()

    def _L0_xattn_setup():
        import jax, jax.numpy as jnp
        import numpy as np
        B, S, D, H = (2, 256, 128, 16)
        DEPTH = D // H

        def _split_heads(x):
            b, s, _ = x.shape
            return x.reshape(b, s, H, DEPTH).transpose(0, 2, 1, 3)
        key = jax.random.key(seed)
        ks = jax.random.split(key, 11)
        scale = 1.0 / np.sqrt(D)
        inp = {'v': jax.random.normal(ks[0], (B, S, D), jnp.float32), 'k': jax.random.normal(ks[1], (B, S, D), jnp.float32), 'q': jax.random.normal(ks[2], (B, S, D), jnp.float32), 'Wq': jax.random.normal(ks[3], (D, D), jnp.float32) * scale, 'bq': jnp.zeros((D,), jnp.float32), 'Wk': jax.random.normal(ks[4], (D, D), jnp.float32) * scale, 'bk': jnp.zeros((D,), jnp.float32), 'Wv': jax.random.normal(ks[5], (D, D), jnp.float32) * scale, 'bv': jnp.zeros((D,), jnp.float32), 'Wo': jax.random.normal(ks[6], (D, D), jnp.float32) * scale, 'bo': jnp.zeros((D,), jnp.float32)}
        return inp
    _L0_xattn_all = _L0_xattn_setup()
    _L0_xattn_in = {k: v for k, v in _L0_xattn_all.items() if k in ('Wq', 'bq', 'Wk', 'bk', 'Wv', 'bv', 'Wo', 'bo')}
    del _L0_xattn_all

    def _L0_attn_setup():
        import jax, jax.numpy as jnp
        import numpy as np
        DIM = 128
        NUM_HEADS = 16
        HEAD_DIM = DIM // NUM_HEADS
        EPS_NORM = 1e-12
        EPS_LN = 1e-05
        key = jax.random.key(seed)
        ks = jax.random.split(key, 6)
        x = jax.random.normal(ks[0], (4, 256, DIM), dtype=jnp.float32)
        ln_w = jnp.ones((DIM,), jnp.float32)
        ln_b = jnp.zeros((DIM,), jnp.float32)
        limit = float(np.sqrt(6.0 / (DIM + 3 * DIM)))
        qkv_w = jax.random.uniform(ks[1], (3 * DIM, DIM), jnp.float32, -limit, limit)
        qkv_b = jnp.zeros((3 * DIM,), jnp.float32)
        out_w = 0.02 * jax.random.normal(ks[2], (DIM, DIM), dtype=jnp.float32)
        out_b = jnp.zeros((DIM,), jnp.float32)
        return {'x': x, 'ln_w': ln_w, 'ln_b': ln_b, 'qkv_w': qkv_w, 'qkv_b': qkv_b, 'out_w': out_w, 'out_b': out_b}
    _L0_attn_all = _L0_attn_setup()
    _L0_attn_in = {k: v for k, v in _L0_attn_all.items() if k in ('ln_w', 'ln_b', 'qkv_w', 'qkv_b', 'out_w', 'out_b')}
    del _L0_attn_all

    def _L0_ffn_setup():
        import jax, jax.numpy as jnp
        import numpy as np
        DIM = 128
        DEPTH = 2
        HEADS = 8
        DIM_HEAD = 64
        WINDOW = 64
        INNER = HEADS * DIM_HEAD
        HID = int(DIM * 4 * 2 / 3)
        B, N = (2, 1024)
        QK_SCALE = 8.0

        def shift_token(t):
            t1, t2 = jnp.split(t, 2, axis=-1)
            t2 = jnp.pad(t2, ((0, 0), (1, 0), (0, 0)))[:, :-1]
            return jnp.concatenate([t1, t2], axis=-1)

        def l2norm(t):
            return t / jnp.clip(jnp.linalg.norm(t, axis=-1, keepdims=True), 1e-12)

        def rotate_half(x):
            x1, x2 = jnp.split(x, 2, axis=-1)
            return jnp.concatenate([-x2, x1], axis=-1)

        def rotary_xpos(q, k):
            n = q.shape[-2]
            half_idx = jnp.arange(0, DIM_HEAD, 2, dtype=jnp.float32)
            inv_freq = 1.0 / 10000.0 ** (half_idx / DIM_HEAD)
            t = jnp.arange(n, dtype=jnp.float32)
            freqs = t[:, None] * inv_freq[None, :]
            freqs = jnp.concatenate([freqs, freqs], axis=-1)
            base = (half_idx + 0.4 * DIM_HEAD) / (1.4 * DIM_HEAD)
            power = (t - n // 2) / float(WINDOW // 2)
            scale = base[None, :] ** power[:, None]
            scale = jnp.concatenate([scale, scale], axis=-1)
            cos, sin = (jnp.cos(freqs), jnp.sin(freqs))
            q = q * cos * scale + rotate_half(q) * sin * scale
            k = k * cos / scale + rotate_half(k) * sin / scale
            return (q, k)

        def local_attention(q, k, v):
            b, h, n, d = q.shape
            w = n // WINDOW
            bq = q.reshape(b, h, w, WINDOW, d) * QK_SCALE
            bk = k.reshape(b, h, w, WINDOW, d)
            bv = v.reshape(b, h, w, WINDOW, d)

            def look_around(t):
                p = jnp.pad(t, ((0, 0), (0, 0), (1, 0), (0, 0), (0, 0)))
                return jnp.concatenate([p[:, :, :w], p[:, :, 1:]], axis=3)
            bk, bv = (look_around(bk), look_around(bv))
            bt = jnp.arange(n).reshape(w, WINDOW)
            btp = jnp.pad(bt, ((1, 0), (0, 0)), constant_values=-1)
            btk = jnp.concatenate([btp[:w], btp[1:]], axis=1)
            sim = jnp.einsum('bhwid,bhwjd->bhwij', bq, bk)
            i = bt[:, :, None]
            j = btk[:, None, :]
            mask = (i < j) | (i > j + WINDOW) | (j == -1)
            sim = jnp.where(mask, -jnp.finfo(sim.dtype).max, sim)
            attn = jax.nn.softmax(sim, axis=-1)
            out = jnp.einsum('bhwij,bhwjd->bhwid', attn, bv)
            return out.reshape(b, h, n, d)

        def _layer(x, wqkv, qs, ksc, wo, lg, lb, w1, b1, w2, b2):
            b, n, _ = x.shape
            h = shift_token(x)
            qkv = h @ wqkv
            q, k, v = jnp.split(qkv, 3, axis=-1)
            to_heads = lambda t: t.reshape(b, n, HEADS, DIM_HEAD).transpose(0, 2, 1, 3)
            q, k, v = (to_heads(q), to_heads(k), to_heads(v))
            q = l2norm(q) * qs
            k = l2norm(k) * ksc
            q, k = rotary_xpos(q, k)
            o = local_attention(q, k, v)
            o = o.transpose(0, 2, 1, 3).reshape(b, n, INNER)
            x = x + o @ wo
            h = shift_token(x)
            mu = h.mean(-1, keepdims=True)
            var = h.var(-1, keepdims=True)
            h = (h - mu) / jnp.sqrt(var + 1e-05) * lg + lb
            h = h @ w1 + b1
            a, g = jnp.split(h, 2, axis=-1)
            h = a * jax.nn.gelu(g, approximate=False)
            x = x + h @ w2 + b2
            return x
        key = jax.random.key(seed)
        ks = jax.random.split(key, 6)
        return {'x': jax.random.normal(ks[0], (B, N, DIM), jnp.float32), 'wqkv': jax.random.normal(ks[1], (DEPTH, DIM, 3 * INNER), jnp.float32) * 0.02, 'q_scale': jnp.ones((DEPTH, DIM_HEAD), jnp.float32), 'k_scale': jnp.ones((DEPTH, DIM_HEAD), jnp.float32), 'wo': jax.random.normal(ks[2], (DEPTH, INNER, DIM), jnp.float32) * 0.02, 'ln_g': jnp.ones((DEPTH, DIM), jnp.float32), 'ln_b': jnp.zeros((DEPTH, DIM), jnp.float32), 'w1': jax.random.normal(ks[3], (DEPTH, DIM, 2 * HID), jnp.float32) * 0.02, 'b1': jnp.zeros((DEPTH, 2 * HID), jnp.float32), 'w2': jax.random.normal(ks[4], (DEPTH, HID, DIM), jnp.float32) * 0.02, 'b2': jnp.zeros((DEPTH, DIM), jnp.float32)}
    _L0_ffn_all = _L0_ffn_setup()
    _L0_ffn_in = {k: v for k, v in _L0_ffn_all.items() if k in ('wqkv', 'q_scale', 'k_scale', 'wo', 'ln_g', 'ln_b', 'w1', 'b1', 'w2', 'b2')}
    del _L0_ffn_all

    def _L1_xattn_setup():
        import jax, jax.numpy as jnp
        import numpy as np
        D_MODEL = 128
        NUM_HEADS = 16
        DEPTH = D_MODEL // NUM_HEADS
        B, S = (4, 256)
        NEG_INF = float('-inf')

        def _split_heads(x, b):
            return x.reshape(b, -1, NUM_HEADS, DEPTH).transpose(0, 2, 1, 3)
        key = jax.random.key(seed)
        ks = jax.random.split(key, 12)
        inp = {'value': jax.random.normal(ks[0], (B, S, D_MODEL), jnp.float32), 'key': jax.random.normal(ks[1], (B, S, D_MODEL), jnp.float32), 'query': jax.random.normal(ks[2], (B, S, D_MODEL), jnp.float32), 'key_padding_mask': jnp.arange(S)[None, :] < 3 * S // 4}
        inp['key_padding_mask'] = jnp.broadcast_to(inp['key_padding_mask'], (B, S))
        scale = 1.0 / np.sqrt(D_MODEL)
        inp['Wq'] = jax.random.normal(ks[3], (D_MODEL, D_MODEL), jnp.float32) * scale
        inp['bq'] = jnp.zeros((D_MODEL,), jnp.float32)
        inp['Wk'] = jax.random.normal(ks[4], (D_MODEL, D_MODEL), jnp.float32) * scale
        inp['bk'] = jnp.zeros((D_MODEL,), jnp.float32)
        inp['Wv'] = jax.random.normal(ks[5], (D_MODEL, D_MODEL), jnp.float32) * scale
        inp['bv'] = jnp.zeros((D_MODEL,), jnp.float32)
        inp['Wo'] = jax.random.normal(ks[6], (D_MODEL, D_MODEL), jnp.float32) * scale
        inp['bo'] = jnp.zeros((D_MODEL,), jnp.float32)
        return inp
    _L1_xattn_all = _L1_xattn_setup()
    _L1_xattn_in = {k: v for k, v in _L1_xattn_all.items() if k in ('Wq', 'bq', 'Wk', 'bk', 'Wv', 'bv', 'Wo', 'bo')}
    del _L1_xattn_all

    def _L1_attn_setup():
        import jax, jax.numpy as jnp
        import numpy as np
        B, N, D_IN, D_OUT = (4, 256, 128, 128)
        key = jax.random.key(seed)
        k = jax.random.split(key, 6)
        x = jax.random.normal(k[0], (B, N, D_IN), dtype=jnp.float32)
        sc_in = 1.0 / np.sqrt(D_IN)
        sc_out = 1.0 / np.sqrt(D_OUT)
        W_spin = jax.random.uniform(k[1], (D_OUT, D_IN), jnp.float32, -sc_in, sc_in)
        b_spin = jax.random.uniform(k[2], (D_OUT,), jnp.float32, -sc_in, sc_in)
        W_global = jax.random.uniform(k[3], (D_OUT, D_OUT), jnp.float32, -sc_out, sc_out)
        W_J = jax.random.uniform(k[4], (D_OUT, D_OUT), jnp.float32, -sc_out, sc_out)
        beta = jnp.ones((1,), dtype=jnp.float32)
        return {'x': x, 'W_spin': W_spin, 'b_spin': b_spin, 'W_global': W_global, 'W_J': W_J, 'beta': beta}
    _L1_attn_all = _L1_attn_setup()
    _L1_attn_in = {k: v for k, v in _L1_attn_all.items() if k in ('W_spin', 'b_spin', 'W_global', 'W_J', 'beta')}
    del _L1_attn_all

    def _L1_ffn_setup():
        import jax, jax.numpy as jnp
        import numpy as np
        H = 128
        I = 256
        E = 8
        B, S = (2, 128)

        def _swiglu(x, wg, wu, wd):
            return jax.nn.silu(x @ wg) * (x @ wu) @ wd
        key = jax.random.key(seed)
        ks = jax.random.split(key, 8)
        sc_h = 1.0 / np.sqrt(H)
        sc_i = 1.0 / np.sqrt(I)
        return {'hidden_states': jax.random.normal(ks[0], (B, S, H), jnp.float32), 'gate_w': jax.random.normal(ks[1], (H, E), jnp.float32) * sc_h, 'sh_gate': jax.random.normal(ks[2], (H, I), jnp.float32) * sc_h, 'sh_up': jax.random.normal(ks[3], (H, I), jnp.float32) * sc_h, 'sh_down': jax.random.normal(ks[4], (I, H), jnp.float32) * sc_i, 'rt_gate': jax.random.normal(ks[5], (E, H, I), jnp.float32) * sc_h, 'rt_up': jax.random.normal(ks[6], (E, H, I), jnp.float32) * sc_h, 'rt_down': jax.random.normal(ks[7], (E, I, H), jnp.float32) * sc_i}
    _L1_ffn_all = _L1_ffn_setup()
    _L1_ffn_in = {k: v for k, v in _L1_ffn_all.items() if k in ('gate_w', 'sh_gate', 'sh_up', 'sh_down', 'rt_gate', 'rt_up', 'rt_down')}
    del _L1_ffn_all
    return {'x': x, 'ctx_1024': ctx_1024, 'mask_BxS2_bk1': mask_BxS2_bk1, 'L0_xattn_Wq': _L0_xattn_in['Wq'], 'L0_xattn_bq': _L0_xattn_in['bq'], 'L0_xattn_Wk': _L0_xattn_in['Wk'], 'L0_xattn_bk': _L0_xattn_in['bk'], 'L0_xattn_Wv': _L0_xattn_in['Wv'], 'L0_xattn_bv': _L0_xattn_in['bv'], 'L0_xattn_Wo': _L0_xattn_in['Wo'], 'L0_xattn_bo': _L0_xattn_in['bo'], 'L0_attn_ln_w': _L0_attn_in['ln_w'], 'L0_attn_ln_b': _L0_attn_in['ln_b'], 'L0_attn_qkv_w': _L0_attn_in['qkv_w'], 'L0_attn_qkv_b': _L0_attn_in['qkv_b'], 'L0_attn_out_w': _L0_attn_in['out_w'], 'L0_attn_out_b': _L0_attn_in['out_b'], 'L0_ffn_wqkv': _L0_ffn_in['wqkv'], 'L0_ffn_q_scale': _L0_ffn_in['q_scale'], 'L0_ffn_k_scale': _L0_ffn_in['k_scale'], 'L0_ffn_wo': _L0_ffn_in['wo'], 'L0_ffn_ln_g': _L0_ffn_in['ln_g'], 'L0_ffn_ln_b': _L0_ffn_in['ln_b'], 'L0_ffn_w1': _L0_ffn_in['w1'], 'L0_ffn_b1': _L0_ffn_in['b1'], 'L0_ffn_w2': _L0_ffn_in['w2'], 'L0_ffn_b2': _L0_ffn_in['b2'], 'L1_xattn_Wq': _L1_xattn_in['Wq'], 'L1_xattn_bq': _L1_xattn_in['bq'], 'L1_xattn_Wk': _L1_xattn_in['Wk'], 'L1_xattn_bk': _L1_xattn_in['bk'], 'L1_xattn_Wv': _L1_xattn_in['Wv'], 'L1_xattn_bv': _L1_xattn_in['bv'], 'L1_xattn_Wo': _L1_xattn_in['Wo'], 'L1_xattn_bo': _L1_xattn_in['bo'], 'L1_attn_W_spin': _L1_attn_in['W_spin'], 'L1_attn_b_spin': _L1_attn_in['b_spin'], 'L1_attn_W_global': _L1_attn_in['W_global'], 'L1_attn_W_J': _L1_attn_in['W_J'], 'L1_attn_beta': _L1_attn_in['beta'], 'L1_ffn_gate_w': _L1_ffn_in['gate_w'], 'L1_ffn_sh_gate': _L1_ffn_in['sh_gate'], 'L1_ffn_sh_up': _L1_ffn_in['sh_up'], 'L1_ffn_sh_down': _L1_ffn_in['sh_down'], 'L1_ffn_rt_gate': _L1_ffn_in['rt_gate'], 'L1_ffn_rt_up': _L1_ffn_in['rt_up'], 'L1_ffn_rt_down': _L1_ffn_in['rt_down']}

def reference(x, ctx_1024, mask_BxS2_bk1, L0_xattn_Wq, L0_xattn_bq, L0_xattn_Wk, L0_xattn_bk, L0_xattn_Wv, L0_xattn_bv, L0_xattn_Wo, L0_xattn_bo, L0_attn_ln_w, L0_attn_ln_b, L0_attn_qkv_w, L0_attn_qkv_b, L0_attn_out_w, L0_attn_out_b, L0_ffn_wqkv, L0_ffn_q_scale, L0_ffn_k_scale, L0_ffn_wo, L0_ffn_ln_g, L0_ffn_ln_b, L0_ffn_w1, L0_ffn_b1, L0_ffn_w2, L0_ffn_b2, L1_xattn_Wq, L1_xattn_bq, L1_xattn_Wk, L1_xattn_bk, L1_xattn_Wv, L1_xattn_bv, L1_xattn_Wo, L1_xattn_bo, L1_attn_W_spin, L1_attn_b_spin, L1_attn_W_global, L1_attn_W_J, L1_attn_beta, L1_ffn_gate_w, L1_ffn_sh_gate, L1_ffn_sh_up, L1_ffn_sh_down, L1_ffn_rt_gate, L1_ffn_rt_up, L1_ffn_rt_down):
    import jax
    import jax.numpy as jnp

    def _L0_xattn_ref(v, k, q, Wq, bq, Wk, bk, Wv, bv, Wo, bo):
        import jax, jax.numpy as jnp
        import numpy as np
        B, S, D, H = (2, 256, 128, 16)
        DEPTH = D // H

        def _split_heads(x):
            b, s, _ = x.shape
            return x.reshape(b, s, H, DEPTH).transpose(0, 2, 1, 3)
        qh = _split_heads(q @ Wq + bq)
        kh = _split_heads(k @ Wk + bk)
        vh = _split_heads(v @ Wv + bv)
        logits = jnp.einsum('bhsd,bhtd->bhst', qh, kh) / jnp.sqrt(jnp.asarray(DEPTH, qh.dtype))
        attn = jax.nn.softmax(logits, axis=-1)
        out = jnp.einsum('bhst,bhtd->bhsd', attn, vh)
        out = out.transpose(0, 2, 1, 3).reshape(out.shape[0], -1, D)
        return out @ Wo + bo

    def _L0_attn_ref(x, ln_w, ln_b, qkv_w, qkv_b, out_w, out_b):
        import jax, jax.numpy as jnp
        import numpy as np
        DIM = 128
        NUM_HEADS = 16
        HEAD_DIM = DIM // NUM_HEADS
        EPS_NORM = 1e-12
        EPS_LN = 1e-05
        B, N, D = x.shape
        mu = jnp.mean(x, axis=-1, keepdims=True)
        var = jnp.mean(jnp.square(x - mu), axis=-1, keepdims=True)
        h = (x - mu) / jnp.sqrt(var + EPS_LN) * ln_w + ln_b
        qkv = h @ qkv_w.T + qkv_b
        qkv = qkv.reshape(B, N, 3, NUM_HEADS, HEAD_DIM)
        q, k, v = (jnp.transpose(qkv[:, :, i], (0, 2, 1, 3)) for i in range(3))
        q = q / jnp.maximum(jnp.linalg.norm(q, axis=-1, keepdims=True), EPS_NORM)
        k = k / jnp.maximum(jnp.linalg.norm(k, axis=-1, keepdims=True), EPS_NORM)
        scale = HEAD_DIM ** 0.5
        attn = jnp.einsum('bhqd,bhkd->bhqk', q, k) * scale
        attn = jax.nn.softmax(attn, axis=-1)
        out = jnp.einsum('bhqk,bhkd->bhqd', attn, v)
        out = jnp.transpose(out, (0, 2, 1, 3)).reshape(B, N, D)
        return x + out @ out_w.T + out_b

    def _L0_ffn_ref(x, wqkv, q_scale, k_scale, wo, ln_g, ln_b, w1, b1, w2, b2):
        import jax, jax.numpy as jnp
        import numpy as np
        DIM = 128
        DEPTH = 2
        HEADS = 8
        DIM_HEAD = 64
        WINDOW = 64
        INNER = HEADS * DIM_HEAD
        HID = int(DIM * 4 * 2 / 3)
        B, N = (2, 1024)
        QK_SCALE = 8.0

        def shift_token(t):
            t1, t2 = jnp.split(t, 2, axis=-1)
            t2 = jnp.pad(t2, ((0, 0), (1, 0), (0, 0)))[:, :-1]
            return jnp.concatenate([t1, t2], axis=-1)

        def l2norm(t):
            return t / jnp.clip(jnp.linalg.norm(t, axis=-1, keepdims=True), 1e-12)

        def rotate_half(x):
            x1, x2 = jnp.split(x, 2, axis=-1)
            return jnp.concatenate([-x2, x1], axis=-1)

        def rotary_xpos(q, k):
            n = q.shape[-2]
            half_idx = jnp.arange(0, DIM_HEAD, 2, dtype=jnp.float32)
            inv_freq = 1.0 / 10000.0 ** (half_idx / DIM_HEAD)
            t = jnp.arange(n, dtype=jnp.float32)
            freqs = t[:, None] * inv_freq[None, :]
            freqs = jnp.concatenate([freqs, freqs], axis=-1)
            base = (half_idx + 0.4 * DIM_HEAD) / (1.4 * DIM_HEAD)
            power = (t - n // 2) / float(WINDOW // 2)
            scale = base[None, :] ** power[:, None]
            scale = jnp.concatenate([scale, scale], axis=-1)
            cos, sin = (jnp.cos(freqs), jnp.sin(freqs))
            q = q * cos * scale + rotate_half(q) * sin * scale
            k = k * cos / scale + rotate_half(k) * sin / scale
            return (q, k)

        def local_attention(q, k, v):
            b, h, n, d = q.shape
            w = n // WINDOW
            bq = q.reshape(b, h, w, WINDOW, d) * QK_SCALE
            bk = k.reshape(b, h, w, WINDOW, d)
            bv = v.reshape(b, h, w, WINDOW, d)

            def look_around(t):
                p = jnp.pad(t, ((0, 0), (0, 0), (1, 0), (0, 0), (0, 0)))
                return jnp.concatenate([p[:, :, :w], p[:, :, 1:]], axis=3)
            bk, bv = (look_around(bk), look_around(bv))
            bt = jnp.arange(n).reshape(w, WINDOW)
            btp = jnp.pad(bt, ((1, 0), (0, 0)), constant_values=-1)
            btk = jnp.concatenate([btp[:w], btp[1:]], axis=1)
            sim = jnp.einsum('bhwid,bhwjd->bhwij', bq, bk)
            i = bt[:, :, None]
            j = btk[:, None, :]
            mask = (i < j) | (i > j + WINDOW) | (j == -1)
            sim = jnp.where(mask, -jnp.finfo(sim.dtype).max, sim)
            attn = jax.nn.softmax(sim, axis=-1)
            out = jnp.einsum('bhwij,bhwjd->bhwid', attn, bv)
            return out.reshape(b, h, n, d)

        def _layer(x, wqkv, qs, ksc, wo, lg, lb, w1, b1, w2, b2):
            b, n, _ = x.shape
            h = shift_token(x)
            qkv = h @ wqkv
            q, k, v = jnp.split(qkv, 3, axis=-1)
            to_heads = lambda t: t.reshape(b, n, HEADS, DIM_HEAD).transpose(0, 2, 1, 3)
            q, k, v = (to_heads(q), to_heads(k), to_heads(v))
            q = l2norm(q) * qs
            k = l2norm(k) * ksc
            q, k = rotary_xpos(q, k)
            o = local_attention(q, k, v)
            o = o.transpose(0, 2, 1, 3).reshape(b, n, INNER)
            x = x + o @ wo
            h = shift_token(x)
            mu = h.mean(-1, keepdims=True)
            var = h.var(-1, keepdims=True)
            h = (h - mu) / jnp.sqrt(var + 1e-05) * lg + lb
            h = h @ w1 + b1
            a, g = jnp.split(h, 2, axis=-1)
            h = a * jax.nn.gelu(g, approximate=False)
            x = x + h @ w2 + b2
            return x
        for l in range(DEPTH):
            x = _layer(x, wqkv[l], q_scale[l], k_scale[l], wo[l], ln_g[l], ln_b[l], w1[l], b1[l], w2[l], b2[l])
        return x

    def _L1_xattn_ref(value, key, query, key_padding_mask, Wq, bq, Wk, bk, Wv, bv, Wo, bo):
        import jax, jax.numpy as jnp
        import numpy as np
        D_MODEL = 128
        NUM_HEADS = 16
        DEPTH = D_MODEL // NUM_HEADS
        B, S = (4, 256)
        NEG_INF = float('-inf')

        def _split_heads(x, b):
            return x.reshape(b, -1, NUM_HEADS, DEPTH).transpose(0, 2, 1, 3)
        b = query.shape[0]
        q = _split_heads(query @ Wq + bq, b)
        k = _split_heads(key @ Wk + bk, b)
        v = _split_heads(value @ Wv + bv, b)
        logits = jnp.einsum('bhqd,bhkd->bhqk', q, k) / jnp.sqrt(jnp.asarray(DEPTH, q.dtype))
        logits = jnp.where(key_padding_mask[:, None, None, :], logits, NEG_INF)
        attn = jax.nn.softmax(logits, axis=-1)
        out = jnp.einsum('bhqk,bhkd->bhqd', attn, v)
        out = out.transpose(0, 2, 1, 3).reshape(b, -1, D_MODEL)
        return out @ Wo + bo

    def _L1_attn_ref(x, W_spin, b_spin, W_global, W_J, beta):
        import jax, jax.numpy as jnp
        import numpy as np
        B, N, D_IN, D_OUT = (4, 256, 128, 128)
        s = jnp.einsum('bni,oi->bno', x, W_spin) + b_spin
        mean_field = jnp.mean(s, axis=1, keepdims=True)
        global_influence = jnp.einsum('bmd,od->bmo', mean_field, W_global)
        energy_fields = jnp.einsum('bnd,od->bno', s, W_J)
        scale = 1.0 / jnp.sqrt(jnp.float32(s.shape[2]))
        scores = jnp.einsum('bnd,bmd->bnm', energy_fields, s) * scale
        affinities = jax.nn.softmax(scores, axis=-1)
        local_field = jnp.einsum('bnm,bmd->bnd', affinities, s)
        return jnp.tanh(beta * (s + global_influence + local_field))

    def _L1_ffn_ref(hidden_states, gate_w, sh_gate, sh_up, sh_down, rt_gate, rt_up, rt_down):
        import jax, jax.numpy as jnp
        import numpy as np
        H = 128
        I = 256
        E = 8
        B, S = (2, 128)

        def _swiglu(x, wg, wu, wd):
            return jax.nn.silu(x @ wg) * (x @ wu) @ wd
        b, s, h = hidden_states.shape
        x = hidden_states.reshape(-1, h)
        logits = x @ gate_w
        top_val = jnp.max(logits, axis=-1, keepdims=True)
        top_id = jnp.argmax(logits, axis=-1)
        score = jax.nn.sigmoid(top_val)
        xs = x * score
        g = jnp.einsum('th,ehi->eti', xs, rt_gate)
        u = jnp.einsum('th,ehi->eti', xs, rt_up)
        act = jax.nn.silu(g) * u
        y = jnp.einsum('eti,eih->eth', act, rt_down)
        onehot = jax.nn.one_hot(top_id, E, dtype=x.dtype)
        routed = jnp.einsum('eth,te->th', y, onehot)
        shared = _swiglu(x, sh_gate, sh_up, sh_down)
        return (shared + routed).reshape(b, s, h)
    x = x + _L0_xattn_ref(ctx_1024, ctx_1024, _layernorm(x, axis=-1), L0_xattn_Wq, L0_xattn_bq, L0_xattn_Wk, L0_xattn_bk, L0_xattn_Wv, L0_xattn_bv, L0_xattn_Wo, L0_xattn_bo)
    x = x + _L0_attn_ref(_layernorm(x, axis=-1), L0_attn_ln_w, L0_attn_ln_b, L0_attn_qkv_w, L0_attn_qkv_b, L0_attn_out_w, L0_attn_out_b)
    x = x + _L0_ffn_ref(_layernorm(x, axis=-1), L0_ffn_wqkv, L0_ffn_q_scale, L0_ffn_k_scale, L0_ffn_wo, L0_ffn_ln_g, L0_ffn_ln_b, L0_ffn_w1, L0_ffn_b1, L0_ffn_w2, L0_ffn_b2)
    x = x + _L1_xattn_ref(ctx_1024, ctx_1024, _layernorm(x, axis=-1), mask_BxS2_bk1, L1_xattn_Wq, L1_xattn_bq, L1_xattn_Wk, L1_xattn_bk, L1_xattn_Wv, L1_xattn_bv, L1_xattn_Wo, L1_xattn_bo)
    x = x + _L1_attn_ref(_layernorm(x, axis=-1), L1_attn_W_spin, L1_attn_b_spin, L1_attn_W_global, L1_attn_W_J, L1_attn_beta)
    x = x + _L1_ffn_ref(_layernorm(x, axis=-1), L1_ffn_gate_w, L1_ffn_sh_gate, L1_ffn_sh_up, L1_ffn_sh_down, L1_ffn_rt_gate, L1_ffn_rt_up, L1_ffn_rt_down)
    return x

_drawn_inputs = setup_inputs


def setup_inputs(seed=0):
    import zlib

    import numpy as np

    out = dict(_drawn_inputs(seed))
    spreads = {'L0_xattn_bq': (0.0, 0.338),
     'L0_xattn_bk': (0.0, 2.0),
     'L0_xattn_bv': (0.0, 0.1),
     'L0_xattn_bo': (0.0, 0.1),
     'L0_attn_ln_w': (1.0, 0.6),
     'L0_attn_ln_b': (0.0, 0.551),
     'L0_attn_qkv_b': (0.0, 0.39),
     'L0_attn_out_b': (0.0, 0.1),
     'L0_ffn_q_scale': (1.0, 0.6),
     'L0_ffn_k_scale': (1.0, 0.6),
     'L0_ffn_ln_g': (1.0, 0.6),
     'L0_ffn_ln_b': (0.0, 0.8),
     'L0_ffn_b1': (0.0, 0.8),
     'L0_ffn_b2': (0.0, 0.633),
     'L1_xattn_bq': (0.0, 2.0),
     'L1_xattn_bk': (0.0, 2.0),
     'L1_xattn_bv': (0.0, 0.8),
     'L1_xattn_bo': (0.0, 0.8)}
    factors = {'L0_ffn_w1': 5.77,
     'L0_ffn_w2': 8.0,
     'L1_attn_W_J': 61.627,
     'L1_xattn_Wq': 3.967,
     'L1_xattn_Wk': 3.21,
     'L1_attn_b_spin': 8.0,
     'L1_attn_W_global': 7.304}
    for name, (base, spread) in spreads.items():
        noise = np.random.default_rng([zlib.crc32(name.encode()), seed]).standard_normal(out[name].shape)
        drawn = base * np.exp(spread * noise) if base else spread * noise
        out[name] = jnp.asarray(drawn.astype(out[name].dtype))
    for name, factor in factors.items():
        out[name] = (out[name] * factor).astype(out[name].dtype)
    return out
```

```python
import concourse.bass as bass
from concourse import mybir
from contextlib import ExitStack

F32 = mybir.dt.float32
BF16 = mybir.dt.bfloat16
U8 = mybir.dt.uint8
ALU = mybir.AluOpType
ACT = mybir.ActivationFunctionType
AX = mybir.AxisListType

P = 128
B = 4
D = 128
H = 16
HD = D // H
CTX = 2048
TILES = CTX // P
PAIRS = H // 2
QUADS = H // 4
BANK = 512
CHUNKS = CTX // BANK
VW = HD + 1
STACK = 6 * HD
PART_K = (0, 0, 1, 1, 2, 0)
PART_Q = (0, 1, 0, 1, 0, 2)
MASK_ROW = 2 * STACK
KROWS_MAX = MASK_ROW + 1
KROWS_EXP = MASK_ROW + 4
MASKED = -1.0e25
MAX_PLAN = (2, 1, 2, 1, 2, 1, 2, 1, 2, 1, 1, 0, 0, 0, 0, 0)

FH = 8
FD = 64
INNER = FH * FD
HID = 341
HT = (128, 128, 85)
E = 8
EI = 256


def spread(ap, axis, n):
    shape = list(ap.shape)
    assert shape[axis] == 1
    shape[axis] = n
    return ap.broadcast_to(shape)


def perceiver(nc, a, out):
    ctx = ExitStack()
    with ctx:
        def sb(name, shape, dt=F32):
            return ctx.enter_context(nc.sbuf_tensor(name, shape, dt))

        sems, loads = {}, {}

        def sem(name):
            if name not in sems:
                sems[name] = ctx.enter_context(nc.semaphore(name))
            return sems[name]

        NORMS = ("xattn0", "a0", "a1", "f0", "g0", "g1", "xattn1", "s1", "m1")
        APART = {"norm_ready": ("f0",), "normT_psum": ("a0", "f0"), "normT_ready": ("a0", "f0")}

        def nth(signal, tag):
            return [t for t in NORMS if t not in APART.get(signal, ())].index(tag) + 1

        x = sb("x", [P, B, D])
        ident = sb("ident", [P, P])
        ident_bf = sb("ident_bf", [P, P], BF16)
        ctx_in = sb("ctx_in", [P, TILES, D])
        ctxT = sb("ctxT", [P, CTX])
        k_part = [sb(f"k_part{i}", [P, CTX], BF16) for i in range(3)]
        k_rest = sb("k_rest", [P, CTX])
        kstack = sb("kstack", [P, 2, PAIRS, CTX], BF16)
        vones = sb("vones", [P, TILES, H, VW])
        qstack = sb("qstack", [P, PAIRS, 2, B, P], BF16)
        q_part = [sb(f"q_part{i}", [P, B * P], BF16) for i in range(3)]
        row_init = sb("row_init", [P, BANK], BF16)
        probs = sb("probs", [P, 4, 4, P])
        sums = sb("sums", [P, P])
        attn_tok = sb("attn_tok", [P, B, D])
        max_part = sb("max_part", [P, 4, 2])
        neg_max = sb("neg_max", [P, 4])
        neg_rest = sb("neg_rest", [P, 4])
        neg_split = sb("neg_split", [P, 4, 4], BF16)
        rden = sb("rden", [P, 4])
        wx = [{n: sb(f"wx{l}_{n}", [P, D]) for n in ("q", "k", "v", "o")} for l in range(2)]
        bx = [{"q": sb(f"bx{l}_q", [P, 1]), "k": sb(f"bx{l}_k", [P, 1]),
               "v": sb(f"bx{l}_v", [P, D]), "o": sb(f"bx{l}_o", [P, D])} for l in range(2)]
        wqkv0 = sb("wqkv0", [P, 3 * D])
        bqkv0 = sb("bqkv0", [P, 3 * D])
        wout0 = sb("wout0", [P, D])
        bout0 = sb("bout0", [P, D])
        lnw0 = sb("lnw0", [P, 1])
        lnb0 = sb("lnb0", [P, 1])
        headmask = sb("headmask", [P, H])
        wqkvf = sb("wqkvf", [P, 2, 3 * INNER])
        wof = sb("wof", [P, 2, 4, D])
        w1f = sb("w1f", [P, 2, 2 * HID])
        w2f = sb("w2f", [P, 2, 3, D])
        lgf = sb("lgf", [P, 2])
        lbf = sb("lbf", [P, 2])
        b1f = sb("b1f", [P, 2, 2, 3])
        b2f = sb("b2f", [P, 2, D])
        rot = sb("rot", [P, 4, FD])
        rot_scale = sb("rot_scale", [P, 2, 4, FD])
        rotl = sb("rotl", [P, 2, 4, FD])
        band = sb("band", [P, P])
        band_bf = sb("band_bf", [P, P], BF16)
        shift = sb("shift", [P, P])
        wspin = sb("wspin", [P, D])
        bspin_col = sb("bspin_col", [P, 1])
        bspin_row = sb("bspin_row", [P, D])
        wglob = sb("wglob", [P, D])
        wj = sb("wj", [P, D])
        beta = sb("beta", [P, 1])
        wgate = sb("wgate", [P, E])
        erank = sb("erank", [P, B, E])
        mask_u8 = sb("mask_u8", [P, B * CTX // P], U8)
        mask_bias = sb("mask_bias", [P, B * CTX // P], BF16)
        ones4 = sb("ones4", [P, 4])
        hT = sb("hT", [P, B, P])
        half_neg = sb("half_neg", [P, B])
        stats = sb("stats", [P, B, 6])
        meanvar = sb("meanvar", [P, B, 2])
        veps = sb("veps", [P, B])
        rstd = sb("rstd", [P, B])
        xn = sb("xn", [P, B, D])
        xn2 = sb("xn2", [P, B, D])
        xnT = sb("xnT", [P, B, P])
        xres = sb("xres", [P, B, D])
        ytmp = sb("ytmp", [P, B, D])
        y = sb("y", [P, B, D])

        q_rest = [t[:, :, :].rearrange("p b d -> p (b d)") for t in (ytmp, xres)]

        scratch = kstack[:, :, :, :].rearrange("p a b c -> p (a b c)").bitcast(F32)
        scratch_at = [0]

        def carve(*shape):
            n = 1
            for s in shape:
                n *= s
            lo = scratch_at[0]
            scratch_at[0] += n
            assert scratch_at[0] <= PAIRS * CTX
            v = scratch[:, lo:lo + n]
            if len(shape) == 2:
                v = v.rearrange("p (a b) -> p a b", a=shape[0])
            if len(shape) == 3:
                v = v.rearrange("p (a b c) -> p a b c", a=shape[0], b=shape[1])
            return v

        ps = ctx.enter_context(nc.psum_tensor("ps", [P, 8, BANK], F32))
        E0, OB, XB = 4, 6, 7

        k_dram = nc.dram_tensor("k_dram", (3, P, CTX), BF16, kind="Internal").ap()
        m_dram = nc.dram_tensor("m_dram", (B, CTX), BF16, kind="Internal").ap()
        q_dram = nc.dram_tensor("q_dram", (3, P, B * P), BF16, kind="Internal").ap()

        block = ctx.enter_context(nc.Block())

        def flat(ap):
            return ap.rearrange("p b q -> p (b q)")

        a_qkv = carve(B, 3 * D)
        a_sq = carve(B, 2 * D)
        a_ss = sb("a_ss", [P, B, 2 * H])
        a_norm = sb("a_norm", [P, B, 2 * H])
        a_inv = sb("a_inv", [P, B, 2 * H])
        a_qk = carve(B, 2 * D)
        a_v = carve(B, H, VW)
        a_kT = carve(B, P)
        a_qblk = [carve(H, P) for _ in range(2)]
        a_probs = [carve(8, P) for _ in range(2)]
        a_sums = carve(4, P)
        a_rden = sb("a_rden", [P, H])
        scratch_at[0] = 0
        f_sq = [carve(2 * INNER) for _ in range(2)]
        f_cos = [carve(2 * INNER) for _ in range(2)]
        f_sin = [carve(2 * INNER) for _ in range(2)]
        f_qk = [carve(2 * INNER) for _ in range(B)]
        f_v = [carve(INNER) for _ in range(B)]
        f_qT = carve(4, P)
        f_kT = carve(4, P)
        f_oT = carve(4, P)
        f_probs = f_sq[0].rearrange("p (h k) -> p h k", h=FH)
        f_probsT = f_cos[0].rearrange("p (h k) -> p h k", h=FH)
        f_gelu = [f_sin[0][:, 0:512], f_sin[0][:, 512:1024], f_sin[1][:, 0:512]]
        f_act = f_qk[0].rearrange("p (a n) -> p a n", a=2), f_qk[1].rearrange("p (a n) -> p a n", a=2)
        f_act = [f_act[0][:, 0, :], f_act[0][:, 1, :], f_act[1][:, 0, :]]
        f_shift = f_cos[1][:, 0:512].rearrange("p (b d) -> p b d", b=B)
        f_ss = sb("f_ss", [P, B, 16])
        f_norm = sb("f_norm", [P, B, 16])
        f_inv = sb("f_inv", [P, B, 16])
        f_qs = sb("f_qs", [P, B, FH])
        f_max = sb("f_max", [P, FH])
        f_bias = sb("f_bias", [P, FH])
        f_den = sb("f_den", [P, FH])
        f_rden = sb("f_rden", [P, FH])
        scratch_at[0] = 0
        gate_up = scratch[:, 0:4096].rearrange("p (a e n) -> p a e n", a=2, e=E)
        down = scratch[:, 4096:6144].rearrange("p (e t n) -> p e t n", e=E, t=2)
        sh_gate_up = scratch[:, 6144:6656].rearrange("p (a n) -> p a n", a=2)
        sh_down = scratch[:, 6656:6912].rearrange("p (a n) -> p a n", a=2)
        scratch_at[0] = 6912
        s_T = carve(B, P)
        s_tok = carve(B, D)
        s_eT = carve(B, P)
        s_probs = carve(B, P)
        s_probsT = carve(B, P)
        s_meanrows = carve(B, P)
        m_xs = carve(B, D)
        m_xsT = carve(B, P)
        m_xe = [carve(B, P) for _ in range(2)]
        m_silu = [carve(B * P) for _ in range(3)]
        m_act = [carve(B, P) for _ in range(3)]
        s_mean = sb("s_mean", [P, B])
        s_max = sb("s_max", [P, B])
        s_bias = sb("s_bias", [P, B])
        s_den = sb("s_den", [P, B])
        s_rden = sb("s_rden", [P, B])
        m_logit = sb("m_logit", [P, B, E])
        m_top = sb("m_top", [P, B])
        m_tanh = sb("m_tanh", [P, B])
        m_score = sb("m_score", [P, B])
        m_rank = sb("m_rank", [P, B, E])
        m_first = sb("m_first", [P, B])
        m_eq = sb("m_eq", [P, B, E])
        m_hot = sb("m_hot", [P, B, E], BF16)
        MU = 2 * E + 2

        def unit_weights(k):
            e, half = k // 2, k % 2
            cols = slice(half * P, (half + 1) * P)
            if e < E:
                return gate_up[:, 0, e, cols], gate_up[:, 1, e, cols], down[:, e, half, :]
            return sh_gate_up[:, 0, cols], sh_gate_up[:, 1, cols], sh_down[:, half, :]

        def pe_self_attention(pe, transposes):
            transposes(xn2, XB, "norm_ready", nth("norm_ready", "a1"), "normT_psum")
            pe.wait_ge(sem("w_a0"), loads["w_a0"])
            pe.wait_ge(sem("normT_ready"), nth("normT_ready", "a1"))
            for b in range(B):
                pe.matmul(ps[:, b, 0:3 * D], xnT[:, b, :], wqkv0[:, :], start=True, stop=True)\
                  .then_inc(sem("a_qkv_psum"), 1)
            pe.wait_ge(sem("a_qk_ready"), B)
            for b in range(B):
                for i in range(2):
                    last = pe.transpose(ps[:, 4 + i, b * P:(b + 1) * P], a_qk[:, b, i * D:(i + 1) * D], ident[:, :])
            last.then_inc(sem("a_qkT_psum"), 1)

            def scores(u):
                b, half = u // 2, u % 2
                if half == 0:
                    pe.wait_ge(sem("a_qblk_ready"), b + 1)
                if u == 0:
                    pe.wait_ge(sem("a_kT_ready"), 1)
                if u >= 2:
                    pe.wait_ge(sem("a_exp_ready"), u - 1)
                for c in range(2):
                    lo = 8 * half + 4 * c
                    last = pe.matmul(ps[:, 2 * (u % 2) + c, :], a_kT[:, b, :], flat(a_qblk[b % 2][:, lo:lo + 4, :]),
                                     start=True, stop=True)
                last.then_inc(sem("a_scores_psum"), 1)

            def weigh(u):
                b, half = u // 2, u % 2
                pe.wait_ge(sem("a_exp_ready"), u + 1)
                if half == 0:
                    pe.wait_ge(sem("a_v_ready"), b + 2)
                    if b:
                        pe.wait_ge(sem("a_sums_ready"), b)
                for i in range(8):
                    h = 8 * half + i
                    last = pe.matmul(ps[32 * (h % 4):32 * (h % 4) + VW, OB, h // 4 * P:(h // 4 + 1) * P],
                                     a_v[:, b, h, :], a_probs[u % 2][:, i, :], start=True, stop=True)
                last.then_inc(sem("a_probs_used"), 1)

            scores(0)
            scores(1)
            for u in range(2 * B):
                weigh(u)
                if u + 2 < 2 * B:
                    scores(u + 2)
                if u % 2:
                    b = u // 2
                    pe.wait_ge(sem("a_sums_ready"), b + 1)
                    if b:
                        pe.wait_ge(sem("a_attended"), b)
                    for j in range(4):
                        last = pe.transpose(ps[:, XB, j * P:(j + 1) * P], a_sums[:, j, :], ident[:, :])
                    last.then_inc(sem("a_sumsT_psum"), 1)
            transposes(attn_tok, XB, "a_attended", B, "a_attnT_psum")
            pe.wait_ge(sem("a_attnT_ready"), 1)
            for b in range(B):
                last = pe.matmul(ps[:, OB, b * P:(b + 1) * P], xnT[:, b, :], wout0[:, :], start=True, stop=True)
            last.then_inc(sem("a_out_psum"), 1)

        def pe_local_attention(pe, transposes, l):
            n = l * B
            transposes(y, XB, "f_y_ready", 2 * l + 1, "f_yT_psum")
            pe.wait_ge(sem("f_hT_ready"), l + 1)
            for b in range(B):
                if b >= 2:
                    pe.wait_ge(sem("f_rot_ready"), n + b - 1)
                    pe.wait_ge(sem("f_v_ready"), n + b - 1)
                for i, bank in enumerate((2 * (b % 2), 2 * (b % 2) + 1, 4 + b % 2)):
                    last = pe.matmul(ps[:, bank, :], hT[:, b, :], wqkvf[:, l, i * INNER:(i + 1) * INNER],
                                     start=True, stop=True)
                last.then_inc(sem("f_qkv_psum"), 1)

            def qk_rows(b):
                pe.wait_ge(sem("f_kn_ready"), n + b + 1)
                if b:
                    pe.wait_ge(sem("f_qT_ready"), n + b)
                    pe.wait_ge(sem("f_kT_ready"), n + b)
                for i in range(2):
                    for t in range(4):
                        lo = i * INNER + t * P
                        last = pe.transpose(ps[:, i, t * P:(t + 1) * P], f_qk[b][:, lo:lo + P], ident[:, :])
                last.then_inc(sem("f_qkT_psum"), 1)

            def scores(b):
                pe.wait_ge(sem("f_qT_ready"), n + b + 1)
                pe.wait_ge(sem("f_kT_ready"), n + b + 1)
                if b:
                    pe.wait_ge(sem("f_exp_ready"), n + b)
                for c in range(2):
                    mask = spread(band_bf[:, :].rearrange("p (a k) -> p a k", a=1), 1, 4)
                    pe.matmul(ps[:, 2 + c, :].rearrange("p (a k) -> p a k", a=4), ident_bf[:, :], mask,
                              start=True, stop=False, skip_group_check=True)
                    for i in range(4):
                        h = 2 * i + c
                        rows = slice(FD * (h % 2), FD * (h % 2) + FD)
                        last = pe.matmul(ps[:, 2 + c, i * P:(i + 1) * P], f_qT[rows, h // 2, :], f_kT[rows, h // 2, :],
                                         start=False, stop=(i == 3), skip_group_check=True)
                last.then_inc(sem("f_scores_psum"), 1)

            def weigh(b):
                pe.wait_ge(sem("f_probsTa_ready"), n + b + 1)
                pe.wait_ge(sem("f_probsTb_ready"), n + b + 1)
                if b:
                    pe.wait_ge(sem("f_oT_ready"), n + b)
                for h in range(FH):
                    last = pe.matmul(ps[FD * (h % 2):FD * (h % 2) + FD, OB, h // 2 * P:(h // 2 + 1) * P],
                                     f_v[b][:, h * FD:(h + 1) * FD], f_probsT[:, h, :], start=True, stop=True)
                last.then_inc(sem("f_o_psum"), 1)

            def probs_rows(b):
                pe.wait_ge(sem("f_probs_ready"), n + b + 1)
                if b:
                    pe.wait_ge(sem("f_probsTa_ready"), n + b)
                    pe.wait_ge(sem("f_probsTb_ready"), n + b)
                for h in range(FH):
                    last = pe.transpose(ps[:, 4 + h // 4, h % 4 * P:(h % 4 + 1) * P], f_probs[:, h, :], ident[:, :])
                last.then_inc(sem("f_probsT_psum"), 1)

            qk_rows(0)
            scores(0)
            for b in range(B):
                if b + 1 < B:
                    qk_rows(b + 1)
                probs_rows(b)
                if b + 1 < B:
                    scores(b + 1)
                weigh(b)
                pe.wait_ge(sem("f_oT_ready"), n + b + 1)
                for t in range(4):
                    last = pe.matmul(ps[:, XB, b * P:(b + 1) * P], f_oT[:, t, :], wof[:, l, t, :],
                                     start=(t == 0), stop=(t == 3))
                last.then_inc(sem("f_attn_psum"), 1)

        def pe_gated(pe, transposes, l):
            pe.wait_ge(sem("f_y_ready"), 2 * l + 2)
            pe.matmul(ps[:, 0, 0:B * 64].rearrange("p (b d) -> p b d", b=B), shift[:, :], y[:, :, 64:D],
                      start=True, stop=True).then_inc(sem("f_shift_psum"), 1)
            transposes(xn, XB, "norm_ready", nth("norm_ready", f"g{l}"), "normT_psum")
            pe.wait_ge(sem("normT_ready"), nth("normT_ready", f"g{l}"))
            for m in range(3):
                for ag in range(2):
                    lo = ag * HID + m * P
                    last = pe.matmul(ps[0:HT[m], (2 + 2 * m + ag) % 6, :], w1f[:, l, lo:lo + HT[m]], flat(xnT[:, :, :]),
                                     start=True, stop=True)
                last.then_inc(sem("f_w1_psum"), 1)
            pe.wait_ge(sem("f_act_ready"), 3 * l + 3)
            for b in range(B):
                for m in range(3):
                    last = pe.matmul(ps[:, OB, b * P:(b + 1) * P], f_act[m][0:HT[m], b * P:(b + 1) * P],
                                     w2f[0:HT[m], l, m, :], start=(m == 0), stop=(m == 2))
            last.then_inc(sem("f_w2_psum"), 1)

        def pe_middle0(pe, transposes):
            pe_self_attention(pe, transposes)
            pe.wait_ge(sem("w_f0"), loads["w_f0"])
            pe.wait_ge(sem("band_ready"), 1)
            for l in range(2):
                pe_local_attention(pe, transposes, l)
                pe_gated(pe, transposes, l)

        def pe_middle1(pe, transposes):
            transposes(xn, XB, "norm_ready", nth("norm_ready", "s1"), "normT_psum")
            pe.wait_ge(sem("normT_ready"), nth("normT_ready", "s1"))
            pe.wait_ge(sem("w_a1"), loads["w_a1"])
            pe.matmul(ps[:, 0, :], wspin[:, :], flat(xnT[:, :, :]), start=True, stop=True).then_inc(sem("s_T_psum"), 1)
            for b in range(B):
                last = pe.matmul(ps[:, 1, b * P:(b + 1) * P], xnT[:, b, :], wspin[:, :], start=True, stop=True)
            last.then_inc(sem("s_tok_psum"), 1)
            pe.wait_ge(sem("s_T_ready"), 1)
            pe.matmul(ps[:, 2, :], wj[:, :], flat(s_T[:, :, :]), start=True, stop=True).then_inc(sem("s_eT_psum"), 1)
            pe.wait_ge(sem("s_eT_ready"), 1)
            for b in range(B):
                last = pe.matmul(ps[:, 3, b * P:(b + 1) * P], s_eT[:, b, :], s_T[:, b, :], start=True, stop=True)
            last.then_inc(sem("s_scores_psum"), 1)
            transposes(s_probs, XB, "s_probs_ready", 1, "s_probsT_psum")
            pe.wait_ge(sem("s_probsT_ready"), 1)
            pe.wait_ge(sem("s_tok_ready"), 1)
            pe.wait_ge(sem("s_mean_ready"), 1)
            for b in range(B):
                pe.matmul(ps[:, 4, b * P:(b + 1) * P], s_probsT[:, b, :], s_tok[:, b, :], start=True, stop=False)
                last = pe.matmul(ps[:, 4, b * P:(b + 1) * P], s_meanrows[:, b, :], wglob[:, :], start=False, stop=True)
            last.then_inc(sem("s_field_psum"), 1)

            transposes(xn, XB, "norm_ready", nth("norm_ready", "m1"), "normT_psum")
            pe.wait_ge(sem("normT_ready"), nth("normT_ready", "m1"))
            pe.wait_ge(sem("w_m1"), loads["w_m1"])
            for b in range(B):
                last = pe.matmul(ps[:, 0, b * E:(b + 1) * E], xnT[:, b, :], wgate[:, :], start=True, stop=True)
            last.then_inc(sem("m_logit_psum"), 1)
            pe.wait_ge(sem("m_hot_ready"), 1)
            transposes(m_xs, 2, "m_xs_ready", 1, "m_xsT_psum")

            def expert_mask(e):
                if e:
                    pe.wait_ge(sem("m_xe_ready"), e)
                for b in range(B):
                    hot = spread(m_hot[:, b, e:e + 1], 1, P)
                    last = pe.matmul(ps[:, 1, b * P:(b + 1) * P], hot, ident_bf[:, :], start=True, stop=True)
                last.then_inc(sem("m_mask_psum"), 1)

            def gate_and_up(k):
                e = k // 2
                if k % 2 == 0 and e < E:
                    pe.wait_ge(sem("m_xe_ready"), e + 1)
                if k >= 3:
                    pe.wait_ge(sem("m_act_ready"), k - 2)
                wg, wu, _ = unit_weights(k)
                src = flat(m_xe[e % 2][:, :, :] if e < E else xnT[:, :, :])
                pe.matmul(ps[:, 2 + 2 * (k % 3), :], wg, src, start=True, stop=True)
                pe.matmul(ps[:, 3 + 2 * (k % 3), :], wu, src, start=True, stop=True).then_inc(sem("m_gu_psum"), 1)

            def project_down(k):
                pe.wait_ge(sem("m_act_ready"), k + 1)
                for b in range(B):
                    last = pe.matmul(ps[:, 0, b * P:(b + 1) * P], m_act[k % 3][:, b, :], unit_weights(k)[2],
                                     start=(k == 0 and b == 0), stop=(k == MU - 1 and b == B - 1),
                                     skip_group_check=True)
                last.then_inc(sem("m_down_psum"), 1)

            expert_mask(0)
            pe.wait_ge(sem("w_e"), loads["w_e"])
            pe.wait_ge(sem("m_xsT_ready"), 1)
            for k in range(MU):
                if k % 2 == 0 and k // 2 + 1 < E:
                    expert_mask(k // 2 + 1)
                gate_and_up(k)
                if k:
                    project_down(k - 1)
            project_down(MU - 1)

        def act_middle0(act, copy):
            def rows_from(bank):
                return ps[:, bank, :].rearrange("p (b q) -> p b q", b=B)

            act.wait_ge(sem("normT_psum"), nth("normT_psum", "a1"))
            act.wait_ge(sem("w_a0"), loads["w_a0"])
            act.activation(xnT[:, :, :], rows_from(XB), ACT.Identity, bias=lnb0[:, :], scale=lnw0[:, :])\
               .then_inc(sem("normT_ready"), 1)
            for b in range(B):
                act.wait_ge(sem("a_qkv_ready"), b + 1)
                act.activation(a_sq[:, b, :], a_qkv[:, b, 0:2 * D], ACT.Square).then_inc(sem("a_sq_ready"), 1)
            act.wait_ge(sem("a_ss_ready"), B)
            act.activation(a_norm[:, :, :], a_ss[:, :, :], ACT.Sqrt).then_inc(sem("a_norm_ready"), 1)
            act.wait_ge(sem("a_qkT_psum"), 1)
            copy(a_kT[:, :, :], rows_from(5)).then_inc(sem("a_kT_ready"), 1)
            for u in range(2 * B):
                act.wait_ge(sem("a_scores_psum"), u + 1)
                if u >= 2:
                    act.wait_ge(sem("a_probs_used"), u - 1)
                bank = 2 * (u % 2)
                act.activation(flat(a_probs[u % 2][:, :, :]), ps[:, bank:bank + 2, :].rearrange("p a c -> p (a c)"),
                               ACT.Exp, scale=HD ** 0.5).then_inc(sem("a_exp_ready"), 1)
                if u % 2:
                    b = u // 2
                    act.wait_ge(sem("a_probs_used"), u + 1)
                    if b:
                        act.wait_ge(sem("a_sumsT_psum"), b)
                    copy(a_sums[:, :, :], rows_from(OB)).then_inc(sem("a_sums_ready"), 1)
            act.wait_ge(sem("a_attnT_psum"), 1)
            copy(xnT[:, :, :], rows_from(XB)).then_inc(sem("a_attnT_ready"), 1)

            act.wait_ge(sem("w_f0"), loads["w_f0"])
            for l in range(2):
                n = l * B
                act.wait_ge(sem("f_yT_psum"), l + 1)
                copy(hT[0:64, :, :], rows_from(XB)[0:64])
                copy(hT[64:P, :, 1:P], rows_from(XB)[64:P, :, 0:P - 1]).then_inc(sem("f_hT_ready"), 1)
                for b in range(B):
                    act.wait_ge(sem("f_qkv_psum"), n + b + 1)
                    if b >= 2:
                        act.wait_ge(sem("f_ss_ready"), n + b - 1)
                    bank = 2 * (b % 2)
                    act.activation(f_sq[b % 2], ps[:, bank:bank + 2, :].rearrange("p a c -> p (a c)"), ACT.Square)\
                       .then_inc(sem("f_sq_ready"), 1)
                    copy(f_v[b], ps[:, 4 + b % 2, :]).then_inc(sem("f_v_ready"), 1)
                act.wait_ge(sem("f_ss_ready"), n + B)
                act.activation(f_norm[:, :, :], f_ss[:, :, :], ACT.Sqrt).then_inc(sem("f_norm_ready"), 1)

                def q_rows(b):
                    act.wait_ge(sem("f_qkT_psum"), n + b + 1)
                    if b:
                        act.wait_ge(sem("f_scores_psum"), n + b)
                    copy(f_qT[:, :, :], ps[:, 0, :].rearrange("p (t q) -> p t q", t=4)).then_inc(sem("f_qT_ready"), 1)

                q_rows(0)
                for b in range(B):
                    act.wait_ge(sem("f_bias_ready"), n + b + 1)
                    if b:
                        act.wait_ge(sem("f_probsT_psum"), n + b)
                    for h in range(FH):
                        last = act.activation(f_probs[:, h, :], ps[:, 2 + h % 2, h // 2 * P:(h // 2 + 1) * P], ACT.Exp,
                                              bias=f_bias[:, h:h + 1], scale=f_qs[:, b, h:h + 1],
                                              accum_out=f_den[:, h:h + 1])
                    last.then_inc(sem("f_exp_ready"), 1)
                    if b + 1 < B:
                        q_rows(b + 1)
                    act.wait_ge(sem("f_probsT_psum"), n + b + 1)
                    if b:
                        act.wait_ge(sem("f_o_psum"), n + b)
                    copy(flat(f_probsT[:, 0:4, :]), ps[:, 4, :]).then_inc(sem("f_probsTa_ready"), 1)
                    act.wait_ge(sem("f_o_psum"), n + b + 1)
                    if b:
                        act.wait_ge(sem("f_attn_psum"), n + b)
                    copy(f_oT[:, :, :], ps[:, OB, :].rearrange("p (t q) -> p t q", t=4)).then_inc(sem("f_oT_ready"), 1)

                act.wait_ge(sem("normT_psum"), nth("normT_psum", f"g{l}"))
                act.activation(xnT[:, :, :], rows_from(XB), ACT.Identity, bias=lbf[:, l:l + 1], scale=lgf[:, l:l + 1])\
                   .then_inc(sem("normT_ready"), 1)
                for m in range(3):
                    act.wait_ge(sem("f_w1_psum"), 3 * l + m + 1)
                    act.activation(f_gelu[m][0:HT[m], :], ps[0:HT[m], (3 + 2 * m) % 6, :], ACT.Gelu,
                                   bias=b1f[0:HT[m], l, 1, m:m + 1]).then_inc(sem("f_gelu_ready"), 1)

        def act_middle1(act, copy):
            def rows_from(bank):
                return ps[:, bank, :].rearrange("p (b q) -> p b q", b=B)

            act.wait_ge(sem("normT_psum"), nth("normT_psum", "s1"))
            copy(xnT[:, :, :], rows_from(XB)).then_inc(sem("normT_ready"), 1)
            act.wait_ge(sem("s_T_psum"), 1)
            act.wait_ge(sem("w_a1"), loads["w_a1"])
            act.activation(s_T[:, :, :], rows_from(0), ACT.Identity, bias=bspin_col[:, :]).then_inc(sem("s_T_ready"), 1)
            act.wait_ge(sem("s_eT_psum"), 1)
            copy(s_eT[:, :, :], rows_from(2)).then_inc(sem("s_eT_ready"), 1)
            act.wait_ge(sem("s_bias_ready"), 1)
            for b in range(B):
                last = act.activation(s_probs[:, b, :], ps[:, 3, b * P:(b + 1) * P], ACT.Exp, bias=s_bias[:, b:b + 1],
                                      scale=D ** -0.5, accum_out=s_den[:, b:b + 1])
            last.then_inc(sem("s_exp_ready"), 1)
            act.wait_ge(sem("s_probsT_psum"), 1)
            copy(s_probsT[:, :, :], rows_from(XB)).then_inc(sem("s_probsT_ready"), 1)
            act.wait_ge(sem("s_sum_ready"), 1)
            act.activation(xn2[:, :, :], ytmp[:, :, :], ACT.Tanh, scale=beta[:, :]).then_inc(sem("s_tanh_ready"), 1)

            act.wait_ge(sem("normT_psum"), nth("normT_psum", "m1"))
            copy(xnT[:, :, :], rows_from(XB)).then_inc(sem("normT_ready"), 1)
            act.wait_ge(sem("m_top_ready"), 1)
            act.activation(m_tanh[:, :], m_top[:, :], ACT.Tanh, scale=0.5).then_inc(sem("m_tanh_ready"), 1)
            act.wait_ge(sem("m_xsT_psum"), 1)
            copy(m_xsT[:, :, :], rows_from(2)).then_inc(sem("m_xsT_ready"), 1)
            for k in range(MU):
                act.wait_ge(sem("m_gu_psum"), k + 1)
                if k >= 3:
                    act.wait_ge(sem("m_act_ready"), k - 2)
                act.activation(m_silu[k % 3], ps[:, 2 + 2 * (k % 3), :], ACT.Silu).then_inc(sem("m_silu_ready"), 1)

        def wide(v, n):
            return spread(v.rearrange("p (a b) -> p a b", b=1), 2, n)

        def dve_middle0(dve, link, norm):
            norm(x, xn, "a0").then_inc(sem("norm_ready"), 1)
            dve.wait_ge(sem("norm_ready"), nth("norm_ready", "a0"))
            norm(xn, xn2, "a1").then_inc(sem("norm_ready"), 1)
            dve.wait_ge(sem("w_a0"), loads["w_a0"])
            for b in range(B):
                dve.wait_ge(sem("a_qkv_psum"), b + 1)
                dve.tensor_tensor(a_qkv[:, b, :], ps[:, b, 0:3 * D], bqkv0[:, :], ALU.add)\
                   .then_inc(sem("a_qkv_ready"), 1)
            for b in range(B):
                dve.wait_ge(sem("a_sq_ready"), b + 1)
                dve.tensor_reduce(a_ss[:, b, :], a_sq[:, b, :].rearrange("p (h d) -> p h d", d=HD), AX.X, ALU.add)\
                   .then_inc(sem("a_ss_ready"), 1)
            dve.wait_ge(sem("a_norm_ready"), 1)
            link(dve.tensor_scalar(a_norm[:, :, :], a_norm[:, :, :], 1e-12, None, ALU.max))
            link(dve.reciprocal(a_inv[:, :, :], a_norm[:, :, :]))
            for b in range(B):
                dve.tensor_tensor(a_qk[:, b, :].rearrange("p (h d) -> p h d", d=HD),
                                  a_qkv[:, b, 0:2 * D].rearrange("p (h d) -> p h d", d=HD),
                                  wide(a_inv[:, b, :], HD), ALU.mult).then_inc(sem("a_qk_ready"), 1)

            def query_block(b):
                q = spread(ps[:, 4, b * P:(b + 1) * P].rearrange("p (a q) -> p a q", a=1), 1, H)
                dve.tensor_tensor(a_qblk[b % 2][:, :, :], q, wide(headmask[:, :], P), ALU.mult)\
                   .then_inc(sem("a_qblk_ready"), 1)

            dve.wait_ge(sem("a_qkT_psum"), 1)
            query_block(0)
            query_block(1)
            for b in range(B):
                if b + 2 < B:
                    dve.wait_ge(sem("a_scores_psum"), 2 * b + 2)
                    query_block(b + 2)
                dve.wait_ge(sem("a_sumsT_psum"), b + 1)
                sumsT = ps[:, XB, :].rearrange("p (h w) -> p h w", w=32)
                link(dve.reciprocal(a_rden[:, :], sumsT[:, :, HD]))
                dve.tensor_tensor(attn_tok[:, b, :].rearrange("p (h d) -> p h d", d=HD), sumsT[:, :, 0:HD],
                                  wide(a_rden[:, :], HD), ALU.mult).then_inc(sem("a_attended"), 1)
            dve.wait_ge(sem("a_out_psum"), 1)
            dve.wait_ge(sem("a_res_ready"), 2)
            link(dve.tensor_tensor(x[:, :, :], xres[:, :, :], ps[:, OB, :].rearrange("p (b d) -> p b d", b=B), ALU.add))

            dve.wait_ge(sem("w_rot"), loads["w_rot"])
            dve.tensor_copy(band_bf[:, :], band[:, :]).then_inc(sem("band_ready"), 1)
            norm(x, y, "f0").then_inc(sem("f_y_ready"), 1)
            dve.wait_ge(sem("rotl_ready"), 2)
            for l in range(2):
                n = l * B
                for b in range(B):
                    dve.wait_ge(sem("f_sq_ready"), n + b + 1)
                    dve.tensor_reduce(f_ss[:, b, :], f_sq[b % 2].rearrange("p (h d) -> p h d", d=FD), AX.X, ALU.add)\
                       .then_inc(sem("f_ss_ready"), 1)
                    if b >= 2:
                        dve.wait_ge(sem("f_rotsum_ready"), n + b - 1)
                    for i in range(2):
                        src = ps[:, 2 * (b % 2) + i, :].rearrange("p (h d) -> p h d", h=FH)
                        cols = slice(i * INNER, (i + 1) * INNER)
                        cos = spread(rotl[:, l, 2 * i:2 * i + 1, :], 1, FH)
                        dve.tensor_tensor(f_cos[b % 2][:, cols].rearrange("p (h d) -> p h d", h=FH), src, cos, ALU.mult)
                        for half in range(2):
                            to = slice(half * 32, half * 32 + 32)
                            of = slice(32 - half * 32, 64 - half * 32)
                            sin = spread(rotl[:, l, 2 * i + 1:2 * i + 2, to], 1, FH)
                            last = dve.tensor_tensor(f_sin[b % 2][:, cols].rearrange("p (h d) -> p h d", h=FH)[:, :, to],
                                                     src[:, :, of], sin, ALU.mult)
                    last.then_inc(sem("f_rot_ready"), 1)
                dve.wait_ge(sem("f_norm_ready"), l + 1)
                link(dve.tensor_scalar(f_norm[:, :, :], f_norm[:, :, :], 1e-12, None, ALU.max))
                link(dve.reciprocal(f_inv[:, :, :], f_norm[:, :, :]))
                link(dve.tensor_scalar(f_qs[:, :, :], f_inv[:, :, 0:FH], 8.0, None, ALU.mult))
                for b in range(B):
                    dve.wait_ge(sem("f_rotsum_ready"), n + b + 1)
                    k = f_qk[b][:, INNER:2 * INNER].rearrange("p (h d) -> p h d", h=FH)
                    dve.tensor_tensor(k, k, wide(f_inv[:, b, FH:2 * FH], FD), ALU.mult).then_inc(sem("f_kn_ready"), 1)

                def k_rows(b):
                    dve.wait_ge(sem("f_qkT_psum"), n + b + 1)
                    if b:
                        dve.wait_ge(sem("f_scores_psum"), n + b)
                    dve.tensor_copy(f_kT[:, :, :], ps[:, 1, :].rearrange("p (t q) -> p t q", t=4))\
                       .then_inc(sem("f_kT_ready"), 1)

                def maxima(b):
                    dve.wait_ge(sem("f_scores_psum"), n + b + 1)
                    link(dve.tensor_reduce(f_max[:, :], ps[:, 2:4, :].rearrange("p a (h k) -> p (a h) k", h=4),
                                           AX.X, ALU.max, negate=True))
                    if b:
                        dve.wait_ge(sem("f_exp_ready"), n + b)
                    dve.tensor_tensor(f_bias[:, :].rearrange("p (j e) -> p e j", e=2),
                                      f_max[:, :].rearrange("p (e j) -> p e j", e=2),
                                      f_qs[:, b, :].rearrange("p (j e) -> p e j", e=2), ALU.mult)\
                       .then_inc(sem("f_bias_ready"), 1)

                k_rows(0)
                maxima(0)
                for b in range(B):
                    dve.wait_ge(sem("f_exp_ready"), n + b + 1)
                    link(dve.reciprocal(f_rden[:, :], f_den[:, :]))
                    dve.tensor_tensor(f_probs[:, :, :], f_probs[:, :, :], wide(f_rden[:, :], P), ALU.mult)\
                       .then_inc(sem("f_probs_ready"), 1)
                    if b + 1 < B:
                        k_rows(b + 1)
                    dve.wait_ge(sem("f_probsT_psum"), n + b + 1)
                    if b:
                        dve.wait_ge(sem("f_o_psum"), n + b)
                    dve.tensor_copy(flat(f_probsT[:, 4:8, :]), ps[:, 5, :]).then_inc(sem("f_probsTb_ready"), 1)
                    if b + 1 < B:
                        maxima(b + 1)
                dve.wait_ge(sem("f_attn_psum"), n + B)
                dve.tensor_tensor(y[:, :, :], y[:, :, :], ps[:, XB, :].rearrange("p (b d) -> p b d", b=B), ALU.add)\
                   .then_inc(sem("f_y_ready"), 1)
                dve.wait_ge(sem("f_shift_psum"), l + 1)
                dve.wait_ge(sem("f_unshifted_ready"), l + 1)
                link(dve.tensor_copy(f_shift[:, :, 64:D], ps[:, 0, 0:B * 64].rearrange("p (b d) -> p b d", b=B)))
                norm(f_shift, xn, f"g{l}").then_inc(sem("norm_ready"), 1)
                for m in range(3):
                    dve.wait_ge(sem("f_gelu_ready"), 3 * l + m + 1)
                    rows = slice(0, HT[m])
                    dve.scalar_tensor_tensor(f_act[m][rows, :], ps[rows, (2 + 2 * m) % 6, :], b1f[rows, l, 0, m:m + 1],
                                             f_gelu[m][rows, :], ALU.add, ALU.mult).then_inc(sem("f_act_ready"), 1)
                dve.wait_ge(sem("f_w2_psum"), l + 1)
                dve.wait_ge(sem("f_biased_ready"), l + 1)
                dve.tensor_tensor(y[:, :, :], ytmp[:, :, :], ps[:, OB, :].rearrange("p (b d) -> p b d", b=B), ALU.add)\
                   .then_inc(sem("f_y_ready"), 1)
                dve.wait_ge(sem("f_y_ready"), 2 * l + 3)
            link(dve.tensor_tensor(x[:, :, :], x[:, :, :], y[:, :, :], ALU.add))

        def dve_middle1(dve, link, norm):
            norm(x, xn, "s1").then_inc(sem("norm_ready"), 1)
            dve.wait_ge(sem("w_a1"), loads["w_a1"])
            dve.wait_ge(sem("s_tok_psum"), 1)
            bias = spread(bspin_row[:, :].rearrange("p (a n) -> p a n", a=1), 1, B)
            dve.tensor_tensor(s_tok[:, :, :], ps[:, 1, :].rearrange("p (b d) -> p b d", b=B), bias, ALU.add)\
               .then_inc(sem("s_tok_ready"), 1)
            dve.wait_ge(sem("s_T_ready"), 1)
            link(dve.tensor_reduce(s_mean[:, :], s_T[:, :, :], AX.X, ALU.add))
            dve.tensor_scalar(s_meanrows[:, :, :], wide(s_mean[:, :], P), 1.0 / P, None, ALU.mult)\
               .then_inc(sem("s_mean_ready"), 1)
            dve.wait_ge(sem("s_scores_psum"), 1)
            link(dve.tensor_reduce(s_max[:, :], ps[:, 3, :].rearrange("p (b q) -> p b q", b=B), AX.X, ALU.max,
                                   negate=True))
            dve.tensor_scalar(s_bias[:, :], s_max[:, :], D ** -0.5, None, ALU.mult).then_inc(sem("s_bias_ready"), 1)
            dve.wait_ge(sem("s_exp_ready"), 1)
            link(dve.reciprocal(s_rden[:, :], s_den[:, :]))
            dve.tensor_tensor(s_probs[:, :, :], s_probs[:, :, :], wide(s_rden[:, :], P), ALU.mult)\
               .then_inc(sem("s_probs_ready"), 1)
            dve.wait_ge(sem("s_field_psum"), 1)
            dve.wait_ge(sem("s_tok_ready"), 1)
            dve.tensor_tensor(ytmp[:, :, :], ps[:, 4, :].rearrange("p (b d) -> p b d", b=B), s_tok[:, :, :], ALU.add)\
               .then_inc(sem("s_sum_ready"), 1)
            dve.wait_ge(sem("s_tanh_ready"), 1)
            link(dve.tensor_tensor(x[:, :, :], x[:, :, :], xn2[:, :, :], ALU.add))

            norm(x, xn, "m1").then_inc(sem("norm_ready"), 1)
            dve.wait_ge(sem("w_m1"), loads["w_m1"])
            dve.wait_ge(sem("m_logit_psum"), 1)
            logits = ps[:, 0, 0:B * E].rearrange("p (b e) -> p b e", b=B)
            link(dve.tensor_copy(m_logit[:, :, :], logits))
            dve.tensor_reduce(m_top[:, :], m_logit[:, :, :], AX.X, ALU.max).then_inc(sem("m_top_ready"), 1)
            dve.wait_ge(sem("m_top_ready"), 1)
            link(dve.tensor_tensor(m_eq[:, :, :], m_logit[:, :, :], wide(m_top[:, :], E), ALU.is_equal))
            link(dve.tensor_tensor(m_rank[:, :, :], m_eq[:, :, :], erank[:, :, :], ALU.mult))
            link(dve.tensor_reduce(m_first[:, :], m_rank[:, :, :], AX.X, ALU.max))
            dve.tensor_tensor(m_hot[:, :, :], m_rank[:, :, :], wide(m_first[:, :], E), ALU.is_equal)\
               .then_inc(sem("m_hot_ready"), 1)
            dve.wait_ge(sem("m_tanh_ready"), 1)
            link(dve.tensor_scalar(m_score[:, :], m_tanh[:, :], 0.5, 0.5, ALU.mult, ALU.add))
            dve.tensor_tensor(m_xs[:, :, :], xn[:, :, :], wide(m_score[:, :], D), ALU.mult)\
               .then_inc(sem("m_xs_ready"), 1)
            dve.wait_ge(sem("m_xsT_ready"), 1)

            def expert_rows(e):
                dve.wait_ge(sem("m_mask_psum"), e + 1)
                if e >= 2:
                    dve.wait_ge(sem("m_gu_psum"), 2 * (e - 1))
                dve.tensor_tensor(m_xe[e % 2][:, :, :], m_xsT[:, :, :], ps[:, 1, :].rearrange("p (b q) -> p b q", b=B),
                                  ALU.mult).then_inc(sem("m_xe_ready"), 1)

            expert_rows(0)
            for k in range(MU):
                if k % 2 == 0 and k // 2 + 1 < E:
                    expert_rows(k // 2 + 1)
                dve.wait_ge(sem("m_silu_ready"), k + 1)
                if k >= 3:
                    dve.wait_ge(sem("m_down_psum"), k - 2)
                dve.tensor_tensor(flat(m_act[k % 3][:, :, :]), m_silu[k % 3], ps[:, 3 + 2 * (k % 3), :], ALU.mult)\
                   .then_inc(sem("m_act_ready"), 1)
            dve.wait_ge(sem("m_down_psum"), MU)
            dve.tensor_tensor(xn2[:, :, :], x[:, :, :], ps[:, 0, :].rearrange("p (b d) -> p b d", b=B), ALU.add)\
               .then_inc(sem("out_ready"), 1)

        def pool_middle0(pool, rstd_of, alone):
            rstd_of("a0")
            pool.wait_ge(sem("norm_ready"), nth("norm_ready", "a0"))
            rstd_of("a1")
            alone(pool.tensor_tensor(xres[:, :, :], x[:, :, :], xn[:, :, :], ALU.add), "a_res_ready", 1)
            pool.wait_ge(sem("w_a0"), loads["w_a0"])
            alone(pool.tensor_tensor(xres[:, :, :], xres[:, :, :],
                                     spread(bout0[:, :].rearrange("p (a n) -> p a n", a=1), 1, B), ALU.add),
                  "a_res_ready", 2)
            alone(pool.memset(a_v[:, :, :, HD], 1.0), "a_v_ready", 1)
            for b in range(B):
                pool.wait_ge(sem("a_qkv_ready"), b + 1)
                alone(pool.tensor_copy(a_v[:, b, :, 0:HD],
                                       a_qkv[:, b, 2 * D:3 * D].rearrange("p (h d) -> p h d", d=HD)),
                      "a_v_ready", b + 2)
            pool.wait_ge(sem("w_rot"), loads["w_rot"])
            for l in range(2):
                alone(pool.tensor_tensor(rotl[:, l, :, :], rot[:, :, :], rot_scale[:, l, :, :], ALU.mult),
                      "rotl_ready", l + 1)
            rstd_of("f0")
            pool.wait_ge(sem("w_f0"), loads["w_f0"])
            for l in range(2):
                n = l * B
                for b in range(B):
                    pool.wait_ge(sem("f_rot_ready"), n + b + 1)
                    alone(pool.tensor_tensor(f_qk[b], f_cos[b % 2], f_sin[b % 2], ALU.add),
                          "f_rotsum_ready", n + b + 1)
                pool.wait_ge(sem("f_y_ready"), 2 * l + 2)
                alone(pool.tensor_copy(f_shift[:, :, 0:64], y[:, :, 0:64]), "f_unshifted_ready", l + 1)
                rstd_of(f"g{l}")
                alone(pool.tensor_tensor(ytmp[:, :, :], y[:, :, :], spread(b2f[:, l:l + 1, :], 1, B), ALU.add),
                      "f_biased_ready", l + 1)

        def pool_middle1(pool, rstd_of):
            rstd_of("s1")
            rstd_of("m1")

        FREED_BY = {"T": "ctxT_ready", "K": "k_rest_ready", "V": "v_ready", "M": "max_taken"}

        @block.sync
        def _(sp):
            def load(dst, src, name):
                sp.dma_start(dst, src).then_inc(sem(name), 16)
                loads[name] = loads.get(name, 0) + 16

            def col(ap):
                return ap.rearrange("(p a) -> p a", a=1)

            def rows(ap):
                return spread(ap.rearrange("(a n) -> a n", a=1), 0, P)

            def load_context(b):
                src = a["ctx"][bass.ds(b, 1), :, :].rearrange("o (t p) d -> p (o t) d", p=P)
                for half in (slice(0, P // 2), slice(P // 2, P)):
                    sp.dma_start(ctx_in[half, :, :], src[half]).then_inc(sem("ctx_in_ready"), 16)

            def stack_queries(l):
                for i in range(3):
                    sp.wait_ge(sem(f"q_part{i}_ready"), l + 1)
                    if l and i == 0:
                        sp.wait_ge(sem("qstack_ready"), 192)
                    sp.dma_start(q_dram[i], q_part[i][:, :]).then_inc(sem("q_stored"), 16)
                sp.wait_ge(sem("q_stored"), 48 * (l + 1))
                sp.wait_ge(sem("qstack_cleared"), 1)
                for par in range(2):
                    for r in range(6):
                        lo = par * STACK + r * HD
                        src = q_dram[PART_Q[r]].rearrange("(j e d) n -> e d j n", e=2, d=HD)[par]
                        sp.dma_start(qstack[lo:lo + HD, :, par, :, :].rearrange("d j b q -> d j (b q)"), src)\
                          .then_inc(sem("qstack_ready"), 16)

            def stack_keys(n, parity, first=False):
                if not first:
                    sp.wait_ge(sem("kstack_ready"), n * 192)
                sp.wait_ge(sem("k_part0_ready"), n * 2 + 2)
                sp.dma_start(k_dram[0], k_part[0][:, :]).then_inc(sem("k_stored"), 16)
                for i in (1, 2):
                    sp.wait_ge(sem(f"k_part{i}_ready"), n * 4 + 4 if i == 1 else n + 1)
                    sp.dma_start(k_dram[i], k_part[i][:, :]).then_inc(sem("k_stored"), 16)
                sp.wait_ge(sem("k_stored"), n * 48 + 48)
                for par in range(2):
                    for r in range(6):
                        lo = par * STACK + r * HD
                        src = k_dram[PART_K[r]].rearrange("(j e d) n -> e d j n", e=2, d=HD)[par]
                        dst = kstack[lo:lo + HD, bass.ds(parity, 1), :, :].rearrange("d o j n -> d (o j) n")
                        sp.dma_start(dst, src).then_inc(sem("kstack_ready"), 16)

            def stack_mask(b, parity):
                src = spread(m_dram[bass.ds(b, 1), :].rearrange("o (a n) -> o a n", a=1), 1, PAIRS)
                dst = kstack[MASK_ROW:MASK_ROW + 1, bass.ds(parity, 1), :, :].rearrange("d o j n -> d (o j) n")
                sp.dma_start(dst, src).then_inc(sem("mask_stacked"), 16)

            def rows_under(times):
                src = spread(row_init[MASK_ROW:KROWS_EXP, :].rearrange("d (a n) -> d a n", a=1), 1, 2 * PAIRS * CTX // BANK)
                dst = kstack[MASK_ROW:KROWS_EXP, :, :, :].rearrange("d o j (c n) -> d (o j c) n", n=BANK)
                sp.dma_start(dst, src)\
                  .then_inc(sem("rows_stacked"), 16)

            def weights_after():
                load(wqkv0[:, :], a["L0_attn_qkv_wT"], "w_a0")
                load(bqkv0[:, :], rows(a["L0_attn_qkv_b"]), "w_a0")
                load(wout0[:, :], a["L0_attn_out_wT"], "w_a0")
                load(bout0[:, :], rows(a["L0_attn_out_b"]), "w_a0")
                load(lnw0[:, :], col(a["L0_attn_ln_w"]), "w_a0")
                load(lnb0[:, :], col(a["L0_attn_ln_b"]), "w_a0")
                load(headmask[:, :], a["c_headmask"], "w_a0")
                load(rot[:, :, :], a["c_rot"], "w_rot")
                for l in range(2):
                    for i, n in enumerate(("q", "k")):
                        s = a[f"L0_ffn_{n}_scale"][l]
                        load(rot_scale[:, l, 2 * i, :], rows(s), "w_rot")
                        load(rot_scale[:, l, 2 * i + 1, 0:32], rows(s[32:64]), "w_rot")
                        load(rot_scale[:, l, 2 * i + 1, 32:64], rows(s[0:32]), "w_rot")
                load(band[:, :], a["c_band"], "w_rot")
                load(shift[:, :], a["c_shift"], "w_f0")
                for l in range(2):
                    load(wqkvf[:, l, :], a["L0_ffn_wqkv"][l], "w_f0")
                    load(wof[:, l, :, :], a["L0_ffn_wo"][l].rearrange("(t p) n -> p t n", p=P), "w_f0")
                    load(w1f[:, l, :], a["L0_ffn_w1"][l], "w_f0")
                    load(w2f[:, l, 0:2, :], a["L0_ffn_w2"][l, 0:2 * P, :].rearrange("(t p) n -> p t n", p=P), "w_f0")
                    load(w2f[0:HT[2], l, 2, :], a["L0_ffn_w2"][l, 2 * P:HID, :], "w_f0")
                    load(lgf[:, l:l + 1], col(a["L0_ffn_ln_g"][l]), "w_f0")
                    load(lbf[:, l:l + 1], col(a["L0_ffn_ln_b"][l]), "w_f0")
                    load(b2f[:, l, :], rows(a["L0_ffn_b2"][l]), "w_f0")
                    for ag in range(2):
                        for m in range(3):
                            lo = ag * HID + m * P
                            load(b1f[0:HT[m], l, ag, m:m + 1], col(a["L0_ffn_b1"][l, lo:lo + HT[m]]), "w_f0")
                load(wspin[:, :], a["L1_attn_W_spinT"], "w_a1")
                load(bspin_col[:, :], col(a["L1_attn_b_spin"]), "w_a1")
                load(bspin_row[:, :], rows(a["L1_attn_b_spin"]), "w_a1")
                load(wglob[:, :], a["L1_attn_W_globalT"], "w_a1")
                load(wj[:, :], a["L1_attn_W_JT"], "w_a1")
                load(beta[:, :], rows(a["L1_attn_beta"]), "w_a1")
                load(wgate[:, :], a["L1_ffn_gate_w"], "w_m1")
                load(erank[:, :, :], spread(a["c_erank"].rearrange("(a b) e -> a b e", a=1), 0, P), "w_m1")

            load(ident[:, :], a["c_ident"], "w_base")
            load_context(0)
            load(x[:, :, :], a["x"].rearrange("b s d -> s b d"), "x_loaded")
            for l in range(2):
                for n in ("q", "k", "v", "o"):
                    load(wx[l][n][:, :], a[f"L{l}_xattn_W{n}"], f"w_x{l}")
                load(bx[l]["q"][:, :], col(a[f"L{l}_xattn_bq"]), f"w_x{l}")
                load(bx[l]["k"][:, :], col(a[f"L{l}_xattn_bk"]), f"w_x{l}")
                load(bx[l]["v"][:, :], rows(a[f"L{l}_xattn_bv"]), f"w_x{l}")
                load(bx[l]["o"][:, :], rows(a[f"L{l}_xattn_bo"]), f"w_x{l}")
            load(mask_u8[:, :], a["mask"].rearrange("(p f) -> p f", p=P), "mask_loaded")
            sp.wait_ge(sem("row_init_ready"), 2)
            rows_under(0)

            for l in range(2):
                n0 = B * l
                if l:
                    sp.wait_ge(sem("q_part2_ready"), 2)
                    rows_under(1)
                    sp.wait_ge(sem("mask_stored"), 16)
                    sp.wait_ge(sem("rows_stacked"), 32)
                    stack_mask(0, 0)
                stack_queries(l)
                stack_keys(n0, 0, first=(l == 0))
                if l == 0:
                    weights_after()
                    sp.wait_ge(sem("mask_bias_ready"), 1)
                    sp.dma_start(m_dram.rearrange("b (p f) -> (b p) f", p=P // B), mask_bias[:, :])\
                      .then_inc(sem("mask_stored"), 16)
                with sp.Fori(0, B - 1) as b:
                    sp.wait_ge(sem("ctxT_psum"), b * 2 + (2 * n0 + 2))
                    load_context(b + 1)
                    nxt_parity = sp.snap((b + 1) % 2)
                    if l:
                        sp.wait_ge(sem("k_part0_ready"), b * 2 + (2 * n0 + 4))
                        stack_mask(b + 1, nxt_parity)
                    stack_keys(b + (n0 + 1), nxt_parity)
                if l == 0:
                    sp.wait_ge(sem("ctxT_psum"), 2 * B)
                    load_context(0)

            sp.wait_ge(sem("x_attended1"), 1)
            load(gate_up[:, 0, :, :], a["L1_ffn_rt_gate"].rearrange("e k n -> k e n"), "w_e")
            load(gate_up[:, 1, :, :], a["L1_ffn_rt_up"].rearrange("e k n -> k e n"), "w_e")
            load(down[:, :, :, :], a["L1_ffn_rt_down"].rearrange("e (t k) n -> k e t n", k=P), "w_e")
            load(sh_gate_up[:, 0, :], a["L1_ffn_sh_gate"], "w_e")
            load(sh_gate_up[:, 1, :], a["L1_ffn_sh_up"], "w_e")
            load(sh_down[:, :, :], a["L1_ffn_sh_down"].rearrange("(t k) n -> k t n", k=P), "w_e")

            sp.wait_ge(sem("out_ready"), 1)
            sp.dma_start(out.rearrange("b s d -> s b d"), xn2[:, :, :]).then_inc(sem("out_stored"), 16)
            sp.wait_ge(sem("out_stored"), 16)

        @block.tensor
        def _(pe):
            def transposes(src, bank, ready, count, name):
                pe.wait_ge(sem(ready), count)
                for b in range(B):
                    last = pe.transpose(ps[:, bank, b * P:(b + 1) * P], src[:, b, :], ident[:, :])
                last.then_inc(sem(name), 1)

            def free_pair(prev):
                kind, value = prev[-2]
                if kind is not None:
                    pe.wait_ge(sem(FREED_BY[kind]), value)
                return 2 * (len(prev) % 2)

            def transpose_context(n, prev):
                for u in range(2):
                    bank = free_pair(prev)
                    if u == 0:
                        pe.wait_ge(sem("ctx_in_ready"), n * 32 + 32)
                    for t in range(8):
                        last = pe.transpose(ps[:, bank + t // 4, (t % 4) * P:(t % 4 + 1) * P],
                                            ctx_in[:, 8 * u + t, :], ident[:, :])
                    last.then_inc(sem("ctxT_psum"), 1)
                    prev.append(("T", n * 2 + (u + 1)))

            def project_keys(l, n, prev):
                for u in range(2):
                    bank = free_pair(prev)
                    pe.wait_ge(sem("ctxT_ready"), n * 2 + (u + 1))
                    for c in range(2):
                        lo = (2 * u + c) * BANK
                        last = pe.matmul(ps[:, bank + c, :], wx[l]["k"][:, :], ctxT[:, lo:lo + BANK],
                                         start=True, stop=True)
                    last.then_inc(sem("k_psum"), 1)
                    prev.append(("K", n * 2 + (u + 1)))

            def project_values(l, n, prev):
                for u in range(2):
                    bank = free_pair(prev)
                    for t in range(8):
                        tile = 8 * u + t
                        last = pe.matmul(ps[:, bank + t // 4, (t % 4) * P:(t % 4 + 1) * P],
                                         ctxT[:, tile * P:(tile + 1) * P], wx[l]["v"][:, :], start=True, stop=True)
                    last.then_inc(sem("v_psum"), 1)
                    prev.append(("V", n * 2 + (u + 1)))

            def max_chunk(n, b, parity, j, c, prev):
                i, k = c // 4, c % 4
                if c % 2 == 0:
                    free_pair(prev)
                bank = 2 * (len(prev) % 2) + c % 2
                if j == 0 and c == 0:
                    pe.wait_ge(sem("kstack_ready"), n * 192 + 192)
                pair, half = 2 * j + i // 2, i % 2
                last = pe.matmul(ps[:, bank, :], qstack[0:KROWS_MAX, pair, half, b, :],
                                 kstack[0:KROWS_MAX, parity, pair, k * BANK:(k + 1) * BANK], start=True, stop=True)
                if c % 2:
                    last.then_inc(sem("max_psum"), 1)
                    prev.append(("M", n * 32 + (8 * j + c // 2 + 1)))

            def max_rows(n, j):
                pe.wait_ge(sem("neg_split_ready"), n * 4 + (j + 1))
                for i in range(4):
                    last = pe.matmul(ps[MASK_ROW:KROWS_EXP, XB, i * P:(i + 1) * P], neg_split[:, i, :], ident_bf[:, :],
                                     start=True, stop=True)
                last.then_inc(sem("max_rows_psum"), 1)

            def weigh(n, j, t):
                pe.wait_ge(sem("exp_ready"), n * 64 + (16 * j + t + 1))
                slot = (16 * j + t) % 4
                if t == 0 and j >= 1:
                    pe.wait_ge(sem("sums_ready"), n * 4 + j)
                for i in range(4):
                    last = pe.matmul(ps[32 * i:32 * i + VW, OB, 0:P], vones[:, t, 4 * j + i, :],
                                     probs[:, slot, i, :], start=(t == 0), stop=(t == TILES - 1))
                last.then_inc(sem("probs_used"), 1)

            def transpose_sums(n, j):
                pe.wait_ge(sem("sums_ready"), n * 4 + (j + 1))
                pe.transpose(ps[:, XB, 0:P], sums[:, :], ident[:, :]).then_inc(sem("sumsT_psum"), 1)

            def quad(l, n, b, parity, j, nxt, prev):
                pe.wait_ge(sem("max_rows_ready"), n * 4 + (j + 1))
                c = 0
                for t in range(TILES):
                    if t >= 2:
                        pe.wait_ge(sem("exp_ready"), n * 64 + (16 * j + t - 1))
                    for p in range(2):
                        pair = 2 * j + p
                        last = pe.matmul(ps[:, E0 + t % 2, p * 2 * P:(p + 1) * 2 * P],
                                         kstack[0:KROWS_EXP, parity, pair, t * P:(t + 1) * P],
                                         qstack[0:KROWS_EXP, pair, :, b, :], start=True, stop=True)
                    last.then_inc(sem("scores_psum"), 1)
                    if nxt is not None:
                        for _ in range(MAX_PLAN[t]):
                            max_chunk(*nxt, c, prev)
                            c += 1
                    if t == 1:
                        if j == 0:
                            pe.wait_ge(sem("v_ready"), n * 2 + 2)
                    if t >= 1:
                        weigh(n, j, t - 1)
                    if t == 3 and j >= 1:
                        transpose_sums(n, j - 1)
                if nxt is None:
                    pe.wait_ge(sem("attended"), n * 4 + j)
                else:
                    max_rows(nxt[0], nxt[3])
                weigh(n, j, TILES - 1)
                if j == QUADS - 1:
                    if nxt is not None:
                        pe.wait_ge(sem("max_rows_ready"), nxt[0] * 4 + 1)
                    transpose_sums(n, j)

            def project_out(l):
                transposes(attn_tok, XB, "attended", 16 * (l + 1), "attnT_psum")
                pe.wait_ge(sem("attnT_ready"), l + 1)
                for b in range(B):
                    last = pe.matmul(ps[:, OB, b * P:(b + 1) * P], xnT[:, b, :], wx[l]["o"][:, :], start=True, stop=True)
                last.then_inc(sem("xo_psum"), 1)

            def cross_attention(l):
                n0 = B * l
                transposes(xn, XB, "norm_ready", nth("norm_ready", f"xattn{l}"), "normT_psum")
                pe.wait_ge(sem("normT_ready"), nth("normT_ready", f"xattn{l}"))
                pe.matmul(ps[:, OB, :], wx[l]["q"][:, :], xnT[:, :, :].rearrange("p b q -> p (b q)"),
                          start=True, stop=True).then_inc(sem("q_psum"), 1)
                prev = [(None, None), (None, None)]
                transpose_context(n0, prev)
                project_keys(l, n0, prev)
                pe.wait_ge(sem("qstack_ready"), 192 * (l + 1))
                pe.wait_ge(sem("rows_stacked"), 16 * (l + 1))
                if l:
                    pe.wait_ge(sem("mask_stacked"), 16)
                for c in range(16):
                    max_chunk(n0, 0, 0, 0, c, prev)
                max_rows(n0, 0)

                def last_maxima(n):
                    return [("M", n * 32 + 7), ("M", n * 32 + 8)]

                with pe.Fori(0, B - 1) as b:
                    n = b + n0
                    parity, nxt_parity, nb = pe.snap(b % 2), pe.snap((b + 1) % 2), pe.snap(b + 1)
                    prev = last_maxima(n)
                    project_values(l, n, prev)
                    transpose_context(n + 1, prev)
                    project_keys(l, n + 1, prev)
                    for j in range(QUADS):
                        if j < QUADS - 1:
                            nxt = (n, b, parity, j + 1)
                        else:
                            if l:
                                pe.wait_ge(sem("mask_stacked"), b * 16 + 32)
                            nxt = (n + 1, nb, nxt_parity, 0)
                        quad(l, n, b, parity, j, nxt, prev)
                    assert len(prev) % 2 == 0
                n, b, parity = n0 + B - 1, B - 1, (B - 1) % 2
                prev = last_maxima(n)
                project_values(l, n, prev)
                for j in range(QUADS):
                    quad(l, n, b, parity, j, (n, b, parity, j + 1) if j < QUADS - 1 else None, prev)
                project_out(l)

            pe.wait_ge(sem("w_base"), loads["w_base"])
            pe.wait_ge(sem("w_x0"), loads["w_x0"])
            pe.wait_ge(sem("w_x1"), loads["w_x1"])
            pe.wait_ge(sem("consts_ready"), 1)
            cross_attention(0)
            pe_middle0(pe, transposes)
            cross_attention(1)
            pe_middle1(pe, transposes)

        @block.scalar
        def _(act):
            def copy(dst, src):
                return act.activation(dst, src, ACT.Copy)

            def context_rows(n, first=False):
                for u in range(2):
                    act.wait_ge(sem("ctxT_psum"), n * 2 + (u + 1))
                    if u == 0 and not first:
                        act.wait_ge(sem("v_psum"), n * 2)
                    copy(ctxT[:, u * 2 * BANK:(u + 1) * 2 * BANK],
                         ps[:, 2 * u:2 * u + 2, :].rearrange("p a c -> p (a c)")).then_inc(sem("ctxT_ready"), 1)

            def keys_high(l, n, first=False):
                for u in range(2):
                    act.wait_ge(sem("k_psum"), n * 2 + (u + 1))
                    if u == 0 and not first:
                        act.wait_ge(sem("k_stored"), n * 48)
                    act.activation(k_part[0][:, u * 2 * BANK:(u + 1) * 2 * BANK],
                                   ps[:, 2 * u:2 * u + 2, :].rearrange("p a c -> p (a c)"),
                                   ACT.Identity, bias=bx[l]["k"][:, :]).then_inc(sem("k_part0_ready"), 1)

            def keys_mid(n, c):
                act.wait_ge(sem("k_rest_ready"), n * 2 + (c // 2 + 1))
                cols = slice(c * BANK, (c + 1) * BANK)
                copy(k_part[1][:, cols], k_rest[:, cols]).then_inc(sem("k_part1_ready"), 1)

            def take_max_rows(n, b, j):
                act.wait_ge(sem("max_rows_psum"), n * 4 + (j + 1))
                for p in range(2):
                    last = copy(qstack[MASK_ROW:KROWS_EXP, 2 * j + p, :, b, :],
                                ps[MASK_ROW:KROWS_EXP, XB, p * 2 * P:(p + 1) * 2 * P]
                                .rearrange("r (h q) -> r h q", h=2))
                last.then_inc(sem("max_rows_ready"), 1)

            def quad(l, n, b, j, nxt, nxt_batch=None):
                for t in range(TILES):
                    act.wait_ge(sem("scores_psum"), n * 64 + (16 * j + t + 1))
                    if t >= 4:
                        act.wait_ge(sem("probs_used"), n * 64 + (16 * j + t - 3))
                    act.activation(probs[:, (16 * j + t) % 4, :, :], ps[:, E0 + t % 2, :]
                                   .rearrange("p (i q) -> p i q", i=4), ACT.Exp, scale=HD ** -0.5)\
                       .then_inc(sem("exp_ready"), 1)
                    if j == 0 and nxt_batch is not None and t in (3, 5, 7, 9):
                        keys_mid(nxt_batch, (t - 3) // 2)
                if nxt is not None:
                    take_max_rows(*nxt)
                act.wait_ge(sem("probs_used"), n * 64 + 16 * (j + 1))
                copy(sums[:, :], ps[:, OB, 0:P]).then_inc(sem("sums_ready"), 1)

            def norm_rows(tag):
                act.wait_ge(sem("normT_psum"), nth("normT_psum", tag))
                copy(xnT[:, :, :], ps[:, XB, :].rearrange("p (b q) -> p b q", b=B)).then_inc(sem("normT_ready"), 1)

            def cross_attention(l):
                n0 = B * l
                norm_rows(f"xattn{l}")
                context_rows(n0, first=(l == 0))
                keys_high(l, n0, first=(l == 0))
                for c in range(CHUNKS):
                    keys_mid(n0, c)
                take_max_rows(n0, 0, 0)
                with act.Fori(0, B - 1) as b:
                    n, nb = b + n0, act.snap(b + 1)
                    context_rows(n + 1)
                    keys_high(l, n + 1)
                    for j in range(QUADS):
                        quad(l, n, b, j, (n, b, j + 1) if j < QUADS - 1 else (n + 1, nb, 0), n + 1)
                n, b = n0 + B - 1, B - 1
                for j in range(QUADS):
                    quad(l, n, b, j, (n, b, j + 1) if j < QUADS - 1 else None)
                act.wait_ge(sem("attnT_psum"), l + 1)
                copy(xnT[:, :, :], ps[:, XB, :].rearrange("p (b q) -> p b q", b=B)).then_inc(sem("attnT_ready"), 1)

            act.wait_ge(sem("w_x0"), loads["w_x0"])
            act.wait_ge(sem("w_x1"), loads["w_x1"])
            act.wait_ge(sem("psum_cleared"), 1)
            cross_attention(0)
            act_middle0(act, copy)
            cross_attention(1)
            act_middle1(act, copy)

        @block.vector
        def _(dve):
            chain = [0]

            def link(ins):
                chain[0] += 1
                ins.then_inc(sem("dve_chain"), 1)
                dve.wait_ge(sem("dve_chain"), chain[0])

            def norm(src, dst, tag, link=link):
                for b in range(B):
                    last = dve.bn_stats(stats[:, b, :], src[:, b, :])
                link(last)
                for b in range(B):
                    last = dve.bn_aggr(meanvar[:, b, :], stats[:, b, :])
                link(last)
                dve.tensor_scalar(veps[:, :], meanvar[:, :, 1], 1e-5, None, ALU.add)\
                   .then_inc(sem("norm_var"), 1)
                dve.wait_ge(sem("norm_rstd"), nth("norm_rstd", tag))
                for b in range(B):
                    last = dve.tensor_scalar(dst[:, b, :], src[:, b, :], meanvar[:, b, 0:1], rstd[:, b:b + 1],
                                             ALU.subtract, ALU.mult)
                return last

            def values(l, n):
                for u in range(2):
                    dve.wait_ge(sem("v_psum"), n * 2 + (u + 1))
                    for c in range(2):
                        bias = spread(bx[l]["v"][:, :].rearrange("p (a n) -> p a n", a=1), 1, 4)
                        last = dve.tensor_tensor(
                            vones[:, 8 * u + 4 * c:8 * u + 4 * c + 4, :, 0:HD],
                            ps[:, 2 * u + c, :].rearrange("p (t h d) -> p t h d", t=4, h=H),
                            bias.rearrange("p t (h d) -> p t h d", h=H), ALU.add)
                    last.then_inc(sem("v_ready"), 1)

            def keys_rest(l, n, first=False):
                for u in range(2):
                    dve.wait_ge(sem("k_part0_ready"), n * 2 + (u + 1))
                    if u == 0 and not first:
                        dve.wait_ge(sem("k_part2_ready"), n)
                    cols = slice(u * 2 * BANK, (u + 1) * 2 * BANK)
                    dve.scalar_tensor_tensor(k_rest[:, cols], ps[:, 2 * u:2 * u + 2, :].rearrange("p a c -> p (a c)"),
                                             bx[l]["k"][:, :], k_part[0][:, cols], ALU.add, ALU.subtract)\
                       .then_inc(sem("k_rest_ready"), 1)

            def take_max(n, j, m):
                dve.wait_ge(sem("max_psum"), n * 32 + (8 * j + m + 1))
                bank = 2 * (m % 2)
                dve.reduce_max(max_part[:, m // 2, m % 2:m % 2 + 1],
                               ps[:, bank:bank + 2, :].rearrange("p a c -> p (a c)"), axis=AX.X)\
                   .then_inc(sem("max_taken"), 1)

            def split_max(n, j, link, first=False):
                dve.wait_ge(sem("max_taken"), n * 32 + 8 * (j + 1))
                link(dve.tensor_reduce(neg_max[:, :], max_part[:, :, :], AX.X, ALU.max, negate=True))
                if not (first and j == 0):
                    dve.wait_ge(sem("max_rows_psum"), n * 4 + j)
                link(dve.tensor_copy(neg_split[:, :, 1], neg_max[:, :]))
                link(dve.tensor_tensor(neg_rest[:, :], neg_max[:, :], neg_split[:, :, 1], ALU.subtract))
                link(dve.tensor_copy(neg_split[:, :, 2], neg_rest[:, :]))
                dve.tensor_tensor(neg_split[:, :, 3], neg_rest[:, :], neg_split[:, :, 2], ALU.subtract)\
                   .then_inc(sem("neg_split_ready"), 1)

            def attend(n, b, j, link):
                dve.wait_ge(sem("sumsT_psum"), n * 4 + (j + 1))
                sumsT = ps[:, XB, 0:P].rearrange("p (i w) -> p i w", i=4)
                link(dve.reciprocal(rden[:, :], sumsT[:, :, HD]))
                dst = attn_tok[:, b, 4 * HD * j:4 * HD * (j + 1)].rearrange("p (i d) -> p i d", i=4)
                weight = spread(rden[:, :].rearrange("p (i a) -> p i a", a=1), 2, HD)
                dve.tensor_tensor(dst, sumsT[:, :, 0:HD], weight, ALU.mult).then_inc(sem("attended"), 1)

            LINKS = {True: QUADS * 4 + QUADS, False: (QUADS - 1) * 4 + QUADS}

            def batch(l, n, b, n_next, link):
                for j in range(QUADS):
                    nxt = (n, j + 1) if j < QUADS - 1 else (n_next, 0) if n_next is not None else None
                    for m in range(8):
                        if nxt is not None:
                            take_max(*nxt, m)
                        if m == 3 and j >= 1:
                            attend(n, b, j - 1, link)
                    if nxt is not None:
                        split_max(*nxt, link)
                attend(n, b, QUADS - 1, link)

            def cross_attention(l):
                n0 = B * l
                norm(x, xn, f"xattn{l}").then_inc(sem("norm_ready"), 1)
                dve.wait_ge(sem("q_psum"), l + 1)
                link(dve.tensor_scalar(q_rest[0], ps[:, OB, :], bx[l]["q"][:, :], None, ALU.add))
                if l:
                    dve.wait_ge(sem("q_stored"), 48)
                dve.tensor_copy(q_part[0][:, :], q_rest[0]).then_inc(sem("q_part0_ready"), 1)
                dve.wait_ge(sem("q_part0_ready"), l + 1)
                link(dve.tensor_tensor(q_rest[1], q_rest[0], q_part[0][:, :], ALU.subtract))
                dve.tensor_copy(q_part[1][:, :], q_rest[1]).then_inc(sem("q_part1_ready"), 1)
                dve.wait_ge(sem("q_part1_ready"), l + 1)
                dve.tensor_tensor(q_part[2][:, :], q_rest[1], q_part[1][:, :], ALU.subtract)\
                   .then_inc(sem("q_part2_ready"), 1)
                keys_rest(l, n0, first=(l == 0))
                for m in range(8):
                    take_max(n0, 0, m)
                split_max(n0, 0, link, first=(l == 0))
                start = chain[0]
                with dve.Fori(0, B - 1) as b:
                    within = [0]

                    def link_b(ins):
                        within[0] += 1
                        ins.then_inc(sem("dve_chain"), 1)
                        dve.wait_ge(sem("dve_chain"), b * LINKS[True] + (start + within[0]))

                    values(l, b + n0)
                    keys_rest(l, b + (n0 + 1))
                    batch(l, b + n0, b, b + (n0 + 1), link_b)
                    assert within[0] == LINKS[True], within
                chain[0] += (B - 1) * LINKS[True]
                values(l, n0 + B - 1)
                batch(l, n0 + B - 1, B - 1, None, link)
                dve.wait_ge(sem("xo_psum"), l + 1)
                bias = spread(bx[l]["o"][:, :].rearrange("p (a n) -> p a n", a=1), 1, B)
                link(dve.tensor_tensor(ytmp[:, :, :], ps[:, OB, :].rearrange("p (b d) -> p b d", b=B), bias, ALU.add))
                dve.tensor_tensor(x[:, :, :], x[:, :, :], ytmp[:, :, :], ALU.add).then_inc(sem(f"x_attended{l}"), 1)
                dve.wait_ge(sem(f"x_attended{l}"), 1)

            dve.memset(ps[:, OB, :], 0.0).then_inc(sem("psum_cleared"), 1)
            link(dve.memset(qstack[:, :, :, :, :].rearrange("p j e b q -> p (j e b q)").bitcast(mybir.dt.uint32), 0))
            ones_bf = qstack[MASK_ROW:MASK_ROW + 1, :, :, :, :].rearrange("p j e b q -> p (j e b q)")
            dve.memset(ones_bf.bitcast(mybir.dt.uint32), 0x3F803F80).then_inc(sem("qstack_cleared"), 1)
            dve.memset(neg_split[:, :, 0], 1.0)
            dve.memset(vones[:, :, :, HD], 1.0)
            dve.memset(hT[:, :, :], 0.0)
            dve.wait_ge(sem("w_base"), loads["w_base"])
            link(dve.tensor_copy(ident_bf[:, :], ident[:, :]))
            dve.memset(ones4[:, :], 1.0).then_inc(sem("consts_ready"), 1)
            dve.wait_ge(sem("mask_loaded"), loads["mask_loaded"])
            dve.tensor_scalar(mask_bias[:, :], mask_u8[:, :], 1.0, -MASKED, ALU.subtract, ALU.mult)\
               .then_inc(sem("mask_bias_ready"), 1)
            dve.wait_ge(sem("x_loaded"), 16)
            dve.wait_ge(sem("w_x0"), loads["w_x0"])
            dve.wait_ge(sem("w_x1"), loads["w_x1"])
            cross_attention(0)
            dve_middle0(dve, link, norm)
            cross_attention(1)
            dve_middle1(dve, link, norm)

        @block.gpsimd
        def _(pool):
            def alone(ins, name, count):
                ins.then_inc(sem(name), 1)
                pool.wait_ge(sem(name), count)

            def rstd_of(tag):
                pool.wait_ge(sem("norm_var"), nth("norm_var", tag))
                alone(pool.tensor_tensor(rstd[:, :], veps[:, :], half_neg[:, :], ALU.pow),
                      "norm_rstd", nth("norm_rstd", tag))

            def split_keys(n, first=False):
                if not first:
                    pool.wait_ge(sem("k_stored"), n * 48)
                pool.wait_ge(sem("k_part1_ready"), n * 4 + 4)
                alone(pool.tensor_tensor(k_part[2][:, :], k_rest[:, :], k_part[1][:, :], ALU.subtract),
                      "k_part2_ready", n + 1)

            def cross_attention(l):
                rstd_of(f"xattn{l}")
                split_keys(B * l, first=(l == 0))
                with pool.Fori(0, B - 1) as b:
                    split_keys(b + (B * l + 1))

            alone(pool.memset(row_init[MASK_ROW:KROWS_EXP, :], 1.0), "row_init_ready", 1)
            alone(pool.memset(row_init[MASK_ROW:MASK_ROW + 1, :], 0.0), "row_init_ready", 2)
            alone(pool.memset(half_neg[:, :], -0.5), "half_ready", 1)
            cross_attention(0)
            pool_middle0(pool, rstd_of, alone)
            cross_attention(1)
            pool_middle1(pool, rstd_of)

        return nc


_TRANSPOSED = ("L0_attn_qkv_w", "L0_attn_out_w", "L1_attn_W_spin", "L1_attn_W_global", "L1_attn_W_J")


def _constants(np):
    tok = np.arange(P)
    half = np.arange(0, FD, 2, dtype=np.float32)
    inv_freq = np.float32(1.0) / np.float32(10000.0) ** (half / np.float32(FD))
    freqs = tok.astype(np.float32)[:, None] * inv_freq[None, :]
    base = (half + np.float32(0.4 * FD)) / np.float32(1.4 * FD)
    power = (tok - P // 2).astype(np.float32) / np.float32(32.0)
    scale = (base[None, :] ** power[:, None]).astype(np.float32)
    cos, sin = np.cos(freqs), np.sin(freqs)
    both = lambda u, v: np.concatenate([u, v], axis=1)
    rot = np.stack([both(cos * scale, cos * scale), both(-sin * scale, sin * scale),
                    both(cos / scale, cos / scale), both(-sin / scale, sin / scale)], axis=1)
    q, k = tok[:, None], tok[None, :]
    return {
        "c_ident": np.eye(P, dtype=np.float32),
        "c_band": np.where((q < k) | (q > k + 64), MASKED, 0.0).astype(np.float32),
        "c_shift": (q + 1 == k).astype(np.float32),
        "c_headmask": (tok[:, None] // HD == np.arange(H)[None, :]).astype(np.float32),
        "c_rot": rot.astype(np.float32),
        "c_erank": np.tile(np.arange(E, 0, -1, dtype=np.float32), (B, 1)),
    }


def kernel(**inputs):
    import numpy as np
    import concourse.bacc as bacc
    from concourse.bass_utils import run_bass_kernel_spmd

    nc = bacc.Bacc("TRN2", target_bir_lowering=False, num_devices=1)
    host = {}
    for name, value in inputs.items():
        v = np.asarray(value)
        if name == "ctx_1024":
            name = "ctx"
        if name == "mask_BxS2_bk1":
            name, v = "mask", v.reshape(-1)
        if name in _TRANSPOSED:
            name, v = name + "T", v.T
        host[name] = np.ascontiguousarray(v)
    host.update(_constants(np))
    arrays, aps = {}, {}
    for name, v in host.items():
        arrays[f"in_{name}"] = v
        aps[name] = nc.dram_tensor(f"in_{name}", v.shape, mybir.dt.from_np(v.dtype), kind="ExternalInput").ap()
    out = nc.dram_tensor("out_0", (B, P, D), F32, kind="ExternalOutput").ap()
    perceiver(nc, aps, out)
    result = run_bass_kernel_spmd(nc, [arrays], core_ids=[0])
    return result.results[0]["out_0"]
```

```python
import concourse.bass as bass
from concourse import mybir
from contextlib import ExitStack

F32 = mybir.dt.float32
BF16 = mybir.dt.bfloat16
U8 = mybir.dt.uint8
ALU = mybir.AluOpType
ACT = mybir.ActivationFunctionType
AX = mybir.AxisListType

P = 128
B = 4
D = 128
H = 16
HD = D // H
CTX = 2048
TILES = CTX // P
PAIRS = H // 2
QUADS = H // 4
BANK = 512
CHUNKS = CTX // BANK
VW = HD + 1
STACK = 6 * HD
PART_K = (0, 0, 0, 1, 1, 2)
PART_Q = (0, 1, 2, 0, 1, 0)
MASK_ROW = 2 * STACK
KROWS_MAX = MASK_ROW + 1
KROWS_EXP = MASK_ROW + 4
MASKED = -1.0e25
SLOTS = QUADS * TILES
AHEAD = 24
MAX_PLAN = [0, 0, 0] + [2 if t in (4, 8, 12) else 1 for t in range(3, SLOTS)]
KEYS_MID_AT = (2, 4, 5, 7)
MAX_ROWS_AT = 12

FH = 8
FD = 64
INNER = FH * FD
HID = 341
HT = (128, 128, 85)
E = 8
EI = 256


def spread(ap, axis, n):
    shape = list(ap.shape)
    assert shape[axis] == 1
    shape[axis] = n
    return ap.broadcast_to(shape)


def perceiver(nc, a, out):
    ctx = ExitStack()
    with ctx:
        def sb(name, shape, dt=F32):
            return ctx.enter_context(nc.sbuf_tensor(name, shape, dt))

        sems, loads = {}, {}

        def sem(name):
            if name not in sems:
                sems[name] = ctx.enter_context(nc.semaphore(name))
            return sems[name]

        NORMS = ("xattn0", "a0", "a1", "f0", "g0", "g1", "xattn1", "s1", "m1")
        APART = {"norm_ready": ("f0",), "normT_psum": ("a0", "f0"), "normT_ready": ("a0", "f0")}

        def nth(signal, tag):
            return [t for t in NORMS if t not in APART.get(signal, ())].index(tag) + 1

        x = sb("x", [P, B, D])
        ident = sb("ident", [P, P])
        ident_bf = sb("ident_bf", [P, P], BF16)
        ctx_in = sb("ctx_in", [P, TILES, D])
        ctxT = sb("ctxT", [P, CTX])
        k_part = [sb(f"k_part{i}", [P, CTX], BF16) for i in range(3)]
        k_rest = sb("k_rest", [P, CTX])
        kstack = sb("kstack", [P, 2, PAIRS, CTX], BF16)
        vones = sb("vones", [P, TILES, H, VW])
        qstack = sb("qstack", [P, PAIRS, 2, B, P], BF16)
        q_part = [sb(f"q_part{i}", [P, B * P], BF16) for i in range(3)]
        row_init = sb("row_init", [P, BANK], BF16)
        probs = sb("probs", [P, 4, 4, P])
        sums = sb("sums", [P, P])
        attn_tok = sb("attn_tok", [P, B, D])
        max_part = sb("max_part", [P, 4, 2])
        neg_max = sb("neg_max", [P, 4])
        neg_rest = sb("neg_rest", [P, 4])
        neg_split = sb("neg_split", [P, 4, 4], BF16)
        rden = sb("rden", [P, 4])
        wx = [{n: sb(f"wx{l}_{n}", [P, D]) for n in ("q", "k", "v", "o")} for l in range(2)]
        bx = [{"q": sb(f"bx{l}_q", [P, 1]), "k": sb(f"bx{l}_k", [P, 1]),
               "v": sb(f"bx{l}_v", [P, D]), "o": sb(f"bx{l}_o", [P, D])} for l in range(2)]
        wqkv0 = sb("wqkv0", [P, 3 * D])
        bqkv0 = sb("bqkv0", [P, 3 * D])
        wout0 = sb("wout0", [P, D])
        bout0 = sb("bout0", [P, D])
        lnw0 = sb("lnw0", [P, 1])
        lnb0 = sb("lnb0", [P, 1])
        headmask = sb("headmask", [P, H])
        wqkvf = sb("wqkvf", [P, 2, 3 * INNER])
        wof = sb("wof", [P, 2, 4, D])
        w1f = sb("w1f", [P, 2, 2 * HID])
        w2f = sb("w2f", [P, 2, 3, D])
        lgf = sb("lgf", [P, 2])
        lbf = sb("lbf", [P, 2])
        b1f = sb("b1f", [P, 2, 2, 3])
        b2f = sb("b2f", [P, 2, D])
        rot = sb("rot", [P, 4, FD])
        rot_scale = sb("rot_scale", [P, 2, 4, FD])
        rotl = sb("rotl", [P, 2, 4, FD])
        band = sb("band", [P, P])
        band_bf = sb("band_bf", [P, P], BF16)
        shift = sb("shift", [P, P])
        wspin = sb("wspin", [P, D])
        bspin_col = sb("bspin_col", [P, 1])
        bspin_row = sb("bspin_row", [P, D])
        wglob = sb("wglob", [P, D])
        wj = sb("wj", [P, D])
        beta = sb("beta", [P, 1])
        wgate = sb("wgate", [P, E])
        erank = sb("erank", [P, B, E])
        mask_u8 = sb("mask_u8", [P, B * CTX // P], U8)
        mask_bias = sb("mask_bias", [P, B * CTX // P], BF16)
        hT = sb("hT", [P, B, P])
        half_neg = sb("half_neg", [P, B])
        stats = sb("stats", [P, B, 6])
        meanvar = sb("meanvar", [P, B, 2])
        veps = sb("veps", [P, B])
        rstd = sb("rstd", [P, B])
        xn = sb("xn", [P, B, D])
        xn2 = sb("xn2", [P, B, D])
        xnT = sb("xnT", [P, B, P])
        xres = sb("xres", [P, B, D])
        ytmp = sb("ytmp", [P, B, D])
        y = sb("y", [P, B, D])

        q_rest = [t[:, :, :].rearrange("p b d -> p (b d)") for t in (ytmp, xres)]

        scratch = kstack[:, :, :, :].rearrange("p a b c -> p (a b c)").bitcast(F32)
        HALF = PAIRS * CTX // 2
        scratch_at = [HALF]

        def carve(*shape):
            n = 1
            for s in shape:
                n *= s
            lo = scratch_at[0]
            scratch_at[0] += n
            assert scratch_at[0] <= PAIRS * CTX
            v = scratch[:, lo:lo + n]
            if len(shape) == 2:
                v = v.rearrange("p (a b) -> p a b", a=shape[0])
            return v

        ps = ctx.enter_context(nc.psum_tensor("ps", [P, 8, BANK], F32))
        E0, OB, XB = 4, 6, 7

        k_dram = nc.dram_tensor("k_dram", (3, P, CTX), BF16, kind="Internal").ap()
        m_dram = nc.dram_tensor("m_dram", (B, CTX), BF16, kind="Internal").ap()
        q_dram = nc.dram_tensor("q_dram", (3, P, B * P), BF16, kind="Internal").ap()

        block = ctx.enter_context(nc.Block())

        def flat(ap):
            return ap.rearrange("p b q -> p (b q)")

        a_qkv = carve(B, 3 * D)
        a_sq = carve(B, 2 * D)
        a_ss = sb("a_ss", [P, B, 2 * H])
        a_norm = sb("a_norm", [P, B, 2 * H])
        a_inv = sb("a_inv", [P, B, 2 * H])
        a_qk = carve(B, 2 * D)
        a_kT = carve(B, P)
        a_qblk = [carve(H, P) for _ in range(2)]
        idle = probs[:, :, :, :].rearrange("p a b c -> p (a b c)")
        a_probs = [idle[:, i * 8 * P:(i + 1) * 8 * P].rearrange("p (a b) -> p a b", a=8) for i in range(2)]
        a_v = k_rest[:, 0:B * H * VW].rearrange("p (b h w) -> p b h w", b=B, h=H)
        a_sums = k_rest[:, B * H * VW:B * H * VW + 4 * P].rearrange("p (a b) -> p a b", a=4)
        a_rden = sb("a_rden", [P, H])
        scratch_at[0] = HALF
        f_sq = [idle[:, i * 2 * INNER:(i + 1) * 2 * INNER] for i in range(2)]
        f_cos = [carve(2 * INNER) for _ in range(2)]
        f_sin = [carve(2 * INNER) for _ in range(2)]
        f_qk = [carve(2 * INNER) for _ in range(B)]
        f_v = [k_rest[:, i * INNER:(i + 1) * INNER] for i in range(B)]
        f_qT, f_kT, f_oT = [ctx_in[:, 4 * i:4 * i + 4, :] for i in range(3)]
        f_probs = f_sq[0].rearrange("p (h k) -> p h k", h=FH)
        f_probsT = f_cos[0].rearrange("p (h k) -> p h k", h=FH)
        f_gelu = [f_sin[0][:, 0:512], f_sin[0][:, 512:1024], f_sin[1][:, 0:512]]
        f_act = f_qk[0].rearrange("p (a n) -> p a n", a=2), f_qk[1].rearrange("p (a n) -> p a n", a=2)
        f_act = [f_act[0][:, 0, :], f_act[0][:, 1, :], f_act[1][:, 0, :]]
        f_shift = f_cos[1][:, 0:512].rearrange("p (b d) -> p b d", b=B)
        f_ss = sb("f_ss", [P, B, 16])
        f_norm = sb("f_norm", [P, B, 16])
        f_inv = sb("f_inv", [P, B, 16])
        f_qs = sb("f_qs", [P, B, FH])
        f_max = sb("f_max", [P, FH])
        f_bias = sb("f_bias", [P, FH])
        f_den = sb("f_den", [P, FH])
        f_rden = sb("f_rden", [P, FH])
        gate_up = scratch[:, 0:4096].rearrange("p (a e n) -> p a e n", a=2, e=E)
        down = scratch[:, 4096:6144].rearrange("p (e t n) -> p e t n", e=E, t=2)
        sh_gate_up = scratch[:, 6144:6656].rearrange("p (a n) -> p a n", a=2)
        sh_down = scratch[:, 6656:6912].rearrange("p (a n) -> p a n", a=2)
        scratch_at[0] = HALF
        s_T = carve(B, P)
        s_tok = carve(B, D)
        s_eT = carve(B, P)
        s_probs = carve(B, P)
        s_probsT = carve(B, P)
        s_meanrows = carve(B, P)
        m_xs = carve(B, D)
        m_xsT = carve(B, P)
        m_xe = [carve(B, P) for _ in range(2)]
        m_silu = [carve(B * P) for _ in range(3)]
        m_act = [carve(B, P) for _ in range(3)]
        s_mean = sb("s_mean", [P, B])
        s_max = sb("s_max", [P, B])
        s_bias = sb("s_bias", [P, B])
        s_den = sb("s_den", [P, B])
        s_rden = sb("s_rden", [P, B])
        m_logit = sb("m_logit", [P, B, E])
        m_top = sb("m_top", [P, B])
        m_tanh = sb("m_tanh", [P, B])
        m_score = sb("m_score", [P, B])
        m_rank = sb("m_rank", [P, B, E])
        m_first = sb("m_first", [P, B])
        m_eq = sb("m_eq", [P, B, E])
        m_hot = sb("m_hot", [P, B, E], BF16)
        MU = 2 * E + 2

        def unit_weights(k):
            e, half = k // 2, k % 2
            cols = slice(half * P, (half + 1) * P)
            if e < E:
                return gate_up[:, 0, e, cols], gate_up[:, 1, e, cols], down[:, e, half, :]
            return sh_gate_up[:, 0, cols], sh_gate_up[:, 1, cols], sh_down[:, half, :]

        def pe_self_attention(pe, transposes):
            transposes(xn2, XB, "norm_ready", nth("norm_ready", "a1"), "normT_psum")
            pe.wait_ge(sem("w_a0"), loads["w_a0"])
            pe.wait_ge(sem("normT_ready"), nth("normT_ready", "a1"))
            for b in range(B):
                pe.matmul(ps[:, b, 0:3 * D], xnT[:, b, :], wqkv0[:, :], start=True, stop=True)\
                  .then_inc(sem("a_qkv_psum"), 1)
            pe.wait_ge(sem("a_qk_ready"), B)
            for b in range(B):
                for i in range(2):
                    last = pe.transpose(ps[:, 4 + i, b * P:(b + 1) * P], a_qk[:, b, i * D:(i + 1) * D], ident[:, :])
            last.then_inc(sem("a_qkT_psum"), 1)

            def scores(u):
                b, half = u // 2, u % 2
                if half == 0:
                    pe.wait_ge(sem("a_qblk_ready"), b + 1)
                if u == 0:
                    pe.wait_ge(sem("a_kT_ready"), 1)
                if u >= 2:
                    pe.wait_ge(sem("a_exp_ready"), u - 1)
                for c in range(2):
                    lo = 8 * half + 4 * c
                    last = pe.matmul(ps[:, 2 * (u % 2) + c, :], a_kT[:, b, :], flat(a_qblk[b % 2][:, lo:lo + 4, :]),
                                     start=True, stop=True)
                last.then_inc(sem("a_scores_psum"), 1)

            def weigh(u):
                b, half = u // 2, u % 2
                pe.wait_ge(sem("a_exp_ready"), u + 1)
                if half == 0:
                    pe.wait_ge(sem("a_v_ready"), b + 2)
                    if b:
                        pe.wait_ge(sem("a_sums_ready"), b)
                for i in range(8):
                    h = 8 * half + i
                    last = pe.matmul(ps[32 * (h % 4):32 * (h % 4) + VW, OB, h // 4 * P:(h // 4 + 1) * P],
                                     a_v[:, b, h, :], a_probs[u % 2][:, i, :], start=True, stop=True)
                last.then_inc(sem("a_probs_used"), 1)

            scores(0)
            scores(1)
            for u in range(2 * B):
                weigh(u)
                if u + 2 < 2 * B:
                    scores(u + 2)
                if u % 2:
                    b = u // 2
                    pe.wait_ge(sem("a_sums_ready"), b + 1)
                    if b:
                        pe.wait_ge(sem("a_attended"), b)
                    for j in range(4):
                        last = pe.transpose(ps[:, XB, j * P:(j + 1) * P], a_sums[:, j, :], ident[:, :])
                    last.then_inc(sem("a_sumsT_psum"), 1)
            transposes(attn_tok, XB, "a_attended", B, "a_attnT_psum")
            pe.wait_ge(sem("a_attnT_ready"), 1)
            for b in range(B):
                last = pe.matmul(ps[:, OB, b * P:(b + 1) * P], xnT[:, b, :], wout0[:, :], start=True, stop=True)
            last.then_inc(sem("a_out_psum"), 1)

        def pe_local_attention(pe, transposes, l):
            n = l * B
            transposes(y, XB, "f_y_ready", 2 * l + 1, "f_yT_psum")
            pe.wait_ge(sem("f_hT_ready"), l + 1)
            for b in range(B):
                if b >= 2:
                    pe.wait_ge(sem("f_rot_ready"), n + b - 1)
                    pe.wait_ge(sem("f_v_ready"), n + b - 1)
                for i, bank in enumerate((2 * (b % 2), 2 * (b % 2) + 1, 4 + b % 2)):
                    last = pe.matmul(ps[:, bank, :], hT[:, b, :], wqkvf[:, l, i * INNER:(i + 1) * INNER],
                                     start=True, stop=True)
                last.then_inc(sem("f_qkv_psum"), 1)

            def qk_rows(b):
                pe.wait_ge(sem("f_kn_ready"), n + b + 1)
                if b:
                    pe.wait_ge(sem("f_qT_ready"), n + b)
                    pe.wait_ge(sem("f_kT_ready"), n + b)
                for i in range(2):
                    for t in range(4):
                        lo = i * INNER + t * P
                        last = pe.transpose(ps[:, i, t * P:(t + 1) * P], f_qk[b][:, lo:lo + P], ident[:, :])
                last.then_inc(sem("f_qkT_psum"), 1)

            def scores(b):
                pe.wait_ge(sem("f_qT_ready"), n + b + 1)
                pe.wait_ge(sem("f_kT_ready"), n + b + 1)
                if b:
                    pe.wait_ge(sem("f_exp_ready"), n + b)
                for c in range(2):
                    mask = spread(band_bf[:, :].rearrange("p (a k) -> p a k", a=1), 1, 4)
                    pe.matmul(ps[:, 2 + c, :].rearrange("p (a k) -> p a k", a=4), ident_bf[:, :], mask,
                              start=True, stop=False, skip_group_check=True)
                    for i in range(4):
                        h = 2 * i + c
                        rows = slice(FD * (h % 2), FD * (h % 2) + FD)
                        last = pe.matmul(ps[:, 2 + c, i * P:(i + 1) * P], f_qT[rows, h // 2, :], f_kT[rows, h // 2, :],
                                         start=False, stop=(i == 3), skip_group_check=True)
                last.then_inc(sem("f_scores_psum"), 1)

            def weigh(b):
                pe.wait_ge(sem("f_probsTa_ready"), n + b + 1)
                pe.wait_ge(sem("f_probsTb_ready"), n + b + 1)
                if b:
                    pe.wait_ge(sem("f_oT_ready"), n + b)
                for h in range(FH):
                    last = pe.matmul(ps[FD * (h % 2):FD * (h % 2) + FD, OB, h // 2 * P:(h // 2 + 1) * P],
                                     f_v[b][:, h * FD:(h + 1) * FD], f_probsT[:, h, :], start=True, stop=True)
                last.then_inc(sem("f_o_psum"), 1)

            def probs_rows(b):
                pe.wait_ge(sem("f_probs_ready"), n + b + 1)
                if b:
                    pe.wait_ge(sem("f_probsTa_ready"), n + b)
                    pe.wait_ge(sem("f_probsTb_ready"), n + b)
                for h in range(FH):
                    last = pe.transpose(ps[:, 4 + h // 4, h % 4 * P:(h % 4 + 1) * P], f_probs[:, h, :], ident[:, :])
                last.then_inc(sem("f_probsT_psum"), 1)

            qk_rows(0)
            scores(0)
            for b in range(B):
                if b + 1 < B:
                    qk_rows(b + 1)
                probs_rows(b)
                if b + 1 < B:
                    scores(b + 1)
                weigh(b)
                pe.wait_ge(sem("f_oT_ready"), n + b + 1)
                for t in range(4):
                    last = pe.matmul(ps[:, XB, b * P:(b + 1) * P], f_oT[:, t, :], wof[:, l, t, :],
                                     start=(t == 0), stop=(t == 3))
                last.then_inc(sem("f_attn_psum"), 1)

        def pe_gated(pe, transposes, l):
            pe.wait_ge(sem("f_y_ready"), 2 * l + 2)
            pe.matmul(ps[:, 0, 0:B * 64].rearrange("p (b d) -> p b d", b=B), shift[:, :], y[:, :, 64:D],
                      start=True, stop=True).then_inc(sem("f_shift_psum"), 1)
            transposes(xn, XB, "norm_ready", nth("norm_ready", f"g{l}"), "normT_psum")
            pe.wait_ge(sem("normT_ready"), nth("normT_ready", f"g{l}"))
            for m in range(3):
                for ag in range(2):
                    lo = ag * HID + m * P
                    last = pe.matmul(ps[0:HT[m], (2 + 2 * m + ag) % 6, :], w1f[:, l, lo:lo + HT[m]], flat(xnT[:, :, :]),
                                     start=True, stop=True)
                last.then_inc(sem("f_w1_psum"), 1)
            pe.wait_ge(sem("f_act_ready"), 3 * l + 3)
            for b in range(B):
                for m in range(3):
                    last = pe.matmul(ps[:, OB, b * P:(b + 1) * P], f_act[m][0:HT[m], b * P:(b + 1) * P],
                                     w2f[0:HT[m], l, m, :], start=(m == 0), stop=(m == 2))
            last.then_inc(sem("f_w2_psum"), 1)

        def pe_middle0(pe, transposes):
            pe_self_attention(pe, transposes)
            pe.wait_ge(sem("w_f0"), loads["w_f0"])
            pe.wait_ge(sem("band_ready"), 1)
            for l in range(2):
                pe_local_attention(pe, transposes, l)
                pe_gated(pe, transposes, l)

        def pe_middle1(pe, transposes):
            transposes(xn, XB, "norm_ready", nth("norm_ready", "s1"), "normT_psum")
            pe.wait_ge(sem("normT_ready"), nth("normT_ready", "s1"))
            pe.wait_ge(sem("w_a1"), loads["w_a1"])
            pe.matmul(ps[:, 0, :], wspin[:, :], flat(xnT[:, :, :]), start=True, stop=True).then_inc(sem("s_T_psum"), 1)
            for b in range(B):
                last = pe.matmul(ps[:, 1, b * P:(b + 1) * P], xnT[:, b, :], wspin[:, :], start=True, stop=True)
            last.then_inc(sem("s_tok_psum"), 1)
            pe.wait_ge(sem("s_T_ready"), 1)
            pe.matmul(ps[:, 2, :], wj[:, :], flat(s_T[:, :, :]), start=True, stop=True).then_inc(sem("s_eT_psum"), 1)
            pe.wait_ge(sem("s_eT_ready"), 1)
            for b in range(B):
                last = pe.matmul(ps[:, 3, b * P:(b + 1) * P], s_eT[:, b, :], s_T[:, b, :], start=True, stop=True)
            last.then_inc(sem("s_scores_psum"), 1)
            transposes(s_probs, XB, "s_probs_ready", 1, "s_probsT_psum")
            pe.wait_ge(sem("s_probsT_ready"), 1)
            pe.wait_ge(sem("s_tok_ready"), 1)
            pe.wait_ge(sem("s_mean_ready"), 1)
            for b in range(B):
                pe.matmul(ps[:, 4, b * P:(b + 1) * P], s_probsT[:, b, :], s_tok[:, b, :], start=True, stop=False)
                last = pe.matmul(ps[:, 4, b * P:(b + 1) * P], s_meanrows[:, b, :], wglob[:, :], start=False, stop=True)
            last.then_inc(sem("s_field_psum"), 1)

            transposes(xn, XB, "norm_ready", nth("norm_ready", "m1"), "normT_psum")
            pe.wait_ge(sem("normT_ready"), nth("normT_ready", "m1"))
            pe.wait_ge(sem("w_m1"), loads["w_m1"])
            for b in range(B):
                last = pe.matmul(ps[:, 0, b * E:(b + 1) * E], xnT[:, b, :], wgate[:, :], start=True, stop=True)
            last.then_inc(sem("m_logit_psum"), 1)
            pe.wait_ge(sem("m_hot_ready"), 1)
            transposes(m_xs, 2, "m_xs_ready", 1, "m_xsT_psum")

            def expert_mask(e):
                if e:
                    pe.wait_ge(sem("m_xe_ready"), e)
                for b in range(B):
                    hot = spread(m_hot[:, b, e:e + 1], 1, P)
                    last = pe.matmul(ps[:, 1, b * P:(b + 1) * P], hot, ident_bf[:, :], start=True, stop=True)
                last.then_inc(sem("m_mask_psum"), 1)

            def gate_and_up(k):
                e = k // 2
                if k % 2 == 0 and e < E:
                    pe.wait_ge(sem("m_xe_ready"), e + 1)
                if k >= 3:
                    pe.wait_ge(sem("m_act_ready"), k - 2)
                wg, wu, _ = unit_weights(k)
                src = flat(m_xe[e % 2][:, :, :] if e < E else xnT[:, :, :])
                pe.matmul(ps[:, 2 + 2 * (k % 3), :], wg, src, start=True, stop=True)
                pe.matmul(ps[:, 3 + 2 * (k % 3), :], wu, src, start=True, stop=True).then_inc(sem("m_gu_psum"), 1)

            def project_down(k):
                pe.wait_ge(sem("m_act_ready"), k + 1)
                for b in range(B):
                    last = pe.matmul(ps[:, 0, b * P:(b + 1) * P], m_act[k % 3][:, b, :], unit_weights(k)[2],
                                     start=(k == 0 and b == 0), stop=(k == MU - 1 and b == B - 1),
                                     skip_group_check=True)
                last.then_inc(sem("m_down_psum"), 1)

            expert_mask(0)
            pe.wait_ge(sem("w_e"), loads["w_e"])
            pe.wait_ge(sem("m_xsT_ready"), 1)
            for k in range(MU):
                if k % 2 == 0 and k // 2 + 1 < E:
                    expert_mask(k // 2 + 1)
                gate_and_up(k)
                if k:
                    project_down(k - 1)
            project_down(MU - 1)

        def act_middle0(act, copy):
            def rows_from(bank):
                return ps[:, bank, :].rearrange("p (b q) -> p b q", b=B)

            act.wait_ge(sem("normT_psum"), nth("normT_psum", "a1"))
            act.wait_ge(sem("w_a0"), loads["w_a0"])
            act.activation(xnT[:, :, :], rows_from(XB), ACT.Identity, bias=lnb0[:, :], scale=lnw0[:, :])\
               .then_inc(sem("normT_ready"), 1)
            for b in range(B):
                act.wait_ge(sem("a_qkv_ready"), b + 1)
                act.activation(a_sq[:, b, :], a_qkv[:, b, 0:2 * D], ACT.Square).then_inc(sem("a_sq_ready"), 1)
            act.wait_ge(sem("a_ss_ready"), B)
            act.activation(a_norm[:, :, :], a_ss[:, :, :], ACT.Sqrt).then_inc(sem("a_norm_ready"), 1)
            act.wait_ge(sem("k_part2_ready"), B + 1)
            act.wait_ge(sem("a_qkT_psum"), 1)
            copy(a_kT[:, :, :], rows_from(5)).then_inc(sem("a_kT_ready"), 1)
            for u in range(2 * B):
                act.wait_ge(sem("a_scores_psum"), u + 1)
                if u >= 2:
                    act.wait_ge(sem("a_probs_used"), u - 1)
                bank = 2 * (u % 2)
                act.activation(flat(a_probs[u % 2][:, :, :]), ps[:, bank:bank + 2, :].rearrange("p a c -> p (a c)"),
                               ACT.Exp, scale=HD ** 0.5).then_inc(sem("a_exp_ready"), 1)
                if u % 2:
                    b = u // 2
                    act.wait_ge(sem("a_probs_used"), u + 1)
                    if b:
                        act.wait_ge(sem("a_sumsT_psum"), b)
                    copy(a_sums[:, :, :], rows_from(OB)).then_inc(sem("a_sums_ready"), 1)
            act.wait_ge(sem("a_attnT_psum"), 1)
            copy(xnT[:, :, :], rows_from(XB)).then_inc(sem("a_attnT_ready"), 1)

            act.wait_ge(sem("w_f0"), loads["w_f0"])
            for l in range(2):
                n = l * B
                act.wait_ge(sem("f_yT_psum"), l + 1)
                copy(hT[0:64, :, :], rows_from(XB)[0:64])
                copy(hT[64:P, :, 1:P], rows_from(XB)[64:P, :, 0:P - 1]).then_inc(sem("f_hT_ready"), 1)
                for b in range(B):
                    act.wait_ge(sem("f_qkv_psum"), n + b + 1)
                    if b >= 2:
                        act.wait_ge(sem("f_ss_ready"), n + b - 1)
                    bank = 2 * (b % 2)
                    act.activation(f_sq[b % 2], ps[:, bank:bank + 2, :].rearrange("p a c -> p (a c)"), ACT.Square)\
                       .then_inc(sem("f_sq_ready"), 1)
                    copy(f_v[b], ps[:, 4 + b % 2, :]).then_inc(sem("f_v_ready"), 1)
                act.wait_ge(sem("f_ss_ready"), n + B)
                act.activation(f_norm[:, :, :], f_ss[:, :, :], ACT.Sqrt).then_inc(sem("f_norm_ready"), 1)

                def q_rows(b):
                    act.wait_ge(sem("f_qkT_psum"), n + b + 1)
                    if b:
                        act.wait_ge(sem("f_scores_psum"), n + b)
                    copy(f_qT[:, :, :], ps[:, 0, :].rearrange("p (t q) -> p t q", t=4)).then_inc(sem("f_qT_ready"), 1)

                q_rows(0)
                for b in range(B):
                    act.wait_ge(sem("f_bias_ready"), n + b + 1)
                    if b:
                        act.wait_ge(sem("f_probsT_psum"), n + b)
                    for h in range(FH):
                        last = act.activation(f_probs[:, h, :], ps[:, 2 + h % 2, h // 2 * P:(h // 2 + 1) * P], ACT.Exp,
                                              bias=f_bias[:, h:h + 1], scale=f_qs[:, b, h:h + 1],
                                              accum_out=f_den[:, h:h + 1])
                    last.then_inc(sem("f_exp_ready"), 1)
                    if b + 1 < B:
                        q_rows(b + 1)
                    act.wait_ge(sem("f_probsT_psum"), n + b + 1)
                    if b:
                        act.wait_ge(sem("f_o_psum"), n + b)
                    copy(flat(f_probsT[:, 0:4, :]), ps[:, 4, :]).then_inc(sem("f_probsTa_ready"), 1)
                    act.wait_ge(sem("f_o_psum"), n + b + 1)
                    if b:
                        act.wait_ge(sem("f_attn_psum"), n + b)
                    copy(f_oT[:, :, :], ps[:, OB, :].rearrange("p (t q) -> p t q", t=4)).then_inc(sem("f_oT_ready"), 1)

                act.wait_ge(sem("normT_psum"), nth("normT_psum", f"g{l}"))
                act.activation(xnT[:, :, :], rows_from(XB), ACT.Identity, bias=lbf[:, l:l + 1], scale=lgf[:, l:l + 1])\
                   .then_inc(sem("normT_ready"), 1)
                for m in range(3):
                    act.wait_ge(sem("f_w1_psum"), 3 * l + m + 1)
                    act.activation(f_gelu[m][0:HT[m], :], ps[0:HT[m], (3 + 2 * m) % 6, :], ACT.Gelu,
                                   bias=b1f[0:HT[m], l, 1, m:m + 1]).then_inc(sem("f_gelu_ready"), 1)

        def act_middle1(act, copy):
            def rows_from(bank):
                return ps[:, bank, :].rearrange("p (b q) -> p b q", b=B)

            act.wait_ge(sem("normT_psum"), nth("normT_psum", "s1"))
            copy(xnT[:, :, :], rows_from(XB)).then_inc(sem("normT_ready"), 1)
            act.wait_ge(sem("s_T_psum"), 1)
            act.wait_ge(sem("w_a1"), loads["w_a1"])
            act.activation(s_T[:, :, :], rows_from(0), ACT.Identity, bias=bspin_col[:, :]).then_inc(sem("s_T_ready"), 1)
            act.wait_ge(sem("s_eT_psum"), 1)
            copy(s_eT[:, :, :], rows_from(2)).then_inc(sem("s_eT_ready"), 1)
            act.wait_ge(sem("s_bias_ready"), 1)
            for b in range(B):
                last = act.activation(s_probs[:, b, :], ps[:, 3, b * P:(b + 1) * P], ACT.Exp, bias=s_bias[:, b:b + 1],
                                      scale=D ** -0.5, accum_out=s_den[:, b:b + 1])
            last.then_inc(sem("s_exp_ready"), 1)
            act.wait_ge(sem("s_probsT_psum"), 1)
            copy(s_probsT[:, :, :], rows_from(XB)).then_inc(sem("s_probsT_ready"), 1)
            act.wait_ge(sem("s_sum_ready"), 1)
            act.activation(xn2[:, :, :], ytmp[:, :, :], ACT.Tanh, scale=beta[:, :]).then_inc(sem("s_tanh_ready"), 1)

            act.wait_ge(sem("normT_psum"), nth("normT_psum", "m1"))
            copy(xnT[:, :, :], rows_from(XB)).then_inc(sem("normT_ready"), 1)
            act.wait_ge(sem("m_top_ready"), 1)
            act.activation(m_tanh[:, :], m_top[:, :], ACT.Tanh, scale=0.5).then_inc(sem("m_tanh_ready"), 1)
            act.wait_ge(sem("m_xsT_psum"), 1)
            copy(m_xsT[:, :, :], rows_from(2)).then_inc(sem("m_xsT_ready"), 1)
            for k in range(MU):
                act.wait_ge(sem("m_gu_psum"), k + 1)
                if k >= 3:
                    act.wait_ge(sem("m_act_ready"), k - 2)
                act.activation(m_silu[k % 3], ps[:, 2 + 2 * (k % 3), :], ACT.Silu).then_inc(sem("m_silu_ready"), 1)

        def wide(v, n):
            return spread(v.rearrange("p (a b) -> p a b", b=1), 2, n)

        def dve_middle0(dve, link, norm):
            norm(x, xn, "a0").then_inc(sem("norm_ready"), 1)
            dve.wait_ge(sem("norm_ready"), nth("norm_ready", "a0"))
            norm(xn, xn2, "a1").then_inc(sem("norm_ready"), 1)
            dve.wait_ge(sem("w_a0"), loads["w_a0"])
            for b in range(B):
                dve.wait_ge(sem("a_qkv_psum"), b + 1)
                dve.tensor_tensor(a_qkv[:, b, :], ps[:, b, 0:3 * D], bqkv0[:, :], ALU.add)\
                   .then_inc(sem("a_qkv_ready"), 1)
            for b in range(B):
                dve.wait_ge(sem("a_sq_ready"), b + 1)
                dve.tensor_reduce(a_ss[:, b, :], a_sq[:, b, :].rearrange("p (h d) -> p h d", d=HD), AX.X, ALU.add)\
                   .then_inc(sem("a_ss_ready"), 1)
            dve.wait_ge(sem("a_norm_ready"), 1)
            link(dve.tensor_scalar(a_norm[:, :, :], a_norm[:, :, :], 1e-12, None, ALU.max))
            link(dve.reciprocal(a_inv[:, :, :], a_norm[:, :, :]))
            for b in range(B):
                dve.tensor_tensor(a_qk[:, b, :].rearrange("p (h d) -> p h d", d=HD),
                                  a_qkv[:, b, 0:2 * D].rearrange("p (h d) -> p h d", d=HD),
                                  wide(a_inv[:, b, :], HD), ALU.mult).then_inc(sem("a_qk_ready"), 1)

            def query_block(b):
                q = spread(ps[:, 4, b * P:(b + 1) * P].rearrange("p (a q) -> p a q", a=1), 1, H)
                dve.tensor_tensor(a_qblk[b % 2][:, :, :], q, wide(headmask[:, :], P), ALU.mult)\
                   .then_inc(sem("a_qblk_ready"), 1)

            dve.wait_ge(sem("a_qkT_psum"), 1)
            query_block(0)
            query_block(1)
            for b in range(B):
                if b + 2 < B:
                    dve.wait_ge(sem("a_scores_psum"), 2 * b + 2)
                    query_block(b + 2)
                dve.wait_ge(sem("a_sumsT_psum"), b + 1)
                sumsT = ps[:, XB, :].rearrange("p (h w) -> p h w", w=32)
                link(dve.reciprocal(a_rden[:, :], sumsT[:, :, HD]))
                dve.tensor_tensor(attn_tok[:, b, :].rearrange("p (h d) -> p h d", d=HD), sumsT[:, :, 0:HD],
                                  wide(a_rden[:, :], HD), ALU.mult).then_inc(sem("a_attended"), 1)
            dve.wait_ge(sem("a_out_psum"), 1)
            dve.wait_ge(sem("a_res_ready"), 2)
            link(dve.tensor_tensor(x[:, :, :], xres[:, :, :], ps[:, OB, :].rearrange("p (b d) -> p b d", b=B), ALU.add))

            dve.wait_ge(sem("w_rot"), loads["w_rot"])
            dve.tensor_copy(band_bf[:, :], band[:, :]).then_inc(sem("band_ready"), 1)
            norm(x, y, "f0").then_inc(sem("f_y_ready"), 1)
            dve.wait_ge(sem("rotl_ready"), 2)
            for l in range(2):
                n = l * B
                for b in range(B):
                    dve.wait_ge(sem("f_sq_ready"), n + b + 1)
                    dve.tensor_reduce(f_ss[:, b, :], f_sq[b % 2].rearrange("p (h d) -> p h d", d=FD), AX.X, ALU.add)\
                       .then_inc(sem("f_ss_ready"), 1)
                    if b >= 2:
                        dve.wait_ge(sem("f_rotsum_ready"), n + b - 1)
                    for i in range(2):
                        src = ps[:, 2 * (b % 2) + i, :].rearrange("p (h d) -> p h d", h=FH)
                        cols = slice(i * INNER, (i + 1) * INNER)
                        cos = spread(rotl[:, l, 2 * i:2 * i + 1, :], 1, FH)
                        dve.tensor_tensor(f_cos[b % 2][:, cols].rearrange("p (h d) -> p h d", h=FH), src, cos, ALU.mult)
                        for half in range(2):
                            to = slice(half * 32, half * 32 + 32)
                            of = slice(32 - half * 32, 64 - half * 32)
                            sin = spread(rotl[:, l, 2 * i + 1:2 * i + 2, to], 1, FH)
                            last = dve.tensor_tensor(f_sin[b % 2][:, cols].rearrange("p (h d) -> p h d", h=FH)[:, :, to],
                                                     src[:, :, of], sin, ALU.mult)
                    last.then_inc(sem("f_rot_ready"), 1)
                dve.wait_ge(sem("f_norm_ready"), l + 1)
                link(dve.tensor_scalar(f_norm[:, :, :], f_norm[:, :, :], 1e-12, None, ALU.max))
                link(dve.reciprocal(f_inv[:, :, :], f_norm[:, :, :]))
                link(dve.tensor_scalar(f_qs[:, :, :], f_inv[:, :, 0:FH], 8.0, None, ALU.mult))
                for b in range(B):
                    dve.wait_ge(sem("f_rotsum_ready"), n + b + 1)
                    k = f_qk[b][:, INNER:2 * INNER].rearrange("p (h d) -> p h d", h=FH)
                    dve.tensor_tensor(k, k, wide(f_inv[:, b, FH:2 * FH], FD), ALU.mult).then_inc(sem("f_kn_ready"), 1)

                def k_rows(b):
                    dve.wait_ge(sem("f_qkT_psum"), n + b + 1)
                    if b:
                        dve.wait_ge(sem("f_scores_psum"), n + b)
                    dve.tensor_copy(f_kT[:, :, :], ps[:, 1, :].rearrange("p (t q) -> p t q", t=4))\
                       .then_inc(sem("f_kT_ready"), 1)

                def maxima(b):
                    dve.wait_ge(sem("f_scores_psum"), n + b + 1)
                    link(dve.tensor_reduce(f_max[:, :], ps[:, 2:4, :].rearrange("p a (h k) -> p (a h) k", h=4),
                                           AX.X, ALU.max, negate=True))
                    if b:
                        dve.wait_ge(sem("f_exp_ready"), n + b)
                    dve.tensor_tensor(f_bias[:, :].rearrange("p (j e) -> p e j", e=2),
                                      f_max[:, :].rearrange("p (e j) -> p e j", e=2),
                                      f_qs[:, b, :].rearrange("p (j e) -> p e j", e=2), ALU.mult)\
                       .then_inc(sem("f_bias_ready"), 1)

                k_rows(0)
                maxima(0)
                for b in range(B):
                    dve.wait_ge(sem("f_exp_ready"), n + b + 1)
                    link(dve.reciprocal(f_rden[:, :], f_den[:, :]))
                    dve.tensor_tensor(f_probs[:, :, :], f_probs[:, :, :], wide(f_rden[:, :], P), ALU.mult)\
                       .then_inc(sem("f_probs_ready"), 1)
                    if b + 1 < B:
                        k_rows(b + 1)
                    dve.wait_ge(sem("f_probsT_psum"), n + b + 1)
                    if b:
                        dve.wait_ge(sem("f_o_psum"), n + b)
                    dve.tensor_copy(flat(f_probsT[:, 4:8, :]), ps[:, 5, :]).then_inc(sem("f_probsTb_ready"), 1)
                    if b + 1 < B:
                        maxima(b + 1)
                dve.wait_ge(sem("f_attn_psum"), n + B)
                dve.tensor_tensor(y[:, :, :], y[:, :, :], ps[:, XB, :].rearrange("p (b d) -> p b d", b=B), ALU.add)\
                   .then_inc(sem("f_y_ready"), 1)
                dve.wait_ge(sem("f_shift_psum"), l + 1)
                dve.wait_ge(sem("f_unshifted_ready"), l + 1)
                link(dve.tensor_copy(f_shift[:, :, 64:D], ps[:, 0, 0:B * 64].rearrange("p (b d) -> p b d", b=B)))
                norm(f_shift, xn, f"g{l}").then_inc(sem("norm_ready"), 1)
                for m in range(3):
                    dve.wait_ge(sem("f_gelu_ready"), 3 * l + m + 1)
                    rows = slice(0, HT[m])
                    dve.scalar_tensor_tensor(f_act[m][rows, :], ps[rows, (2 + 2 * m) % 6, :], b1f[rows, l, 0, m:m + 1],
                                             f_gelu[m][rows, :], ALU.add, ALU.mult).then_inc(sem("f_act_ready"), 1)
                dve.wait_ge(sem("f_w2_psum"), l + 1)
                dve.wait_ge(sem("f_biased_ready"), l + 1)
                dve.tensor_tensor(y[:, :, :], ytmp[:, :, :], ps[:, OB, :].rearrange("p (b d) -> p b d", b=B), ALU.add)\
                   .then_inc(sem("f_y_ready"), 1)
                dve.wait_ge(sem("f_y_ready"), 2 * l + 3)
            link(dve.tensor_tensor(x[:, :, :], x[:, :, :], y[:, :, :], ALU.add))

        def dve_middle1(dve, link, norm):
            norm(x, xn, "s1").then_inc(sem("norm_ready"), 1)
            dve.wait_ge(sem("w_a1"), loads["w_a1"])
            dve.wait_ge(sem("s_tok_psum"), 1)
            bias = spread(bspin_row[:, :].rearrange("p (a n) -> p a n", a=1), 1, B)
            dve.tensor_tensor(s_tok[:, :, :], ps[:, 1, :].rearrange("p (b d) -> p b d", b=B), bias, ALU.add)\
               .then_inc(sem("s_tok_ready"), 1)
            dve.wait_ge(sem("s_T_ready"), 1)
            link(dve.tensor_reduce(s_mean[:, :], s_T[:, :, :], AX.X, ALU.add))
            dve.tensor_scalar(s_meanrows[:, :, :], wide(s_mean[:, :], P), 1.0 / P, None, ALU.mult)\
               .then_inc(sem("s_mean_ready"), 1)
            dve.wait_ge(sem("s_scores_psum"), 1)
            link(dve.tensor_reduce(s_max[:, :], ps[:, 3, :].rearrange("p (b q) -> p b q", b=B), AX.X, ALU.max,
                                   negate=True))
            dve.tensor_scalar(s_bias[:, :], s_max[:, :], D ** -0.5, None, ALU.mult).then_inc(sem("s_bias_ready"), 1)
            dve.wait_ge(sem("s_exp_ready"), 1)
            link(dve.reciprocal(s_rden[:, :], s_den[:, :]))
            dve.tensor_tensor(s_probs[:, :, :], s_probs[:, :, :], wide(s_rden[:, :], P), ALU.mult)\
               .then_inc(sem("s_probs_ready"), 1)
            dve.wait_ge(sem("s_field_psum"), 1)
            dve.wait_ge(sem("s_tok_ready"), 1)
            dve.tensor_tensor(ytmp[:, :, :], ps[:, 4, :].rearrange("p (b d) -> p b d", b=B), s_tok[:, :, :], ALU.add)\
               .then_inc(sem("s_sum_ready"), 1)
            dve.wait_ge(sem("s_tanh_ready"), 1)
            link(dve.tensor_tensor(x[:, :, :], x[:, :, :], xn2[:, :, :], ALU.add))

            norm(x, xn, "m1").then_inc(sem("norm_ready"), 1)
            dve.wait_ge(sem("w_m1"), loads["w_m1"])
            dve.wait_ge(sem("m_logit_psum"), 1)
            logits = ps[:, 0, 0:B * E].rearrange("p (b e) -> p b e", b=B)
            link(dve.tensor_copy(m_logit[:, :, :], logits))
            dve.tensor_reduce(m_top[:, :], m_logit[:, :, :], AX.X, ALU.max).then_inc(sem("m_top_ready"), 1)
            dve.wait_ge(sem("m_top_ready"), 1)
            link(dve.tensor_tensor(m_eq[:, :, :], m_logit[:, :, :], wide(m_top[:, :], E), ALU.is_equal))
            link(dve.tensor_tensor(m_rank[:, :, :], m_eq[:, :, :], erank[:, :, :], ALU.mult))
            link(dve.tensor_reduce(m_first[:, :], m_rank[:, :, :], AX.X, ALU.max))
            dve.tensor_tensor(m_hot[:, :, :], m_rank[:, :, :], wide(m_first[:, :], E), ALU.is_equal)\
               .then_inc(sem("m_hot_ready"), 1)
            dve.wait_ge(sem("m_tanh_ready"), 1)
            link(dve.tensor_scalar(m_score[:, :], m_tanh[:, :], 0.5, 0.5, ALU.mult, ALU.add))
            dve.tensor_tensor(m_xs[:, :, :], xn[:, :, :], wide(m_score[:, :], D), ALU.mult)\
               .then_inc(sem("m_xs_ready"), 1)
            dve.wait_ge(sem("m_xsT_ready"), 1)

            def expert_rows(e):
                dve.wait_ge(sem("m_mask_psum"), e + 1)
                if e >= 2:
                    dve.wait_ge(sem("m_gu_psum"), 2 * (e - 1))
                dve.tensor_tensor(m_xe[e % 2][:, :, :], m_xsT[:, :, :], ps[:, 1, :].rearrange("p (b q) -> p b q", b=B),
                                  ALU.mult).then_inc(sem("m_xe_ready"), 1)

            expert_rows(0)
            for k in range(MU):
                if k % 2 == 0 and k // 2 + 1 < E:
                    expert_rows(k // 2 + 1)
                dve.wait_ge(sem("m_silu_ready"), k + 1)
                if k >= 3:
                    dve.wait_ge(sem("m_down_psum"), k - 2)
                dve.tensor_tensor(flat(m_act[k % 3][:, :, :]), m_silu[k % 3], ps[:, 3 + 2 * (k % 3), :], ALU.mult)\
                   .then_inc(sem("m_act_ready"), 1)
            dve.wait_ge(sem("m_down_psum"), MU)
            dve.tensor_tensor(xn2[:, :, :], x[:, :, :], ps[:, 0, :].rearrange("p (b d) -> p b d", b=B), ALU.add)\
               .then_inc(sem("out_ready"), 1)

        def pool_middle0(pool, rstd_of, alone):
            rstd_of("a0")
            pool.wait_ge(sem("norm_ready"), nth("norm_ready", "a0"))
            rstd_of("a1")
            alone(pool.tensor_tensor(xres[:, :, :], x[:, :, :], xn[:, :, :], ALU.add), "a_res_ready", 1)
            pool.wait_ge(sem("w_a0"), loads["w_a0"])
            alone(pool.tensor_tensor(xres[:, :, :], xres[:, :, :],
                                     spread(bout0[:, :].rearrange("p (a n) -> p a n", a=1), 1, B), ALU.add),
                  "a_res_ready", 2)
            alone(pool.memset(a_v[:, :, :, HD], 1.0), "a_v_ready", 1)
            for b in range(B):
                pool.wait_ge(sem("a_qkv_ready"), b + 1)
                alone(pool.tensor_copy(a_v[:, b, :, 0:HD],
                                       a_qkv[:, b, 2 * D:3 * D].rearrange("p (h d) -> p h d", d=HD)),
                      "a_v_ready", b + 2)
            pool.wait_ge(sem("w_rot"), loads["w_rot"])
            for l in range(2):
                alone(pool.tensor_tensor(rotl[:, l, :, :], rot[:, :, :], rot_scale[:, l, :, :], ALU.mult),
                      "rotl_ready", l + 1)
            rstd_of("f0")
            pool.wait_ge(sem("w_f0"), loads["w_f0"])
            for l in range(2):
                n = l * B
                for b in range(B):
                    pool.wait_ge(sem("f_rot_ready"), n + b + 1)
                    alone(pool.tensor_tensor(f_qk[b], f_cos[b % 2], f_sin[b % 2], ALU.add),
                          "f_rotsum_ready", n + b + 1)
                pool.wait_ge(sem("f_y_ready"), 2 * l + 2)
                alone(pool.tensor_copy(f_shift[:, :, 0:64], y[:, :, 0:64]), "f_unshifted_ready", l + 1)
                rstd_of(f"g{l}")
                alone(pool.tensor_tensor(ytmp[:, :, :], y[:, :, :], spread(b2f[:, l:l + 1, :], 1, B), ALU.add),
                      "f_biased_ready", l + 1)

        def pool_middle1(pool, rstd_of):
            rstd_of("s1")
            rstd_of("m1")

        FREED_BY = {"T": "ctxT_ready", "K": "k_rest_ready", "V": "v_ready", "M": "max_taken"}

        @block.sync
        def _(sp):
            def load(dst, src, name):
                sp.dma_start(dst, src).then_inc(sem(name), 16)
                loads[name] = loads.get(name, 0) + 16

            def col(ap):
                return ap.rearrange("(p a) -> p a", a=1)

            def rows(ap):
                return spread(ap.rearrange("(a n) -> a n", a=1), 0, P)

            def load_context(b):
                src = a["ctx"][bass.ds(b, 1), :, :].rearrange("o (t p) d -> p (o t) d", p=P)
                for half in (slice(0, P // 2), slice(P // 2, P)):
                    sp.dma_start(ctx_in[half, :, :], src[half]).then_inc(sem("ctx_in_ready"), 16)

            def store_queries(l):
                if l:
                    sp.wait_ge(sem("qstack_ready"), 192)
                for i in range(3):
                    sp.wait_ge(sem(f"q_part{i}_ready"), l + 1)
                    sp.dma_start(q_dram[i], q_part[i][:, :]).then_inc(sem("q_stored"), 16)

            def stack_queries(l, par):
                if par == 0:
                    sp.wait_ge(sem("q_stored"), 48 * (l + 1))
                    sp.wait_ge(sem("qstack_cleared"), 2)
                for r in range(6):
                    lo = (2 * r + par) * HD
                    src = q_dram[PART_Q[r]].rearrange("(j e d) n -> e d j n", e=2, d=HD)[par]
                    sp.dma_start(qstack[lo:lo + HD, :, par, :, :].rearrange("d j b q -> d j (b q)"), src)\
                      .then_inc(sem("qstack_ready"), 16)

            def stack_rows(i, parity, lo, hi):
                for r in range(6):
                    if PART_K[r] == i:
                        dst = kstack[2 * HD * r:2 * HD * (r + 1), bass.ds(parity, 1), lo:hi, :]
                        src = k_dram[i][lo * 2 * HD:hi * 2 * HD].rearrange("(j p) n -> p j n", p=2 * HD)
                        sp.dma_start(dst.rearrange("p o j n -> p (o j) n"), src)\
                          .then_inc(sem("first_k_stacked" if hi == 2 else "kstack_ready"), 16)

            def stack_keys(n, parity):
                sp.wait_ge(sem("kstack_ready"), n * 96)
                for i in range(3):
                    per = (2, 4, 1)[i]
                    sp.wait_ge(sem(f"k_part{i}_ready"), n * per + per)
                    sp.dma_start(k_dram[i], k_part[i][:, :]).then_inc(sem("k_stored"), 16)
                    sp.wait_ge(sem("k_stored"), n * 48 + 16 * (i + 1))
                    stack_rows(i, parity, 0, PAIRS)

            def store_first_keys(i, group):
                sp.wait_ge(sem(f"k_part{i}_ready"), (2, 4, 1)[i])
                rows = (slice(0, 4 * HD), slice(4 * HD, P))[group]
                sp.dma_start(k_dram[i][rows], k_part[i][rows, :]).then_inc(sem(("first_k_stored", "k_stored")[group]), 16)

            def stack_first_keys(group):
                sp.wait_ge(sem(("first_k_stored", "k_stored")[group]), 48)
                for i in range(3):
                    stack_rows(i, 0, *((0, 2), (2, PAIRS))[group])

            def stack_mask(b, parity):
                src = spread(m_dram[bass.ds(b, 1), :].rearrange("o (a n) -> o a n", a=1), 1, PAIRS)
                dst = kstack[MASK_ROW:MASK_ROW + 1, bass.ds(parity, 1), :, :].rearrange("d o j n -> d (o j) n")
                sp.dma_start(dst, src).then_inc(sem("mask_stacked"), 16)

            def rows_under(parities):
                times = len(parities) * PAIRS * CTX // BANK
                src = spread(row_init[MASK_ROW:KROWS_EXP, :].rearrange("d (a n) -> d a n", a=1), 1, times)
                dst = kstack[MASK_ROW:KROWS_EXP, parities[0]:, :, :].rearrange("d o j (c n) -> d (o j c) n", n=BANK)
                sp.dma_start(dst, src).then_inc(sem("rows_stacked"), 16)

            def cross_weights(l):
                for n in ("k", "q", "v", "o"):
                    src = a[f"L{l}_xattn_b{n}"]
                    load(wx[l][n][:, :], a[f"L{l}_xattn_W{n}"], f"w_{n}{l}")
                    load(bx[l][n][:, :], col(src) if n in "qk" else rows(src), f"w_{n}{l}")

            def weights_after():
                cross_weights(1)
                load(wqkv0[:, :], a["L0_attn_qkv_wT"], "w_a0")
                load(bqkv0[:, :], rows(a["L0_attn_qkv_b"]), "w_a0")
                load(wout0[:, :], a["L0_attn_out_wT"], "w_a0")
                load(bout0[:, :], rows(a["L0_attn_out_b"]), "w_a0")
                load(lnw0[:, :], col(a["L0_attn_ln_w"]), "w_a0")
                load(lnb0[:, :], col(a["L0_attn_ln_b"]), "w_a0")
                load(headmask[:, :], a["c_headmask"], "w_a0")
                load(rot[:, :, :], a["c_rot"], "w_rot")
                for l in range(2):
                    for i, n in enumerate(("q", "k")):
                        s = a[f"L0_ffn_{n}_scale"][l]
                        load(rot_scale[:, l, 2 * i, :], rows(s), "w_rot")
                        load(rot_scale[:, l, 2 * i + 1, 0:32], rows(s[32:64]), "w_rot")
                        load(rot_scale[:, l, 2 * i + 1, 32:64], rows(s[0:32]), "w_rot")
                load(band[:, :], a["c_band"], "w_rot")
                load(shift[:, :], a["c_shift"], "w_f0")
                for l in range(2):
                    load(wqkvf[:, l, :], a["L0_ffn_wqkv"][l], "w_f0")
                    load(wof[:, l, :, :], a["L0_ffn_wo"][l].rearrange("(t p) n -> p t n", p=P), "w_f0")
                    load(w1f[:, l, :], a["L0_ffn_w1"][l], "w_f0")
                    load(w2f[:, l, 0:2, :], a["L0_ffn_w2"][l, 0:2 * P, :].rearrange("(t p) n -> p t n", p=P), "w_f0")
                    load(w2f[0:HT[2], l, 2, :], a["L0_ffn_w2"][l, 2 * P:HID, :], "w_f0")
                    load(lgf[:, l:l + 1], col(a["L0_ffn_ln_g"][l]), "w_f0")
                    load(lbf[:, l:l + 1], col(a["L0_ffn_ln_b"][l]), "w_f0")
                    load(b2f[:, l, :], rows(a["L0_ffn_b2"][l]), "w_f0")
                    for ag in range(2):
                        for m in range(3):
                            lo = ag * HID + m * P
                            load(b1f[0:HT[m], l, ag, m:m + 1], col(a["L0_ffn_b1"][l, lo:lo + HT[m]]), "w_f0")
                load(wspin[:, :], a["L1_attn_W_spinT"], "w_a1")
                load(bspin_col[:, :], col(a["L1_attn_b_spin"]), "w_a1")
                load(bspin_row[:, :], rows(a["L1_attn_b_spin"]), "w_a1")
                load(wglob[:, :], a["L1_attn_W_globalT"], "w_a1")
                load(wj[:, :], a["L1_attn_W_JT"], "w_a1")
                load(beta[:, :], rows(a["L1_attn_beta"]), "w_a1")
                load(wgate[:, :], a["L1_ffn_gate_w"], "w_m1")
                load(erank[:, :, :], spread(a["c_erank"].rearrange("(a b) e -> a b e", a=1), 0, P), "w_m1")

            load(ident[:, :], a["c_ident"], "w_base")
            load_context(0)
            load(x[:, :, :], a["x"].rearrange("b s d -> s b d"), "x_loaded")
            cross_weights(0)
            load(mask_u8[:, :], a["mask"].rearrange("(p f) -> p f", p=P), "mask_loaded")
            sp.wait_ge(sem("row_init_ready"), 2)
            rows_under((0, 1))

            for l in range(2):
                n0 = B * l
                if l:
                    sp.wait_ge(sem("q_part2_ready"), 2)
                    rows_under((1,))
                store_queries(l)
                if l == 0:
                    store_first_keys(0, 0)
                stack_queries(l, 0)
                if l == 0:
                    store_first_keys(1, 0)
                    store_first_keys(2, 0)
                stack_queries(l, 1)
                if l:
                    sp.wait_ge(sem("rows_stacked"), 32)
                if l == 0:
                    stack_first_keys(0)
                    for i in range(3):
                        store_first_keys(i, 1)
                    stack_first_keys(1)
                with sp.Fori(0, B - 1) as b:
                    sp.wait_ge(sem("ctxT_psum"), b * 2 + (2 * n0 + 2))
                    load_context(b + 1)
                    nxt_parity = sp.snap((b + 1) % 2)
                    if l:
                        sp.wait_ge(sem("k_part0_ready"), b * 2 + (2 * n0 + 4))
                        stack_mask(b + 1, nxt_parity)
                    stack_keys(b + (n0 + 1), nxt_parity)
                if l == 0:
                    sp.wait_ge(sem("ctxT_psum"), 2 * B)
                    load_context(0)
                    sp.wait_ge(sem("mask_bias_ready"), 1)
                    sp.dma_start(m_dram.rearrange("b (p f) -> (b p) f", p=P // B), mask_bias[:, :])\
                      .then_inc(sem("mask_stored"), 16)
                    weights_after()
                    sp.wait_ge(sem("k_part0_ready"), 2 * B + 2)
                    sp.wait_ge(sem("mask_stored"), 16)
                    stack_mask(0, 0)
                    stack_keys(B, 0)

            sp.wait_ge(sem("v_psum"), 4 * B)
            load(gate_up[:, 0, :, :], a["L1_ffn_rt_gate"].rearrange("e k n -> k e n"), "w_e")
            load(gate_up[:, 1, :, :], a["L1_ffn_rt_up"].rearrange("e k n -> k e n"), "w_e")
            load(down[:, :, :, :], a["L1_ffn_rt_down"].rearrange("e (t k) n -> k e t n", k=P), "w_e")
            load(sh_gate_up[:, 0, :], a["L1_ffn_sh_gate"], "w_e")
            load(sh_gate_up[:, 1, :], a["L1_ffn_sh_up"], "w_e")
            load(sh_down[:, :, :], a["L1_ffn_sh_down"].rearrange("(t k) n -> k t n", k=P), "w_e")

            sp.wait_ge(sem("out_ready"), 1)
            sp.dma_start(out.rearrange("b s d -> s b d"), xn2[:, :, :]).then_inc(sem("out_stored"), 16)
            sp.wait_ge(sem("out_stored"), 16)

        @block.tensor
        def _(pe):
            def transposes(src, bank, ready, count, name):
                pe.wait_ge(sem(ready), count)
                for b in range(B):
                    last = pe.transpose(ps[:, bank, b * P:(b + 1) * P], src[:, b, :], ident[:, :])
                last.then_inc(sem(name), 1)

            def free_pair(prev):
                for kind, value in prev[-2]:
                    pe.wait_ge(sem(FREED_BY[kind]), value)
                return 2 * (len(prev) % 2)

            def transpose_context(n, prev):
                for u in range(2):
                    bank = free_pair(prev)
                    if u == 0:
                        pe.wait_ge(sem("ctx_in_ready"), n * 32 + 32)
                    for t in range(8):
                        last = pe.transpose(ps[:, bank + t // 4, (t % 4) * P:(t % 4 + 1) * P],
                                            ctx_in[:, 8 * u + t, :], ident[:, :])
                    last.then_inc(sem("ctxT_psum"), 1)
                    prev.append([("T", n * 2 + (u + 1))])

            def project_keys(l, n, prev):
                for u in range(2):
                    bank = free_pair(prev)
                    pe.wait_ge(sem("ctxT_ready"), n * 2 + (u + 1))
                    for c in range(2):
                        lo = (2 * u + c) * BANK
                        last = pe.matmul(ps[:, bank + c, :], wx[l]["k"][:, :], ctxT[:, lo:lo + BANK],
                                         start=True, stop=True)
                    last.then_inc(sem("k_psum"), 1)
                    prev.append([("K", n * 2 + (u + 1))])

            def project_values(l, n, prev, halves=(0, 1)):
                for u in halves:
                    bank = free_pair(prev)
                    for t in range(8):
                        tile = 8 * u + t
                        last = pe.matmul(ps[:, bank + t // 4, (t % 4) * P:(t % 4 + 1) * P],
                                         ctxT[:, tile * P:(tile + 1) * P], wx[l]["v"][:, :], start=True, stop=True)
                    last.then_inc(sem("v_psum"), 1)
                    prev.append([("V", n * 2 + (u + 1))])

            def max_chunk(n, b, parity, j, c, prev, first=False):
                i, k = c // 4, c % 4
                if c % 2 == 0:
                    free_pair(prev)
                bank = 2 * (len(prev) % 2) + c % 2
                if j == 0 and c == 0 and not first:
                    pe.wait_ge(sem("kstack_ready"), n * 96 + 96)
                pair, half = 2 * j + i // 2, i % 2
                last = pe.matmul(ps[:, bank, :], qstack[0:KROWS_MAX, pair, half, b, :],
                                 kstack[0:KROWS_MAX, parity, pair, k * BANK:(k + 1) * BANK], start=True, stop=True)
                if c % 2:
                    last.then_inc(sem("max_psum"), 1)
                    prev.append([("M", n * 32 + (8 * j + c // 2 + 1))])

            def max_rows(n, j, first=False):
                pe.wait_ge(sem("neg_split_ready"), n * 4 + (j + 1))
                if first:
                    pe.wait_ge(sem("consts_ready"), 1)
                for i in range(4):
                    last = pe.matmul(ps[MASK_ROW:KROWS_EXP, XB, i * P:(i + 1) * P], neg_split[:, i, :], ident_bf[:, :],
                                     start=True, stop=True)
                last.then_inc(sem("max_rows_psum"), 1)

            def weigh(n, s):
                j, t = s // TILES, s % TILES
                pe.wait_ge(sem("exp_ready"), n * 64 + (s + 1))
                if t == 0 and j >= 1:
                    pe.wait_ge(sem("sums_ready"), n * 4 + j)
                for i in range(4):
                    last = pe.matmul(ps[32 * i:32 * i + VW, OB, 0:P], vones[:, t, 4 * j + i, :],
                                     probs[:, s % 4, i, :], start=(t == 0), stop=(t == TILES - 1))
                last.then_inc(sem("probs_used"), 1)

            def transpose_sums(n, j):
                pe.wait_ge(sem("sums_ready"), n * 4 + (j + 1))
                pe.transpose(ps[:, XB, 0:P], sums[:, :], ident[:, :]).then_inc(sem("sumsT_psum"), 1)

            def second_pass(l, n, b, parity, nxt, prev):
                g = AHEAD
                for s in range(SLOTS):
                    j, t = s // TILES, s % TILES
                    if t == 0:
                        pe.wait_ge(sem("max_rows_ready"), n * 4 + (j + 1))
                    if s >= 2:
                        pe.wait_ge(sem("exp_ready"), n * 64 + (s - 1))
                    for p in range(2):
                        pair = 2 * j + p
                        last = pe.matmul(ps[:, E0 + s % 2, p * 2 * P:(p + 1) * 2 * P],
                                         kstack[0:KROWS_EXP, parity, pair, t * P:(t + 1) * P],
                                         qstack[0:KROWS_EXP, pair, :, b, :], start=True, stop=True)
                    last.then_inc(sem("scores_psum"), 1)
                    for _ in range(MAX_PLAN[s]):
                        if g < SLOTS:
                            max_chunk(n, b, parity, g // 16, g % 16, prev)
                        elif nxt is not None and g < SLOTS + AHEAD:
                            if l and g == SLOTS:
                                pe.wait_ge(sem("mask_stacked"), b * 16 + 32)
                            max_chunk(*nxt, g // 16 - QUADS, g % 16, prev)
                        g += 1
                    if s == 1:
                        pe.wait_ge(sem("v_ready"), n * 2 + 2)
                    if s >= 1:
                        weigh(n, s - 1)
                    if t == 3 and j >= 1:
                        transpose_sums(n, j - 1)
                    if t == MAX_ROWS_AT:
                        if j < QUADS - 1:
                            max_rows(n, j + 1)
                        elif nxt is not None:
                            max_rows(nxt[0], 0)

            def end_pass(l, n, nxt, prev):
                if nxt is not None:
                    project_values(l, nxt[0], prev, (0,))
                weigh(n, SLOTS - 1)
                if nxt is not None:
                    project_values(l, nxt[0], prev, (1,))
                else:
                    pe.wait_ge(sem("attended"), n * 4 + (QUADS - 1))
                transpose_sums(n, QUADS - 1)

            def project_out(l):
                transposes(attn_tok, XB, "attended", 16 * (l + 1), "attnT_psum")
                pe.wait_ge(sem(f"w_o{l}"), loads[f"w_o{l}"])
                pe.wait_ge(sem("attnT_ready"), l + 1)
                for b in range(B):
                    last = pe.matmul(ps[:, OB, b * P:(b + 1) * P], xnT[:, b, :], wx[l]["o"][:, :], start=True, stop=True)
                last.then_inc(sem("xo_psum"), 1)

            def cross_attention(l):
                n0 = B * l
                prev = [[], []]
                if l == 0:
                    transpose_context(n0, prev)
                if l:
                    pe.wait_ge(sem("w_v1"), loads["w_v1"])
                    project_values(l, n0, prev)
                transposes(xn, XB, "norm_ready", nth("norm_ready", f"xattn{l}"), "normT_psum")
                pe.wait_ge(sem("normT_ready"), nth("normT_ready", f"xattn{l}"))
                pe.wait_ge(sem(f"w_q{l}"), loads[f"w_q{l}"])
                pe.matmul(ps[:, OB, :], wx[l]["q"][:, :], xnT[:, :, :].rearrange("p b q -> p (b q)"),
                          start=True, stop=True).then_inc(sem("q_psum"), 1)
                if l == 0:
                    pe.wait_ge(sem("w_k0"), loads["w_k0"])
                    project_keys(l, n0, prev)
                    pe.wait_ge(sem("w_v0"), loads["w_v0"])
                    project_values(l, n0, prev)
                    pe.wait_ge(sem("first_k_stacked"), 96)
                    pe.wait_ge(sem("qstack_cleared"), 2)
                pe.wait_ge(sem("qstack_ready"), 192 * (l + 1))
                pe.wait_ge(sem("rows_stacked"), 16 * (l + 1))
                if l:
                    pe.wait_ge(sem("mask_stacked"), 16)
                for g in range(AHEAD):
                    if l == 0 and g == 16:
                        pe.wait_ge(sem("kstack_ready"), 96)
                    max_chunk(n0, 0, 0, g // 16, g % 16, prev, first=(l == 0))
                    if g == 19:
                        max_rows(n0, 0, first=(l == 0))

                def before(n):
                    return [[("V", n * 2 + 1), ("M", n * 32 + (AHEAD // 2 - 1))],
                            [("V", n * 2 + 2), ("M", n * 32 + AHEAD // 2)]]

                with pe.Fori(0, B - 1) as b:
                    n = b + n0
                    parity, nxt_parity, nb = pe.snap(b % 2), pe.snap((b + 1) % 2), pe.snap(b + 1)
                    prev = before(n)
                    transpose_context(n + 1, prev)
                    project_keys(l, n + 1, prev)
                    nxt = (n + 1, nb, nxt_parity)
                    second_pass(l, n, b, parity, nxt, prev)
                    end_pass(l, n, nxt, prev)
                    assert len(prev) % 2 == 0
                n, b, parity = n0 + B - 1, B - 1, (B - 1) % 2
                prev = before(n)
                if l == 0:
                    pe.wait_ge(sem("w_k1"), loads["w_k1"])
                    transpose_context(n + 1, prev)
                    project_keys(1, n + 1, prev)
                second_pass(l, n, b, parity, None, prev)
                end_pass(l, n, None, prev)
                project_out(l)

            pe.wait_ge(sem("w_base"), loads["w_base"])
            cross_attention(0)
            pe_middle0(pe, transposes)
            cross_attention(1)
            pe_middle1(pe, transposes)

        @block.scalar
        def _(act):
            def copy(dst, src):
                return act.activation(dst, src, ACT.Copy)

            def context_rows(n, first=False):
                for u in range(2):
                    act.wait_ge(sem("ctxT_psum"), n * 2 + (u + 1))
                    if u == 0 and not first:
                        act.wait_ge(sem("v_psum"), n * 2)
                    copy(ctxT[:, u * 2 * BANK:(u + 1) * 2 * BANK],
                         ps[:, 2 * u:2 * u + 2, :].rearrange("p a c -> p (a c)")).then_inc(sem("ctxT_ready"), 1)

            def keys_high(l, n, first=False):
                for u in range(2):
                    act.wait_ge(sem("k_psum"), n * 2 + (u + 1))
                    if u == 0 and not first:
                        act.wait_ge(sem("k_stored"), n * 48)
                    act.activation(k_part[0][:, u * 2 * BANK:(u + 1) * 2 * BANK],
                                   ps[:, 2 * u:2 * u + 2, :].rearrange("p a c -> p (a c)"),
                                   ACT.Identity, bias=bx[l]["k"][:, :]).then_inc(sem("k_part0_ready"), 1)

            def keys_mid(n, c):
                act.wait_ge(sem("k_rest_ready"), n * 2 + (c // 2 + 1))
                cols = slice(c * BANK, (c + 1) * BANK)
                copy(k_part[1][:, cols], k_rest[:, cols]).then_inc(sem("k_part1_ready"), 1)

            def take_max_rows(n, b, j):
                act.wait_ge(sem("max_rows_psum"), n * 4 + (j + 1))
                for p in range(2):
                    last = copy(qstack[MASK_ROW:KROWS_EXP, 2 * j + p, :, b, :],
                                ps[MASK_ROW:KROWS_EXP, XB, p * 2 * P:(p + 1) * 2 * P]
                                .rearrange("r (h q) -> r h q", h=2))
                last.then_inc(sem("max_rows_ready"), 1)

            def take_sums(n, j):
                act.wait_ge(sem("probs_used"), n * 64 + 16 * (j + 1))
                copy(sums[:, :], ps[:, OB, 0:P]).then_inc(sem("sums_ready"), 1)

            def second_pass(n, b, nxt, nxt_keys):
                for s in range(SLOTS):
                    j, t = s // TILES, s % TILES
                    act.wait_ge(sem("scores_psum"), n * 64 + (s + 1))
                    if s >= 4:
                        act.wait_ge(sem("probs_used"), n * 64 + (s - 3))
                    act.activation(probs[:, s % 4, :, :], ps[:, E0 + s % 2, :]
                                   .rearrange("p (i q) -> p i q", i=4), ACT.Exp, scale=HD ** -0.5)\
                       .then_inc(sem("exp_ready"), 1)
                    if t == 0 and j >= 1:
                        take_sums(n, j - 1)
                    if t == MAX_ROWS_AT:
                        if j < QUADS - 1:
                            take_max_rows(n, b, j + 1)
                        elif nxt is not None:
                            take_max_rows(*nxt, 0)
                    if nxt_keys is not None and s in KEYS_MID_AT:
                        keys_mid(nxt_keys, KEYS_MID_AT.index(s))
                take_sums(n, QUADS - 1)

            def norm_rows(tag):
                act.wait_ge(sem("normT_psum"), nth("normT_psum", tag))
                copy(xnT[:, :, :], ps[:, XB, :].rearrange("p (b q) -> p b q", b=B)).then_inc(sem("normT_ready"), 1)

            def cross_attention(l):
                n0 = B * l
                if l == 0:
                    context_rows(n0, first=True)
                norm_rows(f"xattn{l}")
                if l == 0:
                    act.wait_ge(sem("w_k0"), loads["w_k0"])
                    keys_high(l, n0, first=True)
                    for c in range(CHUNKS):
                        keys_mid(n0, c)
                take_max_rows(n0, 0, 0)
                with act.Fori(0, B - 1) as b:
                    n, nb = b + n0, act.snap(b + 1)
                    context_rows(n + 1)
                    keys_high(l, n + 1)
                    second_pass(n, b, (n + 1, nb), n + 1)
                n, b = n0 + B - 1, B - 1
                if l == 0:
                    context_rows(n + 1)
                    act.wait_ge(sem("w_k1"), loads["w_k1"])
                    keys_high(1, n + 1)
                second_pass(n, b, None, n + 1 if l == 0 else None)
                act.wait_ge(sem("attnT_psum"), l + 1)
                copy(xnT[:, :, :], ps[:, XB, :].rearrange("p (b q) -> p b q", b=B)).then_inc(sem("attnT_ready"), 1)

            act.wait_ge(sem("psum_cleared"), 1)
            cross_attention(0)
            act_middle0(act, copy)
            cross_attention(1)
            act_middle1(act, copy)

        @block.vector
        def _(dve):
            chain = [0]

            def link(ins):
                chain[0] += 1
                ins.then_inc(sem("dve_chain"), 1)
                dve.wait_ge(sem("dve_chain"), chain[0])

            def norm(src, dst, tag, link=link):
                for b in range(B):
                    last = dve.bn_stats(stats[:, b, :], src[:, b, :])
                link(last)
                for b in range(B):
                    last = dve.bn_aggr(meanvar[:, b, :], stats[:, b, :])
                link(last)
                dve.tensor_scalar(veps[:, :], meanvar[:, :, 1], 1e-5, None, ALU.add)\
                   .then_inc(sem("norm_var"), 1)
                dve.wait_ge(sem("norm_rstd"), nth("norm_rstd", tag))
                for b in range(B):
                    last = dve.tensor_scalar(dst[:, b, :], src[:, b, :], meanvar[:, b, 0:1], rstd[:, b:b + 1],
                                             ALU.subtract, ALU.mult)
                return last

            def values(l, n):
                for u in range(2):
                    dve.wait_ge(sem("v_psum"), n * 2 + (u + 1))
                    for c in range(2):
                        bias = spread(bx[l]["v"][:, :].rearrange("p (a n) -> p a n", a=1), 1, 4)
                        last = dve.tensor_tensor(
                            vones[:, 8 * u + 4 * c:8 * u + 4 * c + 4, :, 0:HD],
                            ps[:, 2 * u + c, :].rearrange("p (t h d) -> p t h d", t=4, h=H),
                            bias.rearrange("p t (h d) -> p t h d", h=H), ALU.add)
                    last.then_inc(sem("v_ready"), 1)

            def keys_rest(l, n, first=False):
                for u in range(2):
                    dve.wait_ge(sem("k_part0_ready"), n * 2 + (u + 1))
                    if u == 0 and not first:
                        dve.wait_ge(sem("k_part2_ready"), n)
                    cols = slice(u * 2 * BANK, (u + 1) * 2 * BANK)
                    dve.scalar_tensor_tensor(k_rest[:, cols], ps[:, 2 * u:2 * u + 2, :].rearrange("p a c -> p (a c)"),
                                             bx[l]["k"][:, :], k_part[0][:, cols], ALU.add, ALU.subtract)\
                       .then_inc(sem("k_rest_ready"), 1)

            def take_max(n, j, m):
                dve.wait_ge(sem("max_psum"), n * 32 + (8 * j + m + 1))
                bank = 2 * (m % 2)
                dve.reduce_max(max_part[:, m // 2, m % 2:m % 2 + 1],
                               ps[:, bank:bank + 2, :].rearrange("p a c -> p (a c)"), axis=AX.X)\
                   .then_inc(sem("max_taken"), 1)

            def split_max(n, j, link, first=False):
                dve.wait_ge(sem("max_taken"), n * 32 + 8 * (j + 1))
                link(dve.tensor_reduce(neg_max[:, :], max_part[:, :, :], AX.X, ALU.max, negate=True))
                if not (first and j == 0):
                    dve.wait_ge(sem("max_rows_psum"), n * 4 + j)
                link(dve.tensor_copy(neg_split[:, :, 1], neg_max[:, :]))
                link(dve.tensor_tensor(neg_rest[:, :], neg_max[:, :], neg_split[:, :, 1], ALU.subtract))
                link(dve.tensor_copy(neg_split[:, :, 2], neg_rest[:, :]))
                dve.tensor_tensor(neg_split[:, :, 3], neg_rest[:, :], neg_split[:, :, 2], ALU.subtract)\
                   .then_inc(sem("neg_split_ready"), 1)

            def attend(n, b, j, link):
                dve.wait_ge(sem("sumsT_psum"), n * 4 + (j + 1))
                sumsT = ps[:, XB, 0:P].rearrange("p (i w) -> p i w", i=4)
                link(dve.reciprocal(rden[:, :], sumsT[:, :, HD]))
                dst = attn_tok[:, b, 4 * HD * j:4 * HD * (j + 1)].rearrange("p (i d) -> p i d", i=4)
                weight = spread(rden[:, :].rearrange("p (i a) -> p i a", a=1), 2, HD)
                dve.tensor_tensor(dst, sumsT[:, :, 0:HD], weight, ALU.mult).then_inc(sem("attended"), 1)

            LINKS = 4 * QUADS + QUADS

            def second_pass(n, b, n_next, link):
                for m in range(AHEAD // 2, (AHEAD + SLOTS) // 2):
                    j = m // 8
                    if m >= AHEAD // 2 + 8 and m % 8 == 6:
                        attend(n, b, j - 2, link)
                    at = (n, j) if j < QUADS else (n_next, j - QUADS) if n_next is not None else None
                    if at is not None:
                        take_max(*at, m % 8)
                        if m % 8 == 7:
                            split_max(*at, link)

            def cross_attention(l):
                n0 = B * l
                norm(x, xn, f"xattn{l}").then_inc(sem("norm_ready"), 1)
                dve.wait_ge(sem("q_psum"), l + 1)
                dve.wait_ge(sem(f"w_q{l}"), loads[f"w_q{l}"])
                link(dve.tensor_scalar(q_rest[0], ps[:, OB, :], bx[l]["q"][:, :], None, ALU.add))
                if l:
                    dve.wait_ge(sem("q_stored"), 48)
                dve.tensor_copy(q_part[0][:, :], q_rest[0]).then_inc(sem("q_part0_ready"), 1)
                dve.wait_ge(sem("q_part0_ready"), l + 1)
                link(dve.tensor_tensor(q_rest[1], q_rest[0], q_part[0][:, :], ALU.subtract))
                dve.tensor_copy(q_part[1][:, :], q_rest[1]).then_inc(sem("q_part1_ready"), 1)
                dve.wait_ge(sem("q_part1_ready"), l + 1)
                dve.tensor_tensor(q_part[2][:, :], q_rest[1], q_part[1][:, :], ALU.subtract)\
                   .then_inc(sem("q_part2_ready"), 1)
                if l == 0:
                    dve.wait_ge(sem("w_k0"), loads["w_k0"])
                    keys_rest(l, n0, first=True)
                    for u in range(2):
                        cols = slice(u * 2 * BANK, (u + 1) * 2 * BANK)
                        dve.wait_ge(sem("k_rest_ready"), u + 1)
                        dve.wait_ge(sem("k_part1_ready"), 2 * u + 2)
                        last = dve.tensor_tensor(k_part[2][:, cols], k_rest[:, cols], k_part[1][:, cols], ALU.subtract)
                    last.then_inc(sem("k_part2_ready"), 1)
                dve.wait_ge(sem(f"w_v{l}"), loads[f"w_v{l}"])
                values(l, n0)
                for m in range(AHEAD // 2):
                    take_max(n0, m // 8, m % 8)
                    if m == 7:
                        split_max(n0, 0, link, first=(l == 0))
                start = chain[0]
                if l == 0:
                    dve.wait_ge(sem("mask_loaded"), loads["mask_loaded"])
                    dve.tensor_scalar(mask_bias[:, :], mask_u8[:, :], 1.0, -MASKED, ALU.subtract, ALU.mult)\
                       .then_inc(sem("mask_bias_ready"), 1)
                with dve.Fori(0, B - 1) as b:
                    within = [0]

                    def link_b(ins):
                        within[0] += 1
                        ins.then_inc(sem("dve_chain"), 1)
                        dve.wait_ge(sem("dve_chain"), b * LINKS + (start + within[0]))

                    keys_rest(l, b + (n0 + 1))
                    second_pass(b + n0, b, b + (n0 + 1), link_b)
                    values(l, b + (n0 + 1))
                    attend(b + n0, b, QUADS - 1, link_b)
                    assert within[0] == LINKS, within
                chain[0] += (B - 1) * LINKS
                if l == 0:
                    dve.wait_ge(sem("w_k1"), loads["w_k1"])
                    keys_rest(1, n0 + B)
                second_pass(n0 + B - 1, B - 1, None, link)
                attend(n0 + B - 1, B - 1, QUADS - 1, link)
                dve.wait_ge(sem(f"w_o{l}"), loads[f"w_o{l}"])
                dve.wait_ge(sem("xo_psum"), l + 1)
                bias = spread(bx[l]["o"][:, :].rearrange("p (a n) -> p a n", a=1), 1, B)
                link(dve.tensor_tensor(ytmp[:, :, :], ps[:, OB, :].rearrange("p (b d) -> p b d", b=B), bias, ALU.add))
                dve.tensor_tensor(x[:, :, :], x[:, :, :], ytmp[:, :, :], ALU.add).then_inc(sem(f"x_attended{l}"), 1)
                dve.wait_ge(sem(f"x_attended{l}"), 1)

            dve.memset(ps[:, OB, :], 0.0).then_inc(sem("psum_cleared"), 1)
            dve.memset(neg_split[:, :, 0], 1.0)
            dve.memset(vones[:, :, :, HD], 1.0)
            dve.wait_ge(sem("w_base"), loads["w_base"])
            dve.tensor_copy(ident_bf[:, :], ident[:, :]).then_inc(sem("consts_ready"), 1)
            dve.memset(hT[:, :, :], 0.0)
            dve.wait_ge(sem("x_loaded"), 16)
            cross_attention(0)
            dve_middle0(dve, link, norm)
            cross_attention(1)
            dve_middle1(dve, link, norm)

        @block.gpsimd
        def _(pool):
            def alone(ins, name, count):
                ins.then_inc(sem(name), 1)
                pool.wait_ge(sem(name), count)

            def rstd_of(tag):
                pool.wait_ge(sem("norm_var"), nth("norm_var", tag))
                alone(pool.tensor_tensor(rstd[:, :], veps[:, :], half_neg[:, :], ALU.pow),
                      "norm_rstd", nth("norm_rstd", tag))

            def split_keys(n):
                pool.wait_ge(sem("k_stored"), n * 48)
                pool.wait_ge(sem("k_part1_ready"), n * 4 + 4)
                alone(pool.tensor_tensor(k_part[2][:, :], k_rest[:, :], k_part[1][:, :], ALU.subtract),
                      "k_part2_ready", n + 1)

            def cross_attention(l):
                if l:
                    rstd_of("xattn1")
                with pool.Fori(0, B - 1) as b:
                    split_keys(b + (B * l + 1))
                if l == 0:
                    split_keys(B)

            alone(pool.memset(row_init[MASK_ROW:KROWS_EXP, :], 1.0), "row_init_ready", 1)
            alone(pool.memset(row_init[MASK_ROW:MASK_ROW + 1, :], 0.0), "row_init_ready", 2)
            alone(pool.memset(half_neg[:, :], -0.5), "half_ready", 1)
            stacked = [qstack[rows, :, :, :, :].rearrange("p j e b q -> p (j e b q)").bitcast(mybir.dt.uint32)
                       for rows in (slice(0, P), slice(MASK_ROW, MASK_ROW + 1))]
            alone(pool.memset(stacked[0], 0), "qstack_cleared", 1)
            rstd_of("xattn0")
            alone(pool.memset(stacked[1], 0x3F803F80), "qstack_cleared", 2)
            cross_attention(0)
            pool_middle0(pool, rstd_of, alone)
            cross_attention(1)
            pool_middle1(pool, rstd_of)

        return nc


_TRANSPOSED = ("L0_attn_qkv_w", "L0_attn_out_w", "L1_attn_W_spin", "L1_attn_W_global", "L1_attn_W_J")


def _constants(np):
    tok = np.arange(P)
    half = np.arange(0, FD, 2, dtype=np.float32)
    inv_freq = np.float32(1.0) / np.float32(10000.0) ** (half / np.float32(FD))
    freqs = tok.astype(np.float32)[:, None] * inv_freq[None, :]
    base = (half + np.float32(0.4 * FD)) / np.float32(1.4 * FD)
    power = (tok - P // 2).astype(np.float32) / np.float32(32.0)
    scale = (base[None, :] ** power[:, None]).astype(np.float32)
    cos, sin = np.cos(freqs), np.sin(freqs)
    both = lambda u, v: np.concatenate([u, v], axis=1)
    rot = np.stack([both(cos * scale, cos * scale), both(-sin * scale, sin * scale),
                    both(cos / scale, cos / scale), both(-sin / scale, sin / scale)], axis=1)
    q, k = tok[:, None], tok[None, :]
    return {
        "c_ident": np.eye(P, dtype=np.float32),
        "c_band": np.where((q < k) | (q > k + 64), MASKED, 0.0).astype(np.float32),
        "c_shift": (q + 1 == k).astype(np.float32),
        "c_headmask": (tok[:, None] // HD == np.arange(H)[None, :]).astype(np.float32),
        "c_rot": rot.astype(np.float32),
        "c_erank": np.tile(np.arange(E, 0, -1, dtype=np.float32), (B, 1)),
    }


def kernel(**inputs):
    import numpy as np
    import concourse.bacc as bacc
    from concourse.bass_utils import run_bass_kernel_spmd

    nc = bacc.Bacc("TRN2", target_bir_lowering=False, num_devices=1)
    host = {}
    for name, value in inputs.items():
        v = np.asarray(value)
        if name == "ctx_1024":
            name = "ctx"
        if name == "mask_BxS2_bk1":
            name, v = "mask", v.reshape(-1)
        if name in _TRANSPOSED:
            name, v = name + "T", v.T
        host[name] = np.ascontiguousarray(v)
    host.update(_constants(np))
    arrays, aps = {}, {}
    for name, v in host.items():
        arrays[f"in_{name}"] = v
        aps[name] = nc.dram_tensor(f"in_{name}", v.shape, mybir.dt.from_np(v.dtype), kind="ExternalInput").ap()
    out = nc.dram_tensor("out_0", (B, P, D), F32, kind="ExternalOutput").ap()
    perceiver(nc, aps, out)
    result = run_bass_kernel_spmd(nc, [arrays], core_ids=[0])
    return result.results[0]["out_0"]
```

```python
import concourse.bass as bass
from concourse import mybir
from contextlib import ExitStack

F32 = mybir.dt.float32
BF16 = mybir.dt.bfloat16
U8 = mybir.dt.uint8
ALU = mybir.AluOpType
ACT = mybir.ActivationFunctionType
AX = mybir.AxisListType

P = 128
B = 4
D = 128
H = 16
HD = D // H
CTX = 2048
TILES = CTX // P
PAIRS = H // 2
QUADS = H // 4
BANK = 512
CHUNKS = CTX // BANK
VW = HD + 1
STACK = 6 * HD
PART_K = (0, 0, 0, 1, 1, 2)
PART_Q = (0, 1, 2, 0, 1, 0)
MASK_ROW = 2 * STACK
KROWS_MAX = MASK_ROW + 1
KROWS_EXP = MASK_ROW + 4
KEEP = {"start": 6, "local": 24, "gated": 22, "spins": 8, "experts": 26}
MASKED = -1.0e25
SLOTS = QUADS * TILES
AHEAD = 20
MAX_PLAN = [0, 0, 0] + [2 if t in (3, 4, 6) else 1 for t in range(3, SLOTS)]
KEYS_MID_AT = (2, 4, 5, 7)
MAX_ROWS_AT = 14

FH = 8
FD = 64
INNER = FH * FD
HID = 341
HT = (128, 128, 85)
E = 8
EI = 256


def spread(ap, axis, n):
    shape = list(ap.shape)
    assert shape[axis] == 1
    shape[axis] = n
    return ap.broadcast_to(shape)


def perceiver(nc, a, out):
    ctx = ExitStack()
    with ctx:
        def sb(name, shape, dt=F32):
            return ctx.enter_context(nc.sbuf_tensor(name, shape, dt))

        sems, loads = {}, {}

        def sem(name):
            if name not in sems:
                sems[name] = ctx.enter_context(nc.semaphore(name))
            return sems[name]

        NORMS = ("xattn0", "a0", "a1", "f0", "g0", "g1", "xattn1", "s1", "m1")
        APART = {"norm_ready": ("f0",), "normT_psum": ("a0", "f0"), "normT_ready": ("a0", "f0")}

        def nth(signal, tag):
            return [t for t in NORMS if t not in APART.get(signal, ())].index(tag) + 1

        x = sb("x", [P, B, D])
        ident = sb("ident", [P, P])
        ident_bf = sb("ident_bf", [P, P], BF16)
        ctx_in = sb("ctx_in", [P, TILES, D])
        ctxT = sb("ctxT", [P, CTX])
        k_part = [sb(f"k_part{i}", [P, CTX], BF16) for i in range(3)]
        k_rest = sb("k_rest", [P, CTX])
        kstack = sb("kstack", [P, 2, PAIRS, CTX], BF16)
        vones = sb("vones", [P, TILES, H, VW])
        qstack = sb("qstack", [P, PAIRS, 2, B, P], BF16)
        q_part = [sb(f"q_part{i}", [P, B * P], BF16) for i in range(3)]
        row_init = sb("row_init", [P, BANK], BF16)
        probs = sb("probs", [P, 4, 4, P])
        sums = sb("sums", [P, P])
        attn_tok = sb("attn_tok", [P, B, D])
        max_part = sb("max_part", [P, 4, 2])
        neg_max = sb("neg_max", [P, 4])
        neg_rest = sb("neg_rest", [P, 4])
        neg_split = sb("neg_split", [P, 4, 4], BF16)
        rden = sb("rden", [P, 4])
        wx = [{n: sb(f"wx{l}_{n}", [P, D]) for n in ("q", "k", "v", "o")} for l in range(2)]
        bx = [{"q": sb(f"bx{l}_q", [P, 1]), "k": sb(f"bx{l}_k", [P, 1]),
               "v": sb(f"bx{l}_v", [P, D]), "o": sb(f"bx{l}_o", [P, D])} for l in range(2)]
        wqkv0 = sb("wqkv0", [P, 3 * D])
        bqkv0 = sb("bqkv0", [P, 3 * D])
        wout0 = sb("wout0", [P, D])
        bout0 = sb("bout0", [P, D])
        lnw0 = sb("lnw0", [P, 1])
        lnb0 = sb("lnb0", [P, 1])
        headmask = sb("headmask", [P, H])
        wqkvf = sb("wqkvf", [P, 2, 3 * INNER])
        wof = sb("wof", [P, 2, 4, D])
        w1f = sb("w1f", [P, 2, 2 * HID])
        w2f = sb("w2f", [P, 2, 3, D])
        lgf = sb("lgf", [P, 2])
        lbf = sb("lbf", [P, 2])
        b1f = sb("b1f", [P, 2, 2, 3])
        b2f = sb("b2f", [P, 2, D])
        rot = sb("rot", [P, 4, FD])
        rot_scale = sb("rot_scale", [P, 2, 4, FD])
        rotl = sb("rotl", [P, 2, 4, FD])
        band = sb("band", [P, P])
        band_bf = sb("band_bf", [P, P], BF16)
        shift = sb("shift", [P, P])
        wspin = sb("wspin", [P, D])
        bspin_col = sb("bspin_col", [P, 1])
        bspin_row = sb("bspin_row", [P, D])
        wglob = sb("wglob", [P, D])
        wj = sb("wj", [P, D])
        beta = sb("beta", [P, 1])
        wgate = sb("wgate", [P, E])
        erank = sb("erank", [P, B, E])
        mask_u8 = sb("mask_u8", [P, B * CTX // P], U8)
        mask_bias = sb("mask_bias", [P, B * CTX // P], BF16)
        hT = sb("hT", [P, B, P])
        half_neg = sb("half_neg", [P, B])
        stats = sb("stats", [P, B, 6])
        meanvar = sb("meanvar", [P, B, 2])
        veps = sb("veps", [P, B])
        rstd = sb("rstd", [P, B])
        xn = sb("xn", [P, B, D])
        xn2 = sb("xn2", [P, B, D])
        xnT = sb("xnT", [P, B, P])
        xres = sb("xres", [P, B, D])
        ytmp = sb("ytmp", [P, B, D])
        y = sb("y", [P, B, D])

        q_rest = [t[:, :, :].rearrange("p b d -> p (b d)") for t in (ytmp, xres)]

        scratch = kstack[:, :, :, :].rearrange("p a b c -> p (a b c)").bitcast(F32)
        HALF = PAIRS * CTX // 2
        scratch_at = [HALF]

        def carve(*shape):
            n = 1
            for s in shape:
                n *= s
            lo = scratch_at[0]
            scratch_at[0] += n
            assert scratch_at[0] <= PAIRS * CTX
            v = scratch[:, lo:lo + n]
            if len(shape) == 2:
                v = v.rearrange("p (a b) -> p a b", a=shape[0])
            return v

        ps = ctx.enter_context(nc.psum_tensor("ps", [P, 8, BANK], F32))
        E0, OB, XB = 4, 6, 7

        k_dram = nc.dram_tensor("k_dram", (3, P, CTX), BF16, kind="Internal").ap()
        m_dram = nc.dram_tensor("m_dram", (B, CTX), BF16, kind="Internal").ap()
        q_dram = nc.dram_tensor("q_dram", (3, P, B * P), BF16, kind="Internal").ap()

        block = ctx.enter_context(nc.Block())

        def flat(ap):
            return ap.rearrange("p b q -> p (b q)")

        a_qkv = carve(B, 3 * D)
        a_sq = carve(B, 2 * D)
        a_ss = sb("a_ss", [P, B, 2 * H])
        a_norm = sb("a_norm", [P, B, 2 * H])
        a_inv = sb("a_inv", [P, B, 2 * H])
        a_qk = carve(B, 2 * D)
        a_qkT = a_sq
        a_qblk = [carve(H, P) for _ in range(2)]
        idle = probs[:, :, :, :].rearrange("p a b c -> p (a b c)")
        a_probs = [idle[:, i * 8 * P:(i + 1) * 8 * P].rearrange("p (a b) -> p a b", a=8) for i in range(2)]
        a_v = k_rest[:, 0:B * H * VW].rearrange("p (b h w) -> p b h w", b=B, h=H)
        a_sums = k_rest[:, B * H * VW:B * H * VW + 4 * P].rearrange("p (a b) -> p a b", a=4)
        a_rden = sb("a_rden", [P, H])
        scratch_at[0] = HALF
        f_sq = [idle[:, i * 2 * INNER:(i + 1) * 2 * INNER] for i in range(2)]
        f_cos = [carve(2 * INNER) for _ in range(2)]
        f_sin = [carve(2 * INNER) for _ in range(2)]
        f_qk = [carve(2 * INNER) for _ in range(B)]
        f_v = [k_rest[:, i * INNER:(i + 1) * INNER] for i in range(B)]
        part_space = [t[:, :].bitcast(F32) for t in k_part]
        f_qkT = [ctx_in[:, 8 * b:8 * b + 8, :] for b in range(2)] + \
                [part_space[i].rearrange("p (t q) -> p t q", t=8) for i in range(2)]
        f_oT = [part_space[2][:, i * INNER:(i + 1) * INNER].rearrange("p (t q) -> p t q", t=4) for i in range(2)]
        f_probs = [t.rearrange("p (h k) -> p h k", h=FH) for t in f_sq]
        f_probsT = [t.rearrange("p (h k) -> p h k", h=FH) for t in f_sin]
        f_gelu = [f_cos[0][:, 0:512], f_cos[0][:, 512:1024], f_cos[1][:, 512:1024]]
        f_act = f_qk[0].rearrange("p (a n) -> p a n", a=2), f_qk[1].rearrange("p (a n) -> p a n", a=2)
        f_act = [f_act[0][:, 0, :], f_act[0][:, 1, :], f_act[1][:, 0, :]]
        f_shift = f_cos[1][:, 0:512].rearrange("p (b d) -> p b d", b=B)
        f_ss = sb("f_ss", [P, B, 16])
        f_norm = sb("f_norm", [P, B, 16])
        f_inv = sb("f_inv", [P, B, 16])
        f_qs = sb("f_qs", [P, B, FH])
        f_max = sb("f_max", [P, 2, FH])
        f_bias = sb("f_bias", [P, 2, FH])
        f_den = sb("f_den", [P, 2, FH])
        f_rden = sb("f_rden", [P, FH])
        expert_at = [0]
        for width in (2 * E * EI, E * EI // P * D, 2 * EI, EI // P * D):
            expert_at.append(expert_at[-1] + width)
        gate_up = scratch[:, expert_at[0]:expert_at[1]].rearrange("p (a e n) -> p a e n", a=2, e=E)
        down = scratch[:, expert_at[1]:expert_at[2]].rearrange("p (e t n) -> p e t n", e=E, t=2)
        sh_gate_up = scratch[:, expert_at[2]:expert_at[3]].rearrange("p (a n) -> p a n", a=2)
        sh_down = scratch[:, expert_at[3]:expert_at[4]].rearrange("p (a n) -> p a n", a=2)
        scratch_at[0] = HALF
        s_T = carve(B, P)
        s_tok = carve(B, D)
        s_eT = carve(B, P)
        s_probs = carve(B, P)
        s_probsT = carve(B, P)
        s_meanrows = carve(B, P)
        m_xs = carve(B, D)
        m_xsT = carve(B, P)
        m_xe = [carve(B, P) for _ in range(2)]
        m_silu = [carve(B * P) for _ in range(3)]
        m_act = [carve(B, P) for _ in range(3)]
        s_mean = sb("s_mean", [P, B])
        s_max = sb("s_max", [P, B])
        s_bias = sb("s_bias", [P, B])
        s_den = sb("s_den", [P, B])
        s_rden = sb("s_rden", [P, B])
        m_logit = sb("m_logit", [P, B, E])
        m_top = sb("m_top", [P, B])
        m_tanh = sb("m_tanh", [P, B])
        m_score = sb("m_score", [P, B])
        m_rank = sb("m_rank", [P, B, E])
        m_first = sb("m_first", [P, B])
        m_eq = sb("m_eq", [P, B, E])
        m_hot = sb("m_hot", [P, B, E], BF16)
        MU = 2 * E + 2

        def unit_expert(k):
            return E if k < 2 else (k - 2) // 2

        def unit_weights(k):
            e, half = unit_expert(k), k % 2
            cols = slice(half * P, (half + 1) * P)
            if e < E:
                return gate_up[:, 0, e, cols], gate_up[:, 1, e, cols], down[:, e, half, :]
            return sh_gate_up[:, 0, cols], sh_gate_up[:, 1, cols], sh_down[:, half, :]

        def pe_self_attention(pe, transposes):
            transposes(xn2, XB, "norm_ready", nth("norm_ready", "a1"), "normT_psum")
            pe.wait_ge(sem("w_a0"), loads["w_a0"])
            pe.wait_ge(sem("normT_ready"), nth("normT_ready", "a1"))
            pe.wait_ge(sem("v_ready"), 2 * B + 2)
            for b in range(B):
                pe.matmul(ps[:, b, 0:3 * D], xnT[:, b, :], wqkv0[:, :], start=True, stop=True)\
                  .then_inc(sem("a_qkv_psum"), 1)
            for b in range(B):
                pe.wait_ge(sem("a_qk_ready"), b + 1)
                for i in range(2):
                    last = pe.transpose(ps[:, 4 + b, i * P:(i + 1) * P], a_qk[:, b, i * D:(i + 1) * D], ident[:, :])
                last.then_inc(sem("a_qkT_psum"), 1)

            def scores(u):
                b, half = u // 2, u % 2
                pe.wait_ge(sem("a_qblk_ready"), u + 1)
                if u >= 2:
                    pe.wait_ge(sem("a_exp_ready"), u - 1)
                for c in range(2):
                    lo = 8 * half + 4 * c
                    last = pe.matmul(ps[:, 2 * (u % 2) + c, :], a_qkT[:, b, P:2 * P], flat(a_qblk[b % 2][:, lo:lo + 4, :]),
                                     start=True, stop=True)
                last.then_inc(sem("a_scores_psum"), 1)

            def weigh(u):
                b, half = u // 2, u % 2
                pe.wait_ge(sem("a_exp_ready"), u + 1)
                if half == 0:
                    pe.wait_ge(sem("a_v_ready"), b + 2)
                    if b == 0:
                        pe.wait_ge(sem("a_qkT_ready"), B)
                    if b:
                        pe.wait_ge(sem("a_sums_ready"), b)
                for i in range(8):
                    h = 8 * half + i
                    last = pe.matmul(ps[32 * (h % 4):32 * (h % 4) + VW, OB, h // 4 * P:(h // 4 + 1) * P],
                                     a_v[:, b, h, :], a_probs[u % 2][:, i, :], start=True, stop=True)
                last.then_inc(sem("a_probs_used"), 1)

            scores(0)
            scores(1)
            for u in range(2 * B):
                weigh(u)
                if u + 2 < 2 * B:
                    scores(u + 2)
                if u % 2:
                    b = u // 2
                    pe.wait_ge(sem("a_sums_ready"), b + 1)
                    if b:
                        pe.wait_ge(sem("a_attended"), b)
                    for j in range(4):
                        last = pe.transpose(ps[:, XB, j * P:(j + 1) * P], a_sums[:, j, :], ident[:, :])
                    last.then_inc(sem("a_sumsT_psum"), 1)
            transposes(attn_tok, XB, "a_attended", B, "a_attnT_psum")
            pe.wait_ge(sem("a_attnT_ready"), 1)
            for b in range(B):
                last = pe.matmul(ps[:, OB, b * P:(b + 1) * P], xnT[:, b, :], wout0[:, :], start=True, stop=True)
            last.then_inc(sem("a_out_psum"), 1)

        def pe_local_attention(pe, transposes, l):
            n = l * B
            transposes(y, XB, "f_y_ready", 2 * l + 1, "f_yT_psum")
            pe.wait_ge(sem("f_hT_ready"), l + 1)

            def project(b):
                if b >= 2:
                    pe.wait_ge(sem("f_rot_ready"), n + b - 1)
                    pe.wait_ge(sem("f_v_ready"), n + b - 1)
                for i, bank in enumerate((2 * (b % 2), 2 * (b % 2) + 1, 4 + b % 2)):
                    last = pe.matmul(ps[:, bank, :], hT[:, b, :], wqkvf[:, l, i * INNER:(i + 1) * INNER],
                                     start=True, stop=True)
                last.then_inc(sem("f_qkv_psum"), 1)

            def qk_rows(b):
                pe.wait_ge(sem("f_kn_ready"), n + b + 1)
                if b:
                    pe.wait_ge(sem("f_qkT_ready"), n + b)
                for i in range(2):
                    for t in range(4):
                        lo = i * INNER + t * P
                        last = pe.transpose(ps[:, OB + i, t * P:(t + 1) * P], f_qk[b][:, lo:lo + P], ident[:, :])
                last.then_inc(sem("f_qkT_psum"), 1)

            def scores(b):
                pe.wait_ge(sem("f_qkT_ready"), n + b + 1)
                if b < 2:
                    pe.wait_ge(sem("f_rot_ready"), n + b + 3)
                    pe.wait_ge(sem("f_v_ready"), n + b + 3)
                else:
                    pe.wait_ge(sem("f_exp_ready"), n + b - 1)
                for c in range(2):
                    bank = 2 * (b % 2) + c
                    mask = spread(band_bf[:, :].rearrange("p (a k) -> p a k", a=1), 1, 4)
                    pe.matmul(ps[:, bank, :].rearrange("p (a k) -> p a k", a=4), ident_bf[:, :], mask,
                              start=True, stop=False, skip_group_check=True)
                    rows = slice(FD * c, FD * c + FD)
                    for i in range(4):
                        last = pe.matmul(ps[:, bank, i * P:(i + 1) * P], f_qkT[b][rows, i, :], f_qkT[b][rows, 4 + i, :],
                                         start=False, stop=(i == 3), skip_group_check=True)
                last.then_inc(sem("f_scores_psum"), 1)

            def probs_rows(b):
                pe.wait_ge(sem("f_probs_ready"), n + b + 1)
                if b:
                    pe.wait_ge(sem("f_probsT_ready"), n + b)
                else:
                    pe.wait_ge(sem("f_v_ready"), n + B)
                for h in range(FH):
                    last = pe.transpose(ps[:, 4 + h // 4, h % 4 * P:(h % 4 + 1) * P], f_probs[b % 2][:, h, :], ident[:, :])
                last.then_inc(sem("f_probsT_psum"), 1)

            def weigh(b):
                pe.wait_ge(sem("f_probsT_ready"), n + b + 1)
                if b == 0:
                    pe.wait_ge(sem("f_qkT_ready"), n + B)
                for h in range(FH):
                    last = pe.matmul(ps[FD * (h % 2):FD * (h % 2) + FD, OB, h // 2 * P:(h // 2 + 1) * P],
                                     f_v[b][:, h * FD:(h + 1) * FD], f_probsT[b % 2][:, h, :], start=True, stop=True)
                last.then_inc(sem("f_o_psum"), 1)

            def output(b):
                pe.wait_ge(sem("f_oT_ready"), n + b + 1)
                for t in range(4):
                    last = pe.matmul(ps[:, XB, b * P:(b + 1) * P], f_oT[b % 2][:, t, :], wof[:, l, t, :],
                                     start=(t == 0), stop=(t == 3))
                last.then_inc(sem("f_attn_psum"), 1)

            project(0)
            project(1)
            project(2)
            project(3)
            qk_rows(0)
            qk_rows(1)
            scores(0)
            scores(1)
            qk_rows(2)
            qk_rows(3)
            for b in range(B):
                if b + 2 < B:
                    scores(b + 2)
                probs_rows(b)
                if b:
                    output(b - 1)
                weigh(b)
            output(B - 1)

        def pe_gated(pe, transposes, keep_clock, l):
            pe.wait_ge(sem("f_y_ready"), 2 * l + 2)
            pe.matmul(ps[:, 0, 0:B * 64].rearrange("p (b d) -> p b d", b=B), shift[:, :], y[:, :, 64:D],
                      start=True, stop=True).then_inc(sem("f_shift_psum"), 1)
            keep_clock(4, KEEP["gated"])
            transposes(xn, XB, "norm_ready", nth("norm_ready", f"g{l}"), "normT_psum")
            pe.wait_ge(sem("normT_ready"), nth("normT_ready", f"g{l}"))
            for m in range(3):
                for ag in (1, 0):
                    lo = ag * HID + m * P
                    pe.matmul(ps[0:HT[m], (2 + 2 * m + ag) % 6, :], w1f[:, l, lo:lo + HT[m]], flat(xnT[:, :, :]),
                              start=True, stop=True).then_inc(sem("f_gate_psum" if ag else "f_up_psum"), 1)
            for m in range(3):
                pe.wait_ge(sem("f_act_ready"), 3 * l + m + 1)
                for b in range(B):
                    last = pe.matmul(ps[:, OB, b * P:(b + 1) * P], f_act[m][0:HT[m], b * P:(b + 1) * P],
                                     w2f[0:HT[m], l, m, :], start=(m == 0 and b == 0), stop=(m == 2 and b == B - 1),
                                     skip_group_check=True)
            last.then_inc(sem("f_w2_psum"), 1)

        def pe_middle0(pe, transposes, keep_clock):
            pe_self_attention(pe, transposes)
            keep_clock(0, KEEP["local"])
            pe.wait_ge(sem("w_f0"), loads["w_f0"])
            pe.wait_ge(sem("band_ready"), 1)
            for l in range(2):
                pe_local_attention(pe, transposes, l)
                pe_gated(pe, transposes, keep_clock, l)

        def pe_middle1(pe, transposes, keep_clock):
            keep_clock(0, KEEP["spins"])
            transposes(xn, XB, "norm_ready", nth("norm_ready", "s1"), "normT_psum")
            pe.wait_ge(sem("normT_ready"), nth("normT_ready", "s1"))
            pe.wait_ge(sem("w_a1"), loads["w_a1"])
            pe.matmul(ps[:, 0, :], wspin[:, :], flat(xnT[:, :, :]), start=True, stop=True).then_inc(sem("s_T_psum"), 1)
            for b in range(B):
                last = pe.matmul(ps[:, 1, b * P:(b + 1) * P], xnT[:, b, :], wspin[:, :], start=True, stop=True)
            last.then_inc(sem("s_tok_psum"), 1)
            pe.wait_ge(sem("s_T_ready"), 1)
            pe.matmul(ps[:, 2, :], wj[:, :], flat(s_T[:, :, :]), start=True, stop=True).then_inc(sem("s_eT_psum"), 1)
            pe.wait_ge(sem("s_eT_ready"), 1)
            for b in range(B):
                last = pe.matmul(ps[:, 3, b * P:(b + 1) * P], s_eT[:, b, :], s_T[:, b, :], start=True, stop=True)
            last.then_inc(sem("s_scores_psum"), 1)
            transposes(s_probs, XB, "s_probs_ready", 1, "s_probsT_psum")
            pe.wait_ge(sem("s_probsT_ready"), 1)
            pe.wait_ge(sem("s_tok_ready"), 1)
            pe.wait_ge(sem("s_mean_ready"), 1)
            for b in range(B):
                pe.matmul(ps[:, 4, b * P:(b + 1) * P], s_probsT[:, b, :], s_tok[:, b, :], start=True, stop=False)
                last = pe.matmul(ps[:, 4, b * P:(b + 1) * P], s_meanrows[:, b, :], wglob[:, :], start=False, stop=True)
            last.then_inc(sem("s_field_psum"), 1)

            keep_clock(2, KEEP["experts"])
            transposes(xn, XB, "norm_ready", nth("norm_ready", "m1"), "normT_psum")
            pe.wait_ge(sem("normT_ready"), nth("normT_ready", "m1"))
            pe.wait_ge(sem("w_m1"), loads["w_m1"])
            for b in range(B):
                last = pe.matmul(ps[:, 0, b * E:(b + 1) * E], xnT[:, b, :], wgate[:, :], start=True, stop=True)
            last.then_inc(sem("m_logit_psum"), 1)

            def expert_mask(e):
                if e:
                    pe.wait_ge(sem("m_xe_ready"), e)
                for b in range(B):
                    hot = spread(m_hot[:, b, e:e + 1], 1, P)
                    last = pe.matmul(ps[:, 1, b * P:(b + 1) * P], hot, ident_bf[:, :], start=True, stop=True)
                last.then_inc(sem("m_mask_psum"), 1)

            def gate_and_up(k):
                e = unit_expert(k)
                if e < E and k % 2 == 0:
                    pe.wait_ge(sem("m_xe_ready"), e + 1)
                if k >= 3:
                    pe.wait_ge(sem("m_act_ready"), k - 2)
                wg, wu, _ = unit_weights(k)
                src = flat(m_xe[e % 2][:, :, :] if e < E else xnT[:, :, :])
                pe.matmul(ps[:, 2 + 2 * (k % 3), :], wg, src, start=True, stop=True)
                pe.matmul(ps[:, 3 + 2 * (k % 3), :], wu, src, start=True, stop=True).then_inc(sem("m_gu_psum"), 1)

            def project_down(k):
                pe.wait_ge(sem("m_act_ready"), k + 1)
                for b in range(B):
                    last = pe.matmul(ps[:, 0, b * P:(b + 1) * P], m_act[k % 3][:, b, :], unit_weights(k)[2],
                                     start=(k == 0 and b == 0), stop=(k == MU - 1 and b == B - 1),
                                     skip_group_check=True)
                last.then_inc(sem("m_down_psum"), 1)

            pe.wait_ge(sem("w_e"), loads["w_e"])
            gate_and_up(0)
            gate_and_up(1)
            pe.wait_ge(sem("m_hot_ready"), 1)
            expert_mask(0)
            transposes(m_xs, 6, "m_xs_ready", 1, "m_xsT_psum")
            project_down(0)
            pe.wait_ge(sem("m_xsT_ready"), 1)
            for k in range(2, MU):
                if k % 2 == 0 and unit_expert(k) + 1 < E:
                    expert_mask(unit_expert(k) + 1)
                gate_and_up(k)
                project_down(k - 1)
            project_down(MU - 1)

        def act_middle0(act, copy):
            def rows_from(bank):
                return ps[:, bank, :].rearrange("p (b q) -> p b q", b=B)

            act.wait_ge(sem("normT_psum"), nth("normT_psum", "a1"))
            act.wait_ge(sem("w_a0"), loads["w_a0"])
            act.activation(xnT[:, :, :], rows_from(XB), ACT.Identity, bias=lnb0[:, :], scale=lnw0[:, :])\
               .then_inc(sem("normT_ready"), 1)
            for s in range(B + 1):
                if s < B:
                    act.wait_ge(sem("a_qkv_ready"), s + 1)
                    act.activation(a_sq[:, s, :], a_qkv[:, s, 0:2 * D], ACT.Square).then_inc(sem("a_sq_ready"), 1)
                if s >= 1:
                    act.wait_ge(sem("a_ss_ready"), s)
                    act.activation(a_norm[:, s - 1, :], a_ss[:, s - 1, :], ACT.Sqrt).then_inc(sem("a_norm_ready"), 1)
            act.wait_ge(sem("k_part2_ready"), B + 1)
            for b in range(B):
                act.wait_ge(sem("a_qkT_psum"), b + 1)
                copy(a_qkT[:, b, :], ps[:, 4 + b, 0:2 * P]).then_inc(sem("a_qkT_ready"), 1)
            for u in range(2 * B):
                act.wait_ge(sem("a_scores_psum"), u + 1)
                if u >= 2:
                    act.wait_ge(sem("a_probs_used"), u - 1)
                bank = 2 * (u % 2)
                act.activation(flat(a_probs[u % 2][:, :, :]), ps[:, bank:bank + 2, :].rearrange("p a c -> p (a c)"),
                               ACT.Exp, scale=HD ** 0.5).then_inc(sem("a_exp_ready"), 1)
                if u % 2:
                    b = u // 2
                    act.wait_ge(sem("a_probs_used"), u + 1)
                    if b:
                        act.wait_ge(sem("a_sumsT_psum"), b)
                    copy(a_sums[:, :, :], rows_from(OB)).then_inc(sem("a_sums_ready"), 1)
            act.wait_ge(sem("a_attnT_psum"), 1)
            copy(xnT[:, :, :], rows_from(XB)).then_inc(sem("a_attnT_ready"), 1)

            act.wait_ge(sem("w_f0"), loads["w_f0"])
            act.wait_ge(sem("k_stored"), stored(B))
            for l in range(2):
                n = l * B
                act.wait_ge(sem("f_yT_psum"), l + 1)
                copy(hT[0:64, :, :], rows_from(XB)[0:64])
                copy(hT[64:P, :, 1:P], rows_from(XB)[64:P, :, 0:P - 1]).then_inc(sem("f_hT_ready"), 1)

                def lengths(b):
                    act.wait_ge(sem("f_ss_ready"), n + b + 1)
                    act.activation(f_norm[:, b, :], f_ss[:, b, :], ACT.Sqrt).then_inc(sem("f_norm_ready"), 1)

                def qk_rows(b):
                    act.wait_ge(sem("f_qkT_psum"), n + b + 1)
                    copy(f_qkT[b], ps[:, OB:OB + 2, :].rearrange("p a (t q) -> p (a t) q", t=4))\
                        .then_inc(sem("f_qkT_ready"), 1)

                for b in range(B):
                    act.wait_ge(sem("f_qkv_psum"), n + b + 1)
                    if b >= 2:
                        act.wait_ge(sem("f_ss_ready"), n + b - 1)
                    bank = 2 * (b % 2)
                    act.activation(f_sq[b % 2], ps[:, bank:bank + 2, :].rearrange("p a c -> p (a c)"), ACT.Square)\
                       .then_inc(sem("f_sq_ready"), 1)
                    copy(f_v[b], ps[:, 4 + b % 2, :]).then_inc(sem("f_v_ready"), 1)
                    if b >= 1:
                        lengths(b - 1)
                qk_rows(0)
                lengths(B - 1)
                qk_rows(1)

                def exponentials(b):
                    act.wait_ge(sem("f_bias_ready"), n + b + 1)
                    if b >= 2:
                        act.wait_ge(sem("f_probsT_psum"), n + b - 1)
                    for h in range(FH):
                        last = act.activation(f_probs[b % 2][:, h, :],
                                              ps[:, 2 * (b % 2) + h % 2, h // 2 * P:(h // 2 + 1) * P], ACT.Exp,
                                              bias=f_bias[:, b % 2, h:h + 1], scale=f_qs[:, b, h:h + 1],
                                              accum_out=f_den[:, b % 2, h:h + 1])
                    last.then_inc(sem("f_exp_ready"), 1)

                exponentials(0)
                qk_rows(2)
                qk_rows(3)
                exponentials(1)
                for b in range(B):
                    if b + 2 < B:
                        exponentials(b + 2)
                    act.wait_ge(sem("f_o_psum"), n + b + 1)
                    if b >= 2:
                        act.wait_ge(sem("f_attn_psum"), n + b - 1)
                    copy(f_oT[b % 2], ps[:, OB, :].rearrange("p (t q) -> p t q", t=4)).then_inc(sem("f_oT_ready"), 1)

                act.wait_ge(sem("normT_psum"), nth("normT_psum", f"g{l}"))
                act.activation(xnT[:, :, :], rows_from(XB), ACT.Identity, bias=lbf[:, l:l + 1], scale=lgf[:, l:l + 1])\
                   .then_inc(sem("normT_ready"), 1)
                for m in range(3):
                    act.wait_ge(sem("f_gate_psum"), 3 * l + m + 1)
                    act.activation(f_gelu[m][0:HT[m], :], ps[0:HT[m], (3 + 2 * m) % 6, :], ACT.Gelu,
                                   bias=b1f[0:HT[m], l, 1, m:m + 1]).then_inc(sem("f_gelu_ready"), 1)

        def act_middle1(act, copy):
            def rows_from(bank):
                return ps[:, bank, :].rearrange("p (b q) -> p b q", b=B)

            act.wait_ge(sem("normT_psum"), nth("normT_psum", "s1"))
            copy(xnT[:, :, :], rows_from(XB)).then_inc(sem("normT_ready"), 1)
            act.wait_ge(sem("s_T_psum"), 1)
            act.wait_ge(sem("w_a1"), loads["w_a1"])
            act.activation(s_T[:, :, :], rows_from(0), ACT.Identity, bias=bspin_col[:, :]).then_inc(sem("s_T_ready"), 1)
            act.wait_ge(sem("s_eT_psum"), 1)
            copy(s_eT[:, :, :], rows_from(2)).then_inc(sem("s_eT_ready"), 1)
            act.wait_ge(sem("s_bias_ready"), 1)
            for b in range(B):
                last = act.activation(s_probs[:, b, :], ps[:, 3, b * P:(b + 1) * P], ACT.Exp, bias=s_bias[:, b:b + 1],
                                      scale=D ** -0.5, accum_out=s_den[:, b:b + 1])
            last.then_inc(sem("s_exp_ready"), 1)
            act.wait_ge(sem("s_probsT_psum"), 1)
            copy(s_probsT[:, :, :], rows_from(XB)).then_inc(sem("s_probsT_ready"), 1)
            act.wait_ge(sem("s_sum_ready"), 1)
            act.activation(xn2[:, :, :], ytmp[:, :, :], ACT.Tanh, scale=beta[:, :]).then_inc(sem("s_tanh_ready"), 1)

            act.wait_ge(sem("normT_psum"), nth("normT_psum", "m1"))
            copy(xnT[:, :, :], rows_from(XB)).then_inc(sem("normT_ready"), 1)
            act.wait_ge(sem("m_top_ready"), 1)
            act.activation(m_tanh[:, :], m_top[:, :], ACT.Tanh, scale=0.5).then_inc(sem("m_tanh_ready"), 1)
            for k in range(MU):
                if k == 2:
                    act.wait_ge(sem("m_xsT_psum"), 1)
                    copy(m_xsT[:, :, :], rows_from(6)).then_inc(sem("m_xsT_ready"), 1)
                act.wait_ge(sem("m_gu_psum"), k + 1)
                if k >= 3:
                    act.wait_ge(sem("m_act_ready"), k - 2)
                act.activation(m_silu[k % 3], ps[:, 2 + 2 * (k % 3), :], ACT.Silu).then_inc(sem("m_silu_ready"), 1)

        def wide(v, n):
            return spread(v.rearrange("p (a b) -> p a b", b=1), 2, n)

        def dve_middle0(dve, link, norm, values):
            norm(x, xn, "a0").then_inc(sem("norm_ready"), 1)
            dve.wait_ge(sem("norm_ready"), nth("norm_ready", "a0"))
            norm(xn, xn2, "a1").then_inc(sem("norm_ready"), 1)
            dve.wait_ge(sem("w_v1"), loads["w_v1"])
            values(1, B)
            dve.wait_ge(sem("w_a0"), loads["w_a0"])

            def biased(b):
                dve.wait_ge(sem("a_qkv_psum"), b + 1)
                dve.tensor_tensor(a_qkv[:, b, :], ps[:, b, 0:3 * D], bqkv0[:, :], ALU.add)\
                   .then_inc(sem("a_qkv_ready"), 1)

            def squared_lengths(b):
                dve.wait_ge(sem("a_sq_ready"), b + 1)
                dve.tensor_reduce(a_ss[:, b, :], a_sq[:, b, :].rearrange("p (h d) -> p h d", d=HD), AX.X, ALU.add)\
                   .then_inc(sem("a_ss_ready"), 1)

            def unit_length(b):
                dve.wait_ge(sem("a_norm_ready"), b + 1)
                link(dve.tensor_scalar(a_norm[:, b, :], a_norm[:, b, :], 1e-12, None, ALU.max))
                link(dve.reciprocal(a_inv[:, b, :], a_norm[:, b, :]))
                dve.tensor_tensor(a_qk[:, b, :].rearrange("p (h d) -> p h d", d=HD),
                                  a_qkv[:, b, 0:2 * D].rearrange("p (h d) -> p h d", d=HD),
                                  wide(a_inv[:, b, :], HD), ALU.mult).then_inc(sem("a_qk_ready"), 1)

            for s in range(B + 2):
                if s < B:
                    biased(s)
                if 1 <= s <= B:
                    squared_lengths(s - 1)
                if s >= 2:
                    unit_length(s - 2)

            def query_block(b, half):
                heads = slice(8 * half, 8 * half + 8)
                q = spread(a_qkT[:, b, 0:P].rearrange("p (a q) -> p a q", a=1), 1, 8)
                dve.tensor_tensor(a_qblk[b % 2][:, heads, :], q, wide(headmask[:, heads], P), ALU.mult)\
                   .then_inc(sem("a_qblk_ready"), 1)

            for b in range(2):
                dve.wait_ge(sem("a_qkT_ready"), b + 1)
                for half in range(2):
                    query_block(b, half)
            for b in range(B):
                if b + 2 < B:
                    dve.wait_ge(sem("a_qkT_ready"), b + 3)
                    dve.wait_ge(sem("a_scores_psum"), 2 * b + 2)
                    for half in range(2):
                        query_block(b + 2, half)
                dve.wait_ge(sem("a_sumsT_psum"), b + 1)
                sumsT = ps[:, XB, :].rearrange("p (h w) -> p h w", w=32)
                link(dve.reciprocal(a_rden[:, :], sumsT[:, :, HD]))
                dve.tensor_tensor(attn_tok[:, b, :].rearrange("p (h d) -> p h d", d=HD), sumsT[:, :, 0:HD],
                                  wide(a_rden[:, :], HD), ALU.mult).then_inc(sem("a_attended"), 1)
            dve.wait_ge(sem("a_out_psum"), 1)
            dve.wait_ge(sem("a_res_ready"), 2)
            link(dve.tensor_tensor(x[:, :, :], xres[:, :, :], ps[:, OB, :].rearrange("p (b d) -> p b d", b=B), ALU.add))

            dve.wait_ge(sem("w_rot"), loads["w_rot"])
            dve.tensor_copy(band_bf[:, :], band[:, :]).then_inc(sem("band_ready"), 1)
            norm(x, y, "f0").then_inc(sem("f_y_ready"), 1)
            dve.wait_ge(sem("rotl_ready"), 2)
            for l in range(2):
                n = l * B

                def inverses(b):
                    dve.wait_ge(sem("f_norm_ready"), n + b + 1)
                    link(dve.tensor_scalar(f_norm[:, b, :], f_norm[:, b, :], 1e-12, None, ALU.max))
                    dve.reciprocal(f_inv[:, b, :], f_norm[:, b, :]).then_inc(sem("f_inv_ready"), 1)
                    dve.wait_ge(sem("f_inv_ready"), n + b + 1)
                    link(dve.tensor_scalar(f_qs[:, b, :], f_inv[:, b, 0:FH], 8.0, None, ALU.mult))

                for b in range(B):
                    dve.wait_ge(sem("f_sq_ready"), n + b + 1)
                    dve.tensor_reduce(f_ss[:, b, :], f_sq[b % 2].rearrange("p (h d) -> p h d", d=FD), AX.X, ALU.add)\
                       .then_inc(sem("f_ss_ready"), 1)
                    if b >= 1:
                        inverses(b - 1)
                    if b >= 2:
                        dve.wait_ge(sem("f_rotsum_ready"), n + b - 1)
                    for i in range(2):
                        src = ps[:, 2 * (b % 2) + i, :].rearrange("p (h d) -> p h d", h=FH)
                        cols = slice(i * INNER, (i + 1) * INNER)
                        cos = spread(rotl[:, l, 2 * i:2 * i + 1, :], 1, FH)
                        dve.tensor_tensor(f_cos[b % 2][:, cols].rearrange("p (h d) -> p h d", h=FH), src, cos, ALU.mult)
                        for half in range(2):
                            to = slice(half * 32, half * 32 + 32)
                            of = slice(32 - half * 32, 64 - half * 32)
                            sin = spread(rotl[:, l, 2 * i + 1:2 * i + 2, to], 1, FH)
                            last = dve.tensor_tensor(f_sin[b % 2][:, cols].rearrange("p (h d) -> p h d", h=FH)[:, :, to],
                                                     src[:, :, of], sin, ALU.mult)
                    last.then_inc(sem("f_rot_ready"), 1)
                inverses(B - 1)

                def maxima(b):
                    dve.wait_ge(sem("f_scores_psum"), n + b + 1)
                    bank = 2 * (b % 2)
                    link(dve.tensor_reduce(f_max[:, b % 2, :], ps[:, bank:bank + 2, :].rearrange("p a (h k) -> p (a h) k", h=4),
                                           AX.X, ALU.max, negate=True))
                    dve.tensor_tensor(f_bias[:, b % 2, :].rearrange("p (j e) -> p e j", e=2),
                                      f_max[:, b % 2, :].rearrange("p (e j) -> p e j", e=2),
                                      f_qs[:, b, :].rearrange("p (j e) -> p e j", e=2), ALU.mult)\
                       .then_inc(sem("f_bias_ready"), 1)

                maxima(0)
                maxima(1)
                for b in range(B):
                    dve.wait_ge(sem("f_exp_ready"), n + b + 1)
                    link(dve.reciprocal(f_rden[:, :], f_den[:, b % 2, :]))
                    dve.tensor_tensor(f_probs[b % 2], f_probs[b % 2], wide(f_rden[:, :], P), ALU.mult)\
                       .then_inc(sem("f_probs_ready"), 1)
                    if b + 2 < B:
                        maxima(b + 2)
                    dve.wait_ge(sem("f_probsT_psum"), n + b + 1)
                    if b >= 2:
                        dve.wait_ge(sem("f_o_psum"), n + b - 1)
                    dve.tensor_copy(flat(f_probsT[b % 2]), ps[:, 4:6, :].rearrange("p a c -> p (a c)"))\
                       .then_inc(sem("f_probsT_ready"), 1)
                dve.wait_ge(sem("f_attn_psum"), n + B)
                dve.tensor_tensor(y[:, :, :], y[:, :, :], ps[:, XB, :].rearrange("p (b d) -> p b d", b=B), ALU.add)\
                   .then_inc(sem("f_y_ready"), 1)
                dve.wait_ge(sem("f_shift_psum"), l + 1)
                dve.wait_ge(sem("f_unshifted_ready"), l + 1)
                link(dve.tensor_copy(f_shift[:, :, 64:D], ps[:, 0, 0:B * 64].rearrange("p (b d) -> p b d", b=B)))
                norm(f_shift, xn, f"g{l}").then_inc(sem("norm_ready"), 1)
                for m in range(3):
                    dve.wait_ge(sem("f_gelu_ready"), 3 * l + m + 1)
                    dve.wait_ge(sem("f_up_psum"), 3 * l + m + 1)
                    rows = slice(0, HT[m])
                    dve.scalar_tensor_tensor(f_act[m][rows, :], ps[rows, (2 + 2 * m) % 6, :], b1f[rows, l, 0, m:m + 1],
                                             f_gelu[m][rows, :], ALU.add, ALU.mult).then_inc(sem("f_act_ready"), 1)
                dve.wait_ge(sem("f_w2_psum"), l + 1)
                dve.wait_ge(sem("f_biased_ready"), l + 1)
                dve.tensor_tensor(y[:, :, :], ytmp[:, :, :], ps[:, OB, :].rearrange("p (b d) -> p b d", b=B), ALU.add)\
                   .then_inc(sem("f_y_ready"), 1)
                dve.wait_ge(sem("f_y_ready"), 2 * l + 3)
            link(dve.tensor_tensor(x[:, :, :], x[:, :, :], y[:, :, :], ALU.add))

        def dve_middle1(dve, link, norm):
            norm(x, xn, "s1").then_inc(sem("norm_ready"), 1)
            dve.wait_ge(sem("w_a1"), loads["w_a1"])
            dve.wait_ge(sem("s_tok_psum"), 1)
            bias = spread(bspin_row[:, :].rearrange("p (a n) -> p a n", a=1), 1, B)
            dve.tensor_tensor(s_tok[:, :, :], ps[:, 1, :].rearrange("p (b d) -> p b d", b=B), bias, ALU.add)\
               .then_inc(sem("s_tok_ready"), 1)
            dve.wait_ge(sem("s_T_ready"), 1)
            link(dve.tensor_reduce(s_mean[:, :], s_T[:, :, :], AX.X, ALU.add))
            dve.tensor_scalar(s_meanrows[:, :, :], wide(s_mean[:, :], P), 1.0 / P, None, ALU.mult)\
               .then_inc(sem("s_mean_ready"), 1)
            dve.wait_ge(sem("s_scores_psum"), 1)
            link(dve.tensor_reduce(s_max[:, :], ps[:, 3, :].rearrange("p (b q) -> p b q", b=B), AX.X, ALU.max,
                                   negate=True))
            dve.tensor_scalar(s_bias[:, :], s_max[:, :], D ** -0.5, None, ALU.mult).then_inc(sem("s_bias_ready"), 1)
            dve.wait_ge(sem("s_exp_ready"), 1)
            link(dve.reciprocal(s_rden[:, :], s_den[:, :]))
            dve.tensor_tensor(s_probs[:, :, :], s_probs[:, :, :], wide(s_rden[:, :], P), ALU.mult)\
               .then_inc(sem("s_probs_ready"), 1)
            dve.wait_ge(sem("s_field_psum"), 1)
            dve.wait_ge(sem("s_tok_ready"), 1)
            dve.tensor_tensor(ytmp[:, :, :], ps[:, 4, :].rearrange("p (b d) -> p b d", b=B), s_tok[:, :, :], ALU.add)\
               .then_inc(sem("s_sum_ready"), 1)
            dve.wait_ge(sem("s_tanh_ready"), 1)
            link(dve.tensor_tensor(x[:, :, :], x[:, :, :], xn2[:, :, :], ALU.add))

            norm(x, xn, "m1").then_inc(sem("norm_ready"), 1)
            dve.wait_ge(sem("w_m1"), loads["w_m1"])
            dve.wait_ge(sem("m_logit_psum"), 1)
            logits = ps[:, 0, 0:B * E].rearrange("p (b e) -> p b e", b=B)
            link(dve.tensor_copy(m_logit[:, :, :], logits))
            dve.tensor_reduce(m_top[:, :], m_logit[:, :, :], AX.X, ALU.max).then_inc(sem("m_top_ready"), 1)
            dve.wait_ge(sem("m_top_ready"), 1)
            link(dve.tensor_tensor(m_eq[:, :, :], m_logit[:, :, :], wide(m_top[:, :], E), ALU.is_equal))
            link(dve.tensor_tensor(m_rank[:, :, :], m_eq[:, :, :], erank[:, :, :], ALU.mult))
            link(dve.tensor_reduce(m_first[:, :], m_rank[:, :, :], AX.X, ALU.max))
            dve.tensor_tensor(m_hot[:, :, :], m_rank[:, :, :], wide(m_first[:, :], E), ALU.is_equal)\
               .then_inc(sem("m_hot_ready"), 1)
            dve.wait_ge(sem("m_tanh_ready"), 1)
            link(dve.tensor_scalar(m_score[:, :], m_tanh[:, :], 0.5, 0.5, ALU.mult, ALU.add))
            dve.tensor_tensor(m_xs[:, :, :], xn[:, :, :], wide(m_score[:, :], D), ALU.mult)\
               .then_inc(sem("m_xs_ready"), 1)

            def expert_rows(e):
                dve.wait_ge(sem("m_mask_psum"), e + 1)
                if e >= 2:
                    dve.wait_ge(sem("m_gu_psum"), 2 * e)
                dve.tensor_tensor(m_xe[e % 2][:, :, :], m_xsT[:, :, :], ps[:, 1, :].rearrange("p (b q) -> p b q", b=B),
                                  ALU.mult).then_inc(sem("m_xe_ready"), 1)

            for k in range(MU):
                if k == 2:
                    dve.wait_ge(sem("m_xsT_ready"), 1)
                    expert_rows(0)
                if k >= 2 and k % 2 == 0 and unit_expert(k) + 1 < E:
                    expert_rows(unit_expert(k) + 1)
                dve.wait_ge(sem("m_silu_ready"), k + 1)
                if k >= 3:
                    dve.wait_ge(sem("m_down_psum"), k - 2)
                dve.tensor_tensor(flat(m_act[k % 3][:, :, :]), m_silu[k % 3], ps[:, 3 + 2 * (k % 3), :], ALU.mult)\
                   .then_inc(sem("m_act_ready"), 1)
            dve.wait_ge(sem("m_down_psum"), MU)
            dve.tensor_tensor(xn2[:, :, :], x[:, :, :], ps[:, 0, :].rearrange("p (b d) -> p b d", b=B), ALU.add)\
               .then_inc(sem("out_ready"), 1)

        def pool_middle0(pool, rstd_of, alone):
            rstd_of("a0")
            pool.wait_ge(sem("norm_ready"), nth("norm_ready", "a0"))
            rstd_of("a1")
            alone(pool.tensor_tensor(xres[:, :, :], x[:, :, :], xn[:, :, :], ALU.add), "a_res_ready", 1)
            pool.wait_ge(sem("w_a0"), loads["w_a0"])
            alone(pool.tensor_tensor(xres[:, :, :], xres[:, :, :],
                                     spread(bout0[:, :].rearrange("p (a n) -> p a n", a=1), 1, B), ALU.add),
                  "a_res_ready", 2)
            alone(pool.memset(a_v[:, :, :, HD], 1.0), "a_v_ready", 1)
            for b in range(B):
                pool.wait_ge(sem("a_qkv_ready"), b + 1)
                alone(pool.tensor_copy(a_v[:, b, :, 0:HD],
                                       a_qkv[:, b, 2 * D:3 * D].rearrange("p (h d) -> p h d", d=HD)),
                      "a_v_ready", b + 2)
            pool.wait_ge(sem("w_rot"), loads["w_rot"])
            for l in range(2):
                alone(pool.tensor_tensor(rotl[:, l, :, :], rot[:, :, :], rot_scale[:, l, :, :], ALU.mult),
                      "rotl_ready", l + 1)
            rstd_of("f0")
            pool.wait_ge(sem("w_f0"), loads["w_f0"])
            for l in range(2):
                n = l * B

                def normal_keys(b):
                    pool.wait_ge(sem("f_inv_ready"), n + b + 1)
                    k = f_qk[b][:, INNER:2 * INNER].rearrange("p (h d) -> p h d", h=FH)
                    alone(pool.tensor_tensor(k, k, wide(f_inv[:, b, FH:2 * FH], FD), ALU.mult), "f_kn_ready", n + b + 1)

                for b in range(B):
                    pool.wait_ge(sem("f_rot_ready"), n + b + 1)
                    alone(pool.tensor_tensor(f_qk[b], f_cos[b % 2], f_sin[b % 2], ALU.add),
                          "f_rotsum_ready", n + b + 1)
                    normal_keys(b)
                pool.wait_ge(sem("f_y_ready"), 2 * l + 2)
                alone(pool.tensor_copy(f_shift[:, :, 0:64], y[:, :, 0:64]), "f_unshifted_ready", l + 1)
                rstd_of(f"g{l}")
                alone(pool.tensor_tensor(ytmp[:, :, :], y[:, :, :], spread(b2f[:, l:l + 1, :], 1, B), ALU.add),
                      "f_biased_ready", l + 1)

        def pool_middle1(pool, rstd_of):
            rstd_of("s1")
            rstd_of("m1")

        FREED_BY = {"T": "ctxT_ready", "K": "k_rest_ready", "V": "v_ready", "M": "max_taken"}

        def stored(n):
            return n * 48 + 32

        @block.sync
        def _(sp):
            def load(dst, src, name):
                sp.dma_start(dst, src).then_inc(sem(name), 16)
                loads[name] = loads.get(name, 0) + 16

            def col(ap):
                return ap.rearrange("(p a) -> p a", a=1)

            def rows(ap):
                return spread(ap.rearrange("(a n) -> a n", a=1), 0, P)

            def load_context(b):
                src = a["ctx"][bass.ds(b, 1), :, :].rearrange("o (t p) d -> p (o t) d", p=P)
                for half in (slice(0, P // 2), slice(P // 2, P)):
                    sp.dma_start(ctx_in[half, :, :], src[half]).then_inc(sem("ctx_in_ready"), 16)

            def store_queries(l):
                if l:
                    sp.wait_ge(sem("qstack_ready"), 192)
                for i in range(3):
                    sp.wait_ge(sem(f"q_part{i}_ready"), l + 1)
                    sp.dma_start(q_dram[i], q_part[i][:, :]).then_inc(sem(f"q{i}_stored"), 16)

            def stack_queries(l, i):
                sp.wait_ge(sem(f"q{i}_stored"), 16 * (l + 1))
                sp.wait_ge(sem("qstack_cleared"), 2)
                for r in range(6):
                    for par in range(2):
                        if PART_Q[r] == i:
                            lo = (2 * r + par) * HD
                            src = q_dram[i].rearrange("(j e d) n -> e d j n", e=2, d=HD)[par]
                            sp.dma_start(qstack[lo:lo + HD, :, par, :, :].rearrange("d j b q -> d j (b q)"), src)\
                              .then_inc(sem("qstack_ready"), 16)

            def stack_rows(i, parity, lo, hi):
                for r in range(6):
                    if PART_K[r] == i:
                        dst = kstack[2 * HD * r:2 * HD * (r + 1), bass.ds(parity, 1), lo:hi, :]
                        src = k_dram[i][lo * 2 * HD:hi * 2 * HD].rearrange("(j p) n -> p j n", p=2 * HD)
                        sp.dma_start(dst.rearrange("p o j n -> p (o j) n"), src)\
                          .then_inc(sem("first_k_stacked" if hi == 2 else "kstack_ready"), 16)

            def stack_keys(n, parity):
                sp.wait_ge(sem("kstack_ready"), n * 96)
                for i in range(3):
                    per = (2, 4, 1)[i]
                    sp.wait_ge(sem(f"k_part{i}_ready"), n * per + per)
                    sp.dma_start(k_dram[i], k_part[i][:, :]).then_inc(sem("k_stored"), 16)
                    sp.wait_ge(sem("k_stored"), stored(n - 1) + 16 * (i + 1))
                    stack_rows(i, parity, 0, PAIRS)

            def store_first_keys(i, rows, name):
                sp.wait_ge(sem(f"k_part{i}_ready"), (2, 4, 1)[i])
                sp.dma_start(k_dram[i][rows], k_part[i][rows, :]).then_inc(sem(name), 16)

            def stack_mask(b, parity):
                src = spread(m_dram[bass.ds(b, 1), :].rearrange("o (a n) -> o a n", a=1), 1, PAIRS)
                dst = kstack[MASK_ROW:MASK_ROW + 1, bass.ds(parity, 1), :, :].rearrange("d o j n -> d (o j) n")
                sp.dma_start(dst, src).then_inc(sem("mask_stacked"), 16)

            def rows_under(parities):
                times = len(parities) * PAIRS * CTX // BANK
                src = spread(row_init[MASK_ROW:KROWS_EXP, :].rearrange("d (a n) -> d a n", a=1), 1, times)
                dst = kstack[MASK_ROW:KROWS_EXP, parities[0]:, :, :].rearrange("d o j (c n) -> d (o j c) n", n=BANK)
                sp.dma_start(dst, src).then_inc(sem("rows_stacked"), 16)

            def cross_weights(l):
                for n in ("k", "q", "v", "o"):
                    src = a[f"L{l}_xattn_b{n}"]
                    load(wx[l][n][:, :], a[f"L{l}_xattn_W{n}"], f"w_{n}{l}")
                    load(bx[l][n][:, :], col(src) if n in "qk" else rows(src), f"w_{n}{l}")

            def weights_after():
                load(wqkv0[:, :], a["L0_attn_qkv_wT"], "w_a0")
                load(bqkv0[:, :], rows(a["L0_attn_qkv_b"]), "w_a0")
                load(wout0[:, :], a["L0_attn_out_wT"], "w_a0")
                load(bout0[:, :], rows(a["L0_attn_out_b"]), "w_a0")
                load(lnw0[:, :], col(a["L0_attn_ln_w"]), "w_a0")
                load(lnb0[:, :], col(a["L0_attn_ln_b"]), "w_a0")
                load(headmask[:, :], a["c_headmask"], "w_a0")
                load(rot[:, :, :], a["c_rot"], "w_rot")
                for l in range(2):
                    for i, n in enumerate(("q", "k")):
                        s = a[f"L0_ffn_{n}_scale"][l]
                        load(rot_scale[:, l, 2 * i, :], rows(s), "w_rot")
                        load(rot_scale[:, l, 2 * i + 1, 0:32], rows(s[32:64]), "w_rot")
                        load(rot_scale[:, l, 2 * i + 1, 32:64], rows(s[0:32]), "w_rot")
                load(band[:, :], a["c_band"], "w_rot")
                load(shift[:, :], a["c_shift"], "w_f0")
                for l in range(2):
                    load(wqkvf[:, l, :], a["L0_ffn_wqkv"][l], "w_f0")
                    load(wof[:, l, :, :], a["L0_ffn_wo"][l].rearrange("(t p) n -> p t n", p=P), "w_f0")
                    load(w1f[:, l, :], a["L0_ffn_w1"][l], "w_f0")
                    load(w2f[:, l, 0:2, :], a["L0_ffn_w2"][l, 0:2 * P, :].rearrange("(t p) n -> p t n", p=P), "w_f0")
                    load(w2f[0:HT[2], l, 2, :], a["L0_ffn_w2"][l, 2 * P:HID, :], "w_f0")
                    load(lgf[:, l:l + 1], col(a["L0_ffn_ln_g"][l]), "w_f0")
                    load(lbf[:, l:l + 1], col(a["L0_ffn_ln_b"][l]), "w_f0")
                    load(b2f[:, l, :], rows(a["L0_ffn_b2"][l]), "w_f0")
                    for ag in range(2):
                        for m in range(3):
                            lo = ag * HID + m * P
                            load(b1f[0:HT[m], l, ag, m:m + 1], col(a["L0_ffn_b1"][l, lo:lo + HT[m]]), "w_f0")
                load(wspin[:, :], a["L1_attn_W_spinT"], "w_a1")
                load(bspin_col[:, :], col(a["L1_attn_b_spin"]), "w_a1")
                load(bspin_row[:, :], rows(a["L1_attn_b_spin"]), "w_a1")
                load(wglob[:, :], a["L1_attn_W_globalT"], "w_a1")
                load(wj[:, :], a["L1_attn_W_JT"], "w_a1")
                load(beta[:, :], rows(a["L1_attn_beta"]), "w_a1")
                load(wgate[:, :], a["L1_ffn_gate_w"], "w_m1")
                load(erank[:, :, :], spread(a["c_erank"].rearrange("(a b) e -> a b e", a=1), 0, P), "w_m1")

            load(ident[:, :], a["c_ident"], "w_base")
            load_context(0)
            load(x[:, :, :], a["x"].rearrange("b s d -> s b d"), "x_loaded")
            cross_weights(0)
            load(mask_u8[:, :], a["mask"].rearrange("(p f) -> p f", p=P), "mask_loaded")
            sp.wait_ge(sem("row_init_ready"), 2)
            rows_under((0, 1))

            first, others = slice(0, 4 * HD), slice(4 * HD, P)
            sp.wait_ge(sem("ctxT_psum"), 2)
            load_context(1)
            store_queries(0)
            store_first_keys(0, slice(0, P), "part0_stored")
            stack_queries(0, 0)
            for i in (1, 2):
                store_first_keys(i, first, "first_k_stored")
            stack_queries(0, 1)
            stack_queries(0, 2)
            sp.wait_ge(sem("part0_stored"), 16)
            sp.wait_ge(sem("first_k_stored"), 32)
            for i in range(3):
                stack_rows(i, 0, 0, 2)
            for i in (1, 2):
                store_first_keys(i, others, "k_stored")
            sp.wait_ge(sem("k_stored"), stored(0))
            for i in range(3):
                stack_rows(i, 0, 2, PAIRS)
            sp.wait_ge(sem("ctxT_psum"), 4)
            load_context(2)
            cross_weights(1)
            with sp.Fori(0, B - 1) as b:
                stack_keys(b + 1, sp.snap((b + 1) % 2))
                sp.wait_ge(sem("ctxT_psum"), b * 2 + 6)
                load_context(sp.snap((b + 3) % 4))
            sp.wait_ge(sem("mask_bias_ready"), 1)
            sp.dma_start(m_dram.rearrange("b (p f) -> (b p) f", p=P // B), mask_bias[:, :])\
              .then_inc(sem("mask_stored"), 16)
            weights_after()
            sp.wait_ge(sem("k_part0_ready"), 2 * B + 2)
            sp.wait_ge(sem("mask_stored"), 16)
            stack_mask(0, 0)
            stack_keys(B, 0)

            store_queries(1)
            for i in range(3):
                stack_queries(1, i)
            rows_under((1,))
            load_context(2)
            sp.wait_ge(sem("rows_stacked"), 32)

            def stack_next(b):
                parity = (b + 1) % 2 if isinstance(b, int) else sp.snap((b + 1) % 2)
                sp.wait_ge(sem("k_part0_ready"), b * 2 + (2 * B + 4))
                stack_mask(b + 1, parity)
                stack_keys(b + (B + 1), parity)

            stack_next(0)
            sp.wait_ge(sem("ctxT_psum"), 2 * (B + 3))
            load_context(3)
            with sp.Fori(1, B - 1) as b:
                stack_next(b)

            sp.wait_ge(sem("v_psum"), 4 * B)
            load(gate_up[:, 0, :, :], a["L1_ffn_rt_gate"].rearrange("e k n -> k e n"), "w_e")
            load(gate_up[:, 1, :, :], a["L1_ffn_rt_up"].rearrange("e k n -> k e n"), "w_e")
            load(down[:, :, :, :], a["L1_ffn_rt_down"].rearrange("e (t k) n -> k e t n", k=P), "w_e")
            load(sh_gate_up[:, 0, :], a["L1_ffn_sh_gate"], "w_e")
            load(sh_gate_up[:, 1, :], a["L1_ffn_sh_up"], "w_e")
            load(sh_down[:, :, :], a["L1_ffn_sh_down"].rearrange("(t k) n -> k t n", k=P), "w_e")

            sp.wait_ge(sem("out_ready"), 1)
            sp.dma_start(out.rearrange("b s d -> s b d"), xn2[:, :, :]).then_inc(sem("out_stored"), 16)
            sp.wait_ge(sem("out_stored"), 16)

        @block.tensor
        def _(pe):
            def transposes(src, bank, ready, count, name):
                pe.wait_ge(sem(ready), count)
                for b in range(B):
                    last = pe.transpose(ps[:, bank, b * P:(b + 1) * P], src[:, b, :], ident[:, :])
                last.then_inc(sem(name), 1)

            def keep_clock(bank, times):
                wide_ident = spread(ident_bf[:, :].rearrange("p (a k) -> p a k", a=1), 1, 4)
                for _ in range(times):
                    pe.matmul(ps[:, bank, :].rearrange("p (a k) -> p a k", a=4), ident_bf[:, :], wide_ident,
                              start=True, stop=True)

            def free_pair(prev):
                for kind, value in prev[-2]:
                    pe.wait_ge(sem(FREED_BY[kind]), value)
                return 2 * (len(prev) % 2)

            def transpose_context(n, prev):
                for u in range(2):
                    bank = free_pair(prev)
                    if u == 0:
                        pe.wait_ge(sem("ctx_in_ready"), n * 32 + 32)
                    transpose_half(u, bank)
                    prev.append([("T", n * 2 + (u + 1))])

            def transpose_half(u, bank):
                for t in range(8):
                    last = pe.transpose(ps[:, bank + t // 4, (t % 4) * P:(t % 4 + 1) * P],
                                        ctx_in[:, 8 * u + t, :], ident[:, :])
                last.then_inc(sem("ctxT_psum"), 1)

            def project_keys(l, n, prev):
                for u in range(2):
                    bank = free_pair(prev)
                    pe.wait_ge(sem("ctxT_ready"), n * 2 + (u + 1))
                    for c in range(2):
                        lo = (2 * u + c) * BANK
                        last = pe.matmul(ps[:, bank + c, :], wx[l]["k"][:, :], ctxT[:, lo:lo + BANK],
                                         start=True, stop=True)
                    last.then_inc(sem("k_psum"), 1)
                    prev.append([("K", n * 2 + (u + 1))])

            def project_values(l, n, prev, halves=(0, 1)):
                for u in halves:
                    bank = free_pair(prev)
                    for t in range(8):
                        tile = 8 * u + t
                        last = pe.matmul(ps[:, bank + t // 4, (t % 4) * P:(t % 4 + 1) * P],
                                         ctxT[:, tile * P:(tile + 1) * P], wx[l]["v"][:, :], start=True, stop=True)
                    last.then_inc(sem("v_psum"), 1)
                    prev.append([("V", n * 2 + (u + 1))])

            def max_chunk(n, b, parity, j, c, prev, first=False):
                i, k = c // 4, c % 4
                if c % 2 == 0:
                    free_pair(prev)
                bank = 2 * (len(prev) % 2) + c % 2
                if j == 0 and c == 0 and not first:
                    pe.wait_ge(sem("kstack_ready"), n * 96 + 96)
                pair, half = 2 * j + i // 2, i % 2
                last = pe.matmul(ps[:, bank, :], qstack[0:KROWS_MAX, pair, half, b, :],
                                 kstack[0:KROWS_MAX, parity, pair, k * BANK:(k + 1) * BANK], start=True, stop=True)
                if c % 2:
                    last.then_inc(sem("max_psum"), 1)
                    prev.append([("M", n * 32 + (8 * j + c // 2 + 1))])

            def max_rows(n, j):
                pe.wait_ge(sem("neg_split_ready"), n * 4 + (j + 1))
                for i in range(4):
                    last = pe.matmul(ps[MASK_ROW:KROWS_EXP, XB, i * P:(i + 1) * P], neg_split[:, i, :], ident_bf[:, :],
                                     start=True, stop=True)
                last.then_inc(sem("max_rows_psum"), 1)

            def weigh(n, s):
                j, t = s // TILES, s % TILES
                pe.wait_ge(sem("exp_ready"), n * 64 + (s + 1))
                if t == 0 and j >= 1:
                    pe.wait_ge(sem("sums_ready"), n * 4 + j)
                for i in range(4):
                    last = pe.matmul(ps[32 * i:32 * i + VW, OB, 0:P], vones[:, t, 4 * j + i, :],
                                     probs[:, s % 4, i, :], start=(t == 0), stop=(t == TILES - 1))
                last.then_inc(sem("probs_used"), 1)

            def transpose_sums(n, j):
                pe.wait_ge(sem("sums_ready"), n * 4 + (j + 1))
                pe.transpose(ps[:, XB, 0:P], sums[:, :], ident[:, :]).then_inc(sem("sumsT_psum"), 1)

            def second_pass(l, n, b, parity, nxt, prev):
                g = AHEAD
                for s in range(SLOTS):
                    j, t = s // TILES, s % TILES
                    if t == 0:
                        pe.wait_ge(sem("max_rows_ready"), n * 4 + (j + 1))
                    if s >= 2:
                        pe.wait_ge(sem("exp_ready"), n * 64 + (s - 1))
                    for p in range(2):
                        pair = 2 * j + p
                        last = pe.matmul(ps[:, E0 + s % 2, p * 2 * P:(p + 1) * 2 * P],
                                         kstack[0:KROWS_EXP, parity, pair, t * P:(t + 1) * P],
                                         qstack[0:KROWS_EXP, pair, :, b, :], start=True, stop=True)
                    last.then_inc(sem("scores_psum"), 1)
                    for _ in range(MAX_PLAN[s]):
                        if g < SLOTS:
                            max_chunk(n, b, parity, g // 16, g % 16, prev)
                        elif nxt is not None and g < SLOTS + AHEAD:
                            if l and g == SLOTS:
                                pe.wait_ge(sem("mask_stacked"), b * 16 + 32)
                            max_chunk(*nxt, g // 16 - QUADS, g % 16, prev)
                        g += 1
                    if s == 1:
                        pe.wait_ge(sem("v_ready"), n * 2 + 2)
                    if s >= 1:
                        weigh(n, s - 1)
                    if t == 3 and j >= 1:
                        transpose_sums(n, j - 1)
                    if t == MAX_ROWS_AT:
                        if j < QUADS - 1:
                            max_rows(n, j + 1)
                        elif nxt is not None:
                            max_rows(nxt[0], 0)

            def end_pass(n, prev, l_values=None, l_context=None, l_keys=None):
                if l_values is not None:
                    project_values(l_values, n + 1, prev, (0,))
                weigh(n, SLOTS - 1)
                if l_values is not None:
                    project_values(l_values, n + 1, prev, (1,))
                else:
                    pe.wait_ge(sem("attended"), n * 4 + (QUADS - 1))
                transpose_sums(n, QUADS - 1)
                if l_context is not None:
                    transpose_context(n + 2, prev)
                if l_keys is not None:
                    project_keys(l_keys, n + 2, prev)

            def project_out(l):
                transposes(attn_tok, XB, "attended", 16 * (l + 1), "attnT_psum")
                pe.wait_ge(sem(f"w_o{l}"), loads[f"w_o{l}"])
                pe.wait_ge(sem("attnT_ready"), l + 1)
                for b in range(B):
                    last = pe.matmul(ps[:, OB, b * P:(b + 1) * P], xnT[:, b, :], wx[l]["o"][:, :], start=True, stop=True)
                last.then_inc(sem("xo_psum"), 1)

            def cross_attention(l):
                n0 = B * l
                prev = [[], []]
                if l == 0:
                    transpose_context(n0, prev)
                if l:
                    pe.wait_ge(sem("mask_stacked"), 16)
                    project_keys(1, n0 + 1, prev)
                transposes(xn, XB, "norm_ready", nth("norm_ready", f"xattn{l}"), "normT_psum")
                pe.wait_ge(sem("normT_ready"), nth("normT_ready", f"xattn{l}"))
                pe.wait_ge(sem(f"w_q{l}"), loads[f"w_q{l}"])
                pe.matmul(ps[:, OB, :], wx[l]["q"][:, :], xnT[:, :, :].rearrange("p b q -> p (b q)"),
                          start=True, stop=True).then_inc(sem("q_psum"), 1)
                if l == 0:
                    pe.wait_ge(sem("w_k0"), loads["w_k0"])
                    project_keys(l, n0, prev)
                    pe.wait_ge(sem("w_v0"), loads["w_v0"])
                    project_values(l, n0, prev)
                    transpose_context(1, prev)
                    project_keys(l, 1, prev)
                    pe.wait_ge(sem("rows_stacked"), 16)
                    pe.wait_ge(sem("first_k_stacked"), 96)
                    pe.wait_ge(sem("qstack_cleared"), 2)
                pe.wait_ge(sem("qstack_ready"), 192 * (l + 1))
                for g in range(AHEAD):
                    if l == 0 and g == 16:
                        pe.wait_ge(sem("kstack_ready"), 96)
                    max_chunk(n0, 0, 0, g // 16, g % 16, prev, first=(l == 0))
                    if g == AHEAD - 4:
                        max_rows(n0, 0)

                with pe.Fori(0, B - 2) as b:
                    n = b + n0
                    parity, nxt_parity, nb = pe.snap(b % 2), pe.snap((b + 1) % 2), pe.snap(b + 1)
                    prev = [[("K", n * 2 + 3), ("M", n * 32 + (AHEAD // 2 - 1))],
                            [("K", n * 2 + 4), ("M", n * 32 + AHEAD // 2)]]
                    nxt = (n + 1, nb, nxt_parity)
                    second_pass(l, n, b, parity, nxt, prev)
                    end_pass(n, prev, l, l, l)
                    assert len(prev) % 2 == 0
                n = n0 + B - 2
                prev = [[("K", n * 2 + 3)], [("K", n * 2 + 4)]]
                second_pass(l, n, B - 2, 0, (n + 1, B - 1, 1), prev)
                if l == 0:
                    pe.wait_ge(sem("w_k1"), loads["w_k1"])
                    end_pass(n, prev, 0, 1, 1)
                else:
                    end_pass(n, prev, 1)
                n = n0 + B - 1
                second_pass(l, n, B - 1, 1, None, prev)
                end_pass(n, prev)
                project_out(l)
                if l == 0:
                    pe.wait_ge(sem("w_v1"), loads["w_v1"])
                    project_values(1, n + 1, prev)
                    pe.wait_ge(sem("ctx_in_ready"), (n + 2) * 32 + 32)
                    for u in range(2):
                        if u:
                            pe.wait_ge(sem("ctxT_ready"), 2 * (n + 2) + 1)
                        transpose_half(u, E0)

            pe.wait_ge(sem("w_base"), loads["w_base"])
            pe.wait_ge(sem("consts_ready"), 1)
            keep_clock(0, KEEP["start"])
            cross_attention(0)
            pe_middle0(pe, transposes, keep_clock)
            cross_attention(1)
            pe_middle1(pe, transposes, keep_clock)

        @block.scalar
        def _(act):
            def copy(dst, src):
                return act.activation(dst, src, ACT.Copy)

            def context_rows(n, first=False, banks=(0, 2)):
                for u in range(2):
                    act.wait_ge(sem("ctxT_psum"), n * 2 + (u + 1))
                    if u == 0 and not first:
                        act.wait_ge(sem("v_psum"), n * 2)
                    copy(ctxT[:, u * 2 * BANK:(u + 1) * 2 * BANK],
                         ps[:, banks[u]:banks[u] + 2, :].rearrange("p a c -> p (a c)")).then_inc(sem("ctxT_ready"), 1)

            def keys_high(l, n, first=False):
                for u in range(2):
                    act.wait_ge(sem("k_psum"), n * 2 + (u + 1))
                    if u == 0 and not first:
                        if first is None:
                            act.wait_ge(sem("part0_stored"), 16)
                        else:
                            act.wait_ge(sem("k_stored"), stored(n - 1))
                    act.activation(k_part[0][:, u * 2 * BANK:(u + 1) * 2 * BANK],
                                   ps[:, 2 * u:2 * u + 2, :].rearrange("p a c -> p (a c)"),
                                   ACT.Identity, bias=bx[l]["k"][:, :]).then_inc(sem("k_part0_ready"), 1)

            def keys_mid(n, c, first=False):
                act.wait_ge(sem("k_rest_ready"), n * 2 + (c // 2 + 1))
                if c == 0 and not first:
                    act.wait_ge(sem("k_stored"), stored(n - 1))
                cols = slice(c * BANK, (c + 1) * BANK)
                copy(k_part[1][:, cols], k_rest[:, cols]).then_inc(sem("k_part1_ready"), 1)

            def take_max_rows(n, b, j):
                act.wait_ge(sem("max_rows_psum"), n * 4 + (j + 1))
                for p in range(2):
                    last = copy(qstack[MASK_ROW:KROWS_EXP, 2 * j + p, :, b, :],
                                ps[MASK_ROW:KROWS_EXP, XB, p * 2 * P:(p + 1) * 2 * P]
                                .rearrange("r (h q) -> r h q", h=2))
                last.then_inc(sem("max_rows_ready"), 1)

            def take_sums(n, j):
                act.wait_ge(sem("probs_used"), n * 64 + 16 * (j + 1))
                copy(sums[:, :], ps[:, OB, 0:P]).then_inc(sem("sums_ready"), 1)

            def second_pass(n, b, nxt, nxt_keys):
                for s in range(SLOTS):
                    j, t = s // TILES, s % TILES
                    act.wait_ge(sem("scores_psum"), n * 64 + (s + 1))
                    if s >= 4:
                        act.wait_ge(sem("probs_used"), n * 64 + (s - 3))
                    act.activation(probs[:, s % 4, :, :], ps[:, E0 + s % 2, :]
                                   .rearrange("p (i q) -> p i q", i=4), ACT.Exp, scale=HD ** -0.5)\
                       .then_inc(sem("exp_ready"), 1)
                    if t == 0 and j >= 1:
                        take_sums(n, j - 1)
                    if t == MAX_ROWS_AT:
                        if j < QUADS - 1:
                            take_max_rows(n, b, j + 1)
                        elif nxt is not None:
                            take_max_rows(*nxt, 0)
                    if nxt_keys is not None and s in KEYS_MID_AT:
                        keys_mid(nxt_keys, KEYS_MID_AT.index(s))
                take_sums(n, QUADS - 1)

            def norm_rows(tag):
                act.wait_ge(sem("normT_psum"), nth("normT_psum", tag))
                copy(xnT[:, :, :], ps[:, XB, :].rearrange("p (b q) -> p b q", b=B)).then_inc(sem("normT_ready"), 1)

            def cross_attention(l):
                n0 = B * l
                if l == 0:
                    context_rows(n0, first=True)
                else:
                    keys_high(1, n0 + 1)
                norm_rows(f"xattn{l}")
                if l == 0:
                    act.wait_ge(sem("w_k0"), loads["w_k0"])
                    keys_high(l, n0, first=True)
                    for c in range(CHUNKS):
                        keys_mid(n0, c, first=True)
                    context_rows(1)
                    keys_high(l, 1, first=None)
                take_max_rows(n0, 0, 0)
                with act.Fori(0, B - 2) as b:
                    n, nb = b + n0, act.snap(b + 1)
                    second_pass(n, b, (n + 1, nb), n + 1)
                    context_rows(n + 2)
                    keys_high(l, n + 2)
                n = n0 + B - 2
                second_pass(n, B - 2, (n + 1, B - 1), n + 1)
                if l == 0:
                    act.wait_ge(sem("w_k1"), loads["w_k1"])
                    context_rows(n + 2)
                    keys_high(1, n + 2)
                n = n0 + B - 1
                second_pass(n, B - 1, None, n + 1 if l == 0 else None)
                act.wait_ge(sem("attnT_psum"), l + 1)
                copy(xnT[:, :, :], ps[:, XB, :].rearrange("p (b q) -> p b q", b=B)).then_inc(sem("attnT_ready"), 1)
                if l == 0:
                    context_rows(n + 2, banks=(E0, E0))

            act.wait_ge(sem("psum_cleared"), 1)
            cross_attention(0)
            act_middle0(act, copy)
            cross_attention(1)
            act_middle1(act, copy)

        @block.vector
        def _(dve):
            chain = [0]

            def link(ins):
                chain[0] += 1
                ins.then_inc(sem("dve_chain"), 1)
                dve.wait_ge(sem("dve_chain"), chain[0])

            def norm(src, dst, tag, link=link):
                for b in range(B):
                    last = dve.bn_stats(stats[:, b, :], src[:, b, :])
                link(last)
                for b in range(B):
                    last = dve.bn_aggr(meanvar[:, b, :], stats[:, b, :])
                link(last)
                dve.tensor_scalar(veps[:, :], meanvar[:, :, 1], 1e-5, None, ALU.add)\
                   .then_inc(sem("norm_var"), 1)
                dve.wait_ge(sem("norm_rstd"), nth("norm_rstd", tag))
                for b in range(B):
                    last = dve.tensor_scalar(dst[:, b, :], src[:, b, :], meanvar[:, b, 0:1], rstd[:, b:b + 1],
                                             ALU.subtract, ALU.mult)
                return last

            def values(l, n):
                for u in range(2):
                    dve.wait_ge(sem("v_psum"), n * 2 + (u + 1))
                    for c in range(2):
                        bias = spread(bx[l]["v"][:, :].rearrange("p (a n) -> p a n", a=1), 1, 4)
                        last = dve.tensor_tensor(
                            vones[:, 8 * u + 4 * c:8 * u + 4 * c + 4, :, 0:HD],
                            ps[:, 2 * u + c, :].rearrange("p (t h d) -> p t h d", t=4, h=H),
                            bias.rearrange("p t (h d) -> p t h d", h=H), ALU.add)
                    last.then_inc(sem("v_ready"), 1)

            def keys_rest(l, n, first=False):
                for u in range(2):
                    dve.wait_ge(sem("k_part0_ready"), n * 2 + (u + 1))
                    if u == 0 and not first:
                        dve.wait_ge(sem("k_part2_ready"), n)
                    cols = slice(u * 2 * BANK, (u + 1) * 2 * BANK)
                    dve.scalar_tensor_tensor(k_rest[:, cols], ps[:, 2 * u:2 * u + 2, :].rearrange("p a c -> p (a c)"),
                                             bx[l]["k"][:, :], k_part[0][:, cols], ALU.add, ALU.subtract)\
                       .then_inc(sem("k_rest_ready"), 1)

            def take_max(n, j, m):
                dve.wait_ge(sem("max_psum"), n * 32 + (8 * j + m + 1))
                bank = 2 * (m % 2)
                dve.reduce_max(max_part[:, m // 2, m % 2:m % 2 + 1],
                               ps[:, bank:bank + 2, :].rearrange("p a c -> p (a c)"), axis=AX.X)\
                   .then_inc(sem("max_taken"), 1)

            def split_max(n, j, link, first=False):
                dve.wait_ge(sem("max_taken"), n * 32 + 8 * (j + 1))
                link(dve.tensor_reduce(neg_max[:, :], max_part[:, :, :], AX.X, ALU.max, negate=True))
                if not (first and j == 0):
                    dve.wait_ge(sem("max_rows_psum"), n * 4 + j)
                link(dve.tensor_copy(neg_split[:, :, 1], neg_max[:, :]))
                link(dve.tensor_tensor(neg_rest[:, :], neg_max[:, :], neg_split[:, :, 1], ALU.subtract))
                link(dve.tensor_copy(neg_split[:, :, 2], neg_rest[:, :]))
                dve.tensor_tensor(neg_split[:, :, 3], neg_rest[:, :], neg_split[:, :, 2], ALU.subtract)\
                   .then_inc(sem("neg_split_ready"), 1)

            def attend(n, b, j, link):
                dve.wait_ge(sem("sumsT_psum"), n * 4 + (j + 1))
                sumsT = ps[:, XB, 0:P].rearrange("p (i w) -> p i w", i=4)
                link(dve.reciprocal(rden[:, :], sumsT[:, :, HD]))
                dst = attn_tok[:, b, 4 * HD * j:4 * HD * (j + 1)].rearrange("p (i d) -> p i d", i=4)
                weight = spread(rden[:, :].rearrange("p (i a) -> p i a", a=1), 2, HD)
                dve.tensor_tensor(dst, sumsT[:, :, 0:HD], weight, ALU.mult).then_inc(sem("attended"), 1)

            LINKS = 4 * QUADS + QUADS

            def second_pass(n, b, n_next, link):
                for m in range(AHEAD // 2, (AHEAD + SLOTS) // 2):
                    j = m // 8
                    if m >= AHEAD // 2 + 8 and m % 8 == 6:
                        attend(n, b, j - 2, link)
                    at = (n, j) if j < QUADS else (n_next, j - QUADS) if n_next is not None else None
                    if at is not None:
                        take_max(*at, m % 8)
                        if m % 8 == 7:
                            split_max(*at, link)

            def cross_attention(l):
                n0 = B * l
                norm(x, xn, f"xattn{l}").then_inc(sem("norm_ready"), 1)
                dve.wait_ge(sem("q_psum"), l + 1)
                dve.wait_ge(sem(f"w_q{l}"), loads[f"w_q{l}"])
                link(dve.tensor_scalar(q_rest[0], ps[:, OB, :], bx[l]["q"][:, :], None, ALU.add))
                if l:
                    dve.wait_ge(sem("q0_stored"), 16)
                dve.tensor_copy(q_part[0][:, :], q_rest[0]).then_inc(sem("q_part0_ready"), 1)
                dve.wait_ge(sem("q_part0_ready"), l + 1)
                link(dve.tensor_tensor(q_rest[1], q_rest[0], q_part[0][:, :], ALU.subtract))
                dve.tensor_copy(q_part[1][:, :], q_rest[1]).then_inc(sem("q_part1_ready"), 1)
                dve.wait_ge(sem("q_part1_ready"), l + 1)
                dve.tensor_tensor(q_part[2][:, :], q_rest[1], q_part[1][:, :], ALU.subtract)\
                   .then_inc(sem("q_part2_ready"), 1)
                if l == 0:
                    dve.wait_ge(sem("w_k0"), loads["w_k0"])
                    keys_rest(l, n0, first=True)
                    for u in range(2):
                        cols = slice(u * 2 * BANK, (u + 1) * 2 * BANK)
                        dve.wait_ge(sem("k_rest_ready"), u + 1)
                        dve.wait_ge(sem("k_part1_ready"), 2 * u + 2)
                        last = dve.tensor_tensor(k_part[2][:, cols], k_rest[:, cols], k_part[1][:, cols], ALU.subtract)
                    last.then_inc(sem("k_part2_ready"), 1)
                if l == 0:
                    dve.wait_ge(sem("w_v0"), loads["w_v0"])
                    values(l, n0)
                keys_rest(l, n0 + 1)
                for m in range(AHEAD // 2):
                    take_max(n0, m // 8, m % 8)
                    if m == 7:
                        split_max(n0, 0, link, first=(l == 0))
                start = chain[0]
                if l == 0:
                    dve.wait_ge(sem("mask_loaded"), loads["mask_loaded"])
                    dve.tensor_scalar(mask_bias[:, :], mask_u8[:, :], 1.0, -MASKED, ALU.subtract, ALU.mult)\
                       .then_inc(sem("mask_bias_ready"), 1)
                with dve.Fori(0, B - 2) as b:
                    within = [0]

                    def link_b(ins):
                        within[0] += 1
                        ins.then_inc(sem("dve_chain"), 1)
                        dve.wait_ge(sem("dve_chain"), b * LINKS + (start + within[0]))

                    second_pass(b + n0, b, b + (n0 + 1), link_b)
                    values(l, b + (n0 + 1))
                    attend(b + n0, b, QUADS - 1, link_b)
                    keys_rest(l, b + (n0 + 2))
                    assert within[0] == LINKS, within
                chain[0] += (B - 2) * LINKS
                n = n0 + B - 2
                second_pass(n, B - 2, n + 1, link)
                values(l, n + 1)
                attend(n, B - 2, QUADS - 1, link)
                if l == 0:
                    dve.wait_ge(sem("w_k1"), loads["w_k1"])
                    keys_rest(1, n + 2)
                n = n0 + B - 1
                second_pass(n, B - 1, None, link)
                attend(n, B - 1, QUADS - 1, link)
                dve.wait_ge(sem("xo_psum"), l + 1)
                dve.wait_ge(sem("x_biased"), l + 1)
                dve.tensor_tensor(x[:, :, :], xn2[:, :, :], ps[:, OB, :].rearrange("p (b d) -> p b d", b=B), ALU.add)\
                   .then_inc(sem("x_attended"), 1)
                dve.wait_ge(sem("x_attended"), l + 1)

            dve.memset(ps[:, OB, :], 0.0).then_inc(sem("psum_cleared"), 1)
            dve.memset(neg_split[:, :, 0], 1.0)
            dve.memset(vones[:, :, :, HD], 1.0)
            dve.wait_ge(sem("w_base"), loads["w_base"])
            dve.tensor_copy(ident_bf[:, :], ident[:, :]).then_inc(sem("consts_ready"), 1)
            dve.memset(hT[:, :, :], 0.0)
            dve.wait_ge(sem("x_loaded"), 16)
            cross_attention(0)
            dve_middle0(dve, link, norm, values)
            cross_attention(1)
            dve_middle1(dve, link, norm)

        @block.gpsimd
        def _(pool):
            def alone(ins, name, count):
                ins.then_inc(sem(name), 1)
                pool.wait_ge(sem(name), count)

            def rstd_of(tag):
                pool.wait_ge(sem("norm_var"), nth("norm_var", tag))
                alone(pool.tensor_tensor(rstd[:, :], veps[:, :], half_neg[:, :], ALU.pow),
                      "norm_rstd", nth("norm_rstd", tag))

            def split_keys(n):
                pool.wait_ge(sem("k_stored"), stored(n - 1))
                pool.wait_ge(sem("k_part1_ready"), n * 4 + 4)
                alone(pool.tensor_tensor(k_part[2][:, :], k_rest[:, :], k_part[1][:, :], ALU.subtract),
                      "k_part2_ready", n + 1)

            def cross_attention(l):
                if l:
                    rstd_of("xattn1")
                pool.wait_ge(sem(f"w_o{l}"), loads[f"w_o{l}"])
                alone(pool.tensor_tensor(xn2[:, :, :], x[:, :, :],
                                         spread(bx[l]["o"][:, :].rearrange("p (a n) -> p a n", a=1), 1, B), ALU.add),
                      "x_biased", l + 1)
                with pool.Fori(0, B - 1) as b:
                    split_keys(b + (B * l + 1))
                if l == 0:
                    split_keys(B)

            alone(pool.memset(row_init[MASK_ROW:KROWS_EXP, :], 1.0), "row_init_ready", 1)
            alone(pool.memset(row_init[MASK_ROW:MASK_ROW + 1, :], 0.0), "row_init_ready", 2)
            alone(pool.memset(half_neg[:, :], -0.5), "half_ready", 1)
            stacked = [qstack[rows, :, :, :, :].rearrange("p j e b q -> p (j e b q)").bitcast(mybir.dt.uint32)
                       for rows in (slice(0, P), slice(MASK_ROW, MASK_ROW + 1))]
            alone(pool.memset(stacked[0], 0), "qstack_cleared", 1)
            rstd_of("xattn0")
            alone(pool.memset(stacked[1], 0x3F803F80), "qstack_cleared", 2)
            cross_attention(0)
            pool_middle0(pool, rstd_of, alone)
            cross_attention(1)
            pool_middle1(pool, rstd_of)

        return nc


_TRANSPOSED = ("L0_attn_qkv_w", "L0_attn_out_w", "L1_attn_W_spin", "L1_attn_W_global", "L1_attn_W_J")


def _constants(np):
    tok = np.arange(P)
    half = np.arange(0, FD, 2, dtype=np.float32)
    inv_freq = np.float32(1.0) / np.float32(10000.0) ** (half / np.float32(FD))
    freqs = tok.astype(np.float32)[:, None] * inv_freq[None, :]
    base = (half + np.float32(0.4 * FD)) / np.float32(1.4 * FD)
    power = (tok - P // 2).astype(np.float32) / np.float32(32.0)
    scale = (base[None, :] ** power[:, None]).astype(np.float32)
    cos, sin = np.cos(freqs), np.sin(freqs)
    both = lambda u, v: np.concatenate([u, v], axis=1)
    rot = np.stack([both(cos * scale, cos * scale), both(-sin * scale, sin * scale),
                    both(cos / scale, cos / scale), both(-sin / scale, sin / scale)], axis=1)
    q, k = tok[:, None], tok[None, :]
    return {
        "c_ident": np.eye(P, dtype=np.float32),
        "c_band": np.where((q < k) | (q > k + 64), MASKED, 0.0).astype(np.float32),
        "c_shift": (q + 1 == k).astype(np.float32),
        "c_headmask": (tok[:, None] // HD == np.arange(H)[None, :]).astype(np.float32),
        "c_rot": rot.astype(np.float32),
        "c_erank": np.tile(np.arange(E, 0, -1, dtype=np.float32), (B, 1)),
    }


def kernel(**inputs):
    import numpy as np
    import concourse.bacc as bacc
    from concourse.bass_utils import run_bass_kernel_spmd

    nc = bacc.Bacc("TRN2", target_bir_lowering=False, num_devices=1)
    host = {}
    for name, value in inputs.items():
        v = np.asarray(value)
        if name == "ctx_1024":
            name = "ctx"
        if name == "mask_BxS2_bk1":
            name, v = "mask", v.reshape(-1)
        if name in _TRANSPOSED:
            name, v = name + "T", v.T
        host[name] = np.ascontiguousarray(v)
    host.update(_constants(np))
    arrays, aps = {}, {}
    for name, v in host.items():
        arrays[f"in_{name}"] = v
        aps[name] = nc.dram_tensor(f"in_{name}", v.shape, mybir.dt.from_np(v.dtype), kind="ExternalInput").ap()
    out = nc.dram_tensor("out_0", (B, P, D), F32, kind="ExternalOutput").ap()
    perceiver(nc, aps, out)
    result = run_bass_kernel_spmd(nc, [arrays], core_ids=[0])
    return result.results[0]["out_0"]
```
